# Optimizing a Trainium2 kernel written in Bass

```python
import numpy as np
import jax
import jax.numpy as jnp

def _softmax(x, axis=-1):
    return jax.nn.softmax(x, axis=axis)

def _gelu(x):
    return jax.nn.gelu(x, approximate=True)

def _silu(x):
    return jax.nn.silu(x)

def _sigmoid(x):
    return jax.nn.sigmoid(x)

def _layernorm(x, axis=-1, eps=1e-05):
    m = jnp.mean(x, axis=axis, keepdims=True)
    v = jnp.var(x, axis=axis, keepdims=True)
    return (x - m) / jnp.sqrt(v + eps)

def _scatter_add(tgt, idx, src, axis=0):
    return tgt.at[idx].add(src)

def _segment_sum(src, seg, n):
    return jax.ops.segment_sum(src, seg, n)
kernel_name = 'mk_seq_preln_d2_jaxref_r8_282c75'

def setup_inputs(seed: int=0):
    np.random.seed(seed)
    _w = jnp.asarray

    def _L0_attn_setup():
        import jax, jax.numpy as jnp
        import numpy as np
        N_LAYER, N_HEAD, D_MODEL, D_FF = (6, 16, 128, 512)
        D_HEAD = D_MODEL // N_HEAD
        M_FEAT = 2 * D_MODEL // N_HEAD
        CHUNK = 128
        LN_EPS = 1e-05
        ATT_EPS = 1e-06
        B, S = (4, 256)

        def _layer_norm(x, g, b):
            mu = x.mean(-1, keepdims=True)
            var = ((x - mu) ** 2).mean(-1, keepdims=True)
            return (x - mu) * jax.lax.rsqrt(var + LN_EPS) * g + b

        def _favor_phi(x, omega):
            x = x * D_HEAD ** (-0.25)
            u = jnp.einsum('bhsd,dm->bhsm', x, omega)
            nrm = 0.5 * jnp.sum(x * x, axis=-1, keepdims=True)
            phi = jnp.concatenate([jnp.exp(u - nrm), jnp.exp(-u - nrm)], axis=-1)
            return phi * M_FEAT ** (-0.5)

        def _causal_linear_attention(Qp, Kp, V):
            b, h, s, m = Qp.shape
            d = V.shape[-1]
            c = s // CHUNK
            Qc = Qp.reshape(b, h, c, CHUNK, m)
            Kc = Kp.reshape(b, h, c, CHUNK, m)
            Vc = V.reshape(b, h, c, CHUNK, d)
            kv = jnp.einsum('bhclm,bhcld->bhcmd', Kc, Vc)
            ksum = Kc.sum(axis=3)
            kv_pre = jnp.cumsum(kv, axis=2) - kv
            ks_pre = jnp.cumsum(ksum, axis=2) - ksum
            scores = jnp.einsum('bhcim,bhcjm->bhcij', Qc, Kc)
            mask = jnp.tril(jnp.ones((CHUNK, CHUNK), bool))
            scores = jnp.where(mask, scores, 0.0)
            num = jnp.einsum('bhcij,bhcjd->bhcid', scores, Vc) + jnp.einsum('bhcim,bhcmd->bhcid', Qc, kv_pre)
            den = scores.sum(-1) + jnp.einsum('bhcim,bhcm->bhci', Qc, ks_pre)
            out = num / (den[..., None] + ATT_EPS)
            return out.reshape(b, h, s, d)

        def _forward(x, Wq, bq, Wk, bk, Wv, bv, Wo, bo, omega, g1, be1, W1, bf1, W2, bf2, g2, be2):
            bsz, slen, _ = x.shape
            out = x
            for l in range(N_LAYER):

                def proj(W, bvec):
                    y = jnp.einsum('bsd,de->bse', out, W) + bvec
                    return y.reshape(bsz, slen, N_HEAD, D_HEAD).transpose(0, 2, 1, 3)
                q = proj(Wq[l], bq[l])
                k = proj(Wk[l], bk[l])
                v = proj(Wv[l], bv[l])
                Qp = _favor_phi(q, omega[l])
                Kp = _favor_phi(k, omega[l])
                a = _causal_linear_attention(Qp, Kp, v)
                a = a.transpose(0, 2, 1, 3).reshape(bsz, slen, D_MODEL)
                a = jnp.einsum('bsd,de->bse', a, Wo[l]) + bo[l]
                h1 = _layer_norm(out + a, g1[l], be1[l])
                y = jax.nn.relu(jnp.einsum('bsd,df->bsf', h1, W1[l]) + bf1[l])
                y = jnp.einsum('bsf,fd->bsd', y, W2[l]) + bf2[l]
                out = _layer_norm(h1 + y, g2[l], be2[l])
            return out
        key = jax.random.key(seed)
        ks = jax.random.split(key, 12)
        s = D_MODEL ** (-0.5)
        f32 = jnp.float32
        return {'x': jax.random.normal(ks[0], (B, S, D_MODEL), f32), 'Wq': jax.random.normal(ks[1], (N_LAYER, D_MODEL, D_MODEL), f32) * s, 'bq': jnp.zeros((N_LAYER, D_MODEL), f32), 'Wk': jax.random.normal(ks[2], (N_LAYER, D_MODEL, D_MODEL), f32) * s, 'bk': jnp.zeros((N_LAYER, D_MODEL), f32), 'Wv': jax.random.normal(ks[3], (N_LAYER, D_MODEL, D_MODEL), f32) * s, 'bv': jnp.zeros((N_LAYER, D_MODEL), f32), 'Wo': jax.random.normal(ks[4], (N_LAYER, D_MODEL, D_MODEL), f32) * s, 'bo': jnp.zeros((N_LAYER, D_MODEL), f32), 'omega': jax.random.normal(ks[5], (N_LAYER, D_HEAD, M_FEAT // 2), f32), 'g1': jnp.ones((N_LAYER, D_MODEL), f32), 'be1': jnp.zeros((N_LAYER, D_MODEL), f32), 'W1': jax.random.normal(ks[6], (N_LAYER, D_MODEL, D_FF), f32) * s, 'bf1': jnp.zeros((N_LAYER, D_FF), f32), 'W2': jax.random.normal(ks[7], (N_LAYER, D_FF, D_MODEL), f32) * D_FF ** (-0.5), 'bf2': jnp.zeros((N_LAYER, D_MODEL), f32), 'g2': jnp.ones((N_LAYER, D_MODEL), f32), 'be2': jnp.zeros((N_LAYER, D_MODEL), f32)}
    _L0_attn_in = _L0_attn_setup()

    def _L0_ffn_setup():
        import jax, jax.numpy as jnp
        import numpy as np
        B, T, C = (4, 256, 128)
        E, F, K = (8, 256, 2)
        key = jax.random.key(seed)
        k0, k1, k2, k3 = jax.random.split(key, 4)
        s = lambda d: 1.0 / np.sqrt(d)
        x = jax.random.normal(k0, (B, T, C), dtype=jnp.float32)
        Wr = jax.random.normal(k1, (E, C), dtype=jnp.float32) * s(C)
        W1 = jax.random.normal(k2, (E, 2 * F, C), dtype=jnp.float32) * s(C)
        W2 = jax.random.normal(k3, (E, C, F), dtype=jnp.float32) * s(F)
        return {'x': x, 'Wr': Wr, 'W1': W1, 'W2': W2}
    _L0_ffn_in = _L0_ffn_setup()

    def _L1_attn_setup():
        import jax, jax.numpy as jnp
        import numpy as np
        import math
        B, L, D = (2, 512, 128)
        H, DK, DV = (4, 32, 32)
        CHUNK = 32
        PROB_FLOOR = 0.02

        def _l2norm(x, eps=1e-06):
            return x * jax.lax.rsqrt(jnp.sum(x * x, -1, keepdims=True) + eps)

        def _silu(x):
            return x * jax.nn.sigmoid(x)

        def _short_conv(x, w):
            K = w.shape[-1]
            xp = jnp.pad(x, ((0, 0), (K - 1, 0), (0, 0)))
            y = sum((xp[:, j:j + x.shape[1], :] * w[:, j] for j in range(K)))
            return _silu(y)

        def _fir_conv(x, filt):
            b, l, h, d = x.shape
            K = filt.shape[-1]
            xf = jnp.pad(x.reshape(b, l, h * d).transpose(0, 2, 1), ((0, 0), (0, 0), (K - 1, 0)))
            w = filt.reshape(h * d, 1, K)
            y = jax.lax.conv_general_dilated(xf, w, (1,), 'VALID', dimension_numbers=('NCH', 'OIH', 'NCH'), feature_group_count=h * d)
            return y.transpose(0, 2, 1).reshape(b, l, h, d)

        def _delta_rule_chunkwise(q, k, v, beta, chunk=CHUNK):
            b, h, Lq, dk = q.shape
            dv = v.shape[-1]
            n = Lq // chunk
            q = _l2norm(q)
            k = _l2norm(k)
            v = v * beta[..., None]
            kb = k * beta[..., None]
            rs = lambda t: t.reshape(b, h, n, chunk, t.shape[-1])
            qc, kc, vc, kbc = (rs(q), rs(k), rs(v), rs(kb))
            strict_lower = jnp.tril(jnp.ones((chunk, chunk), bool), -1)
            M = jnp.where(strict_lower, jnp.einsum('bhncd,bhnmd->bhncm', kbc, kc), 0.0)
            eye = jnp.eye(chunk, dtype=q.dtype)
            T = jax.scipy.linalg.solve_triangular(eye + M, jnp.broadcast_to(eye, M.shape), lower=True, unit_diagonal=True)
            u = T @ vc
            w = T @ kbc
            incl_lower = jnp.tril(jnp.ones((chunk, chunk), bool), 0)

            def step(S, xs):
                q_i, k_i, u_i, w_i = xs
                attn = jnp.where(incl_lower, q_i @ k_i.swapaxes(-1, -2), 0.0)
                u_adj = u_i - w_i @ S
                out_i = q_i @ S + attn @ u_adj
                S = S + k_i.swapaxes(-1, -2) @ u_adj
                return (S, out_i)
            S0 = jnp.zeros((b, h, dk, dv), q.dtype)
            xs = tuple((jnp.moveaxis(t, 2, 0) for t in (qc, kc, u, w)))
            S, out = jax.lax.scan(step, S0, xs)
            out = jnp.moveaxis(out, 0, 2).reshape(b, h, Lq, dv)
            return (out, S)

        def _rmsnorm(x, w, eps=1e-05):
            return x * jax.lax.rsqrt(jnp.mean(x * x, -1, keepdims=True) + eps) * w

        def _per_head_stats(x):
            mean = jnp.mean(x, -1, keepdims=True)
            var = jnp.var(x, -1, keepdims=True)
            am = jnp.mean(jnp.abs(x), -1, keepdims=True)
            l2 = jnp.sqrt(jnp.sum(x * x, -1, keepdims=True))
            return jnp.concatenate([mean, var, am, l2], -1)

        def _forward(hidden_states, q_w, k_w, v_w, b_w, q_cw, k_cw, v_cw, fir_short_w, fir_long_w, mlp1_w, mlp1_b, mlp2_w, mlp2_b, logit_temp, conv_res_logit, norm_w, o_w):
            b, l, _ = hidden_states.shape
            q_in = _short_conv(hidden_states @ q_w.T, q_cw)
            k_in = _short_conv(hidden_states @ k_w.T, k_cw)
            v_in = _short_conv(hidden_states @ v_w.T, v_cw)
            q = q_in.reshape(b, l, H, DK)
            k = k_in.reshape(b, l, H, DK)
            v_direct = v_in.reshape(b, l, H, DV)
            beta = jnp.maximum(jax.nn.sigmoid(hidden_states @ b_w.T), 1e-06)
            delta_out, _S = _delta_rule_chunkwise(q.transpose(0, 2, 1, 3), k.transpose(0, 2, 1, 3), v_direct.transpose(0, 2, 1, 3), beta.transpose(0, 2, 1))
            delta_out = delta_out.transpose(0, 2, 1, 3)
            local_short = _fir_conv(v_direct, fir_short_w)
            local_long = _fir_conv(v_direct, fir_long_w)
            stats = jnp.concatenate([_per_head_stats(local_short), _per_head_stats(local_long), _per_head_stats(delta_out), _per_head_stats(v_direct)], -1)
            hs_exp = jnp.broadcast_to(hidden_states[:, :, None, :], (b, l, H, hidden_states.shape[-1]))
            gate_in = jnp.concatenate([hs_exp, stats], -1)
            h1 = jax.nn.gelu(gate_in @ mlp1_w.T + mlp1_b)
            logits = h1 @ mlp2_w.T + mlp2_b
            temp = jax.nn.softplus(logit_temp)
            p = jax.nn.softmax(logits / temp, -1)
            p = jnp.maximum(p, PROB_FLOOR)
            p = p / jnp.sum(p, -1, keepdims=True)
            o = p[..., 0:1] * local_short + p[..., 1:2] * local_long + p[..., 2:3] * delta_out + p[..., 3:4] * v_direct
            o = o + jax.nn.sigmoid(conv_res_logit)[None, None, :, None] * local_short
            o = _rmsnorm(o, norm_w)
            o = o.reshape(b, l, H * DV) @ o_w.T
            return o
        key = jax.random.key(seed)
        ks = jax.random.split(key, 16)
        s = 0.02
        hidden_gate = D * 2 // 2
        gate_in_dim = D + 16
        inp = {'hidden_states': jax.random.normal(ks[0], (B, L, D), jnp.float32), 'q_w': jax.random.normal(ks[1], (D, D), jnp.float32) * s, 'k_w': jax.random.normal(ks[2], (D, D), jnp.float32) * s, 'v_w': jax.random.normal(ks[3], (D, D), jnp.float32) * s, 'b_w': jax.random.normal(ks[4], (H, D), jnp.float32) * s, 'q_cw': jax.random.normal(ks[5], (D, 4), jnp.float32) * s, 'k_cw': jax.random.normal(ks[6], (D, 4), jnp.float32) * s, 'v_cw': jax.random.normal(ks[7], (D, 4), jnp.float32) * s, 'fir_short_w': jax.random.normal(ks[8], (H, DV, 5), jnp.float32) * s, 'fir_long_w': jax.random.normal(ks[9], (H, DV, 64), jnp.float32) * s, 'mlp1_w': jax.random.normal(ks[10], (hidden_gate, gate_in_dim), jnp.float32) * s, 'mlp1_b': jnp.zeros((hidden_gate,), jnp.float32), 'mlp2_w': jax.random.normal(ks[11], (4, hidden_gate), jnp.float32) * s, 'mlp2_b': jnp.array([-0.5, -0.5, 1.0, 3.0], jnp.float32), 'logit_temp': jnp.full((1,), math.log(math.expm1(0.7)), jnp.float32), 'conv_res_logit': jnp.full((H,), -2.0, jnp.float32), 'norm_w': jnp.ones((DV,), jnp.float32), 'o_w': jax.random.normal(ks[12], (D, D), jnp.float32) * s}
        return inp
    _L1_attn_in = _L1_attn_setup()

    def _L1_ffn_setup():
        import jax, jax.numpy as jnp
        import numpy as np
        E = 8
        K = 2
        D = 128
        H = 128
        B, T = (2, 128)
        key = jax.random.key(seed)
        ks = jax.random.split(key, 6)
        s = 0.02
        return {'x': jax.random.normal(ks[0], (B, T, D), dtype=jnp.float32), 'gate_w': jax.random.normal(ks[1], (E, D), dtype=jnp.float32) * s, 'lb_bias': jnp.zeros((E,), dtype=jnp.float32), 'w1': jax.random.normal(ks[2], (E, H, D), dtype=jnp.float32) * s, 'w2': jax.random.normal(ks[3], (E, D, H), dtype=jnp.float32) * s, 'cfc': jax.random.normal(ks[4], (H, D), dtype=jnp.float32) * s, 'cproj': jax.random.normal(ks[5], (D, H), dtype=jnp.float32) * s}
    _L1_ffn_in = _L1_ffn_setup()
    _d = {'L0_attn_x': _L0_attn_in['x'], 'L0_attn_Wq': _L0_attn_in['Wq'], 'L0_attn_bq': _L0_attn_in['bq'], 'L0_attn_Wk': _L0_attn_in['Wk'], 'L0_attn_bk': _L0_attn_in['bk'], 'L0_attn_Wv': _L0_attn_in['Wv'], 'L0_attn_bv': _L0_attn_in['bv'], 'L0_attn_Wo': _L0_attn_in['Wo'], 'L0_attn_bo': _L0_attn_in['bo'], 'L0_attn_omega': _L0_attn_in['omega'], 'L0_attn_g1': _L0_attn_in['g1'], 'L0_attn_be1': _L0_attn_in['be1'], 'L0_attn_W1': _L0_attn_in['W1'], 'L0_attn_bf1': _L0_attn_in['bf1'], 'L0_attn_W2': _L0_attn_in['W2'], 'L0_attn_bf2': _L0_attn_in['bf2'], 'L0_attn_g2': _L0_attn_in['g2'], 'L0_attn_be2': _L0_attn_in['be2'], 'L0_ffn_Wr': _L0_ffn_in['Wr'], 'L0_ffn_W1': _L0_ffn_in['W1'], 'L0_ffn_W2': _L0_ffn_in['W2'], 'L1_attn_q_w': _L1_attn_in['q_w'], 'L1_attn_k_w': _L1_attn_in['k_w'], 'L1_attn_v_w': _L1_attn_in['v_w'], 'L1_attn_b_w': _L1_attn_in['b_w'], 'L1_attn_q_cw': _L1_attn_in['q_cw'], 'L1_attn_k_cw': _L1_attn_in['k_cw'], 'L1_attn_v_cw': _L1_attn_in['v_cw'], 'L1_attn_fir_short_w': _L1_attn_in['fir_short_w'], 'L1_attn_fir_long_w': _L1_attn_in['fir_long_w'], 'L1_attn_mlp1_w': _L1_attn_in['mlp1_w'], 'L1_attn_mlp1_b': _L1_attn_in['mlp1_b'], 'L1_attn_mlp2_w': _L1_attn_in['mlp2_w'], 'L1_attn_mlp2_b': _L1_attn_in['mlp2_b'], 'L1_attn_logit_temp': _L1_attn_in['logit_temp'], 'L1_attn_conv_res_logit': _L1_attn_in['conv_res_logit'], 'L1_attn_norm_w': _L1_attn_in['norm_w'], 'L1_attn_o_w': _L1_attn_in['o_w'], 'L1_ffn_gate_w': _L1_ffn_in['gate_w'], 'L1_ffn_lb_bias': _L1_ffn_in['lb_bias'], 'L1_ffn_w1': _L1_ffn_in['w1'], 'L1_ffn_w2': _L1_ffn_in['w2'], 'L1_ffn_cfc': _L1_ffn_in['cfc'], 'L1_ffn_cproj': _L1_ffn_in['cproj']}
    _x0 = _d['L0_attn_x']
    _d['L0_attn_x'] = jax.random.normal(jax.random.fold_in(jax.random.key(seed), 1), (16, 256, 128), dtype=_x0.dtype)
    del _x0
    return _d

def reference(L0_attn_x, L0_attn_Wq, L0_attn_bq, L0_attn_Wk, L0_attn_bk, L0_attn_Wv, L0_attn_bv, L0_attn_Wo, L0_attn_bo, L0_attn_omega, L0_attn_g1, L0_attn_be1, L0_attn_W1, L0_attn_bf1, L0_attn_W2, L0_attn_bf2, L0_attn_g2, L0_attn_be2, L0_ffn_Wr, L0_ffn_W1, L0_ffn_W2, L1_attn_q_w, L1_attn_k_w, L1_attn_v_w, L1_attn_b_w, L1_attn_q_cw, L1_attn_k_cw, L1_attn_v_cw, L1_attn_fir_short_w, L1_attn_fir_long_w, L1_attn_mlp1_w, L1_attn_mlp1_b, L1_attn_mlp2_w, L1_attn_mlp2_b, L1_attn_logit_temp, L1_attn_conv_res_logit, L1_attn_norm_w, L1_attn_o_w, L1_ffn_gate_w, L1_ffn_lb_bias, L1_ffn_w1, L1_ffn_w2, L1_ffn_cfc, L1_ffn_cproj):

    def _L0_attn_ref(x, Wq, bq, Wk, bk, Wv, bv, Wo, bo, omega, g1, be1, W1, bf1, W2, bf2, g2, be2):
        import jax, jax.numpy as jnp
        import numpy as np
        N_LAYER, N_HEAD, D_MODEL, D_FF = (6, 16, 128, 512)
        D_HEAD = D_MODEL // N_HEAD
        M_FEAT = 2 * D_MODEL // N_HEAD
        CHUNK = 128
        LN_EPS = 1e-05
        ATT_EPS = 1e-06
        B, S = (4, 256)

        def _layer_norm(x, g, b):
            mu = x.mean(-1, keepdims=True)
            var = ((x - mu) ** 2).mean(-1, keepdims=True)
            return (x - mu) * jax.lax.rsqrt(var + LN_EPS) * g + b

        def _favor_phi(x, omega):
            x = x * D_HEAD ** (-0.25)
            u = jnp.einsum('bhsd,dm->bhsm', x, omega)
            nrm = 0.5 * jnp.sum(x * x, axis=-1, keepdims=True)
            phi = jnp.concatenate([jnp.exp(u - nrm), jnp.exp(-u - nrm)], axis=-1)
            return phi * M_FEAT ** (-0.5)

        def _causal_linear_attention(Qp, Kp, V):
            b, h, s, m = Qp.shape
            d = V.shape[-1]
            c = s // CHUNK
            Qc = Qp.reshape(b, h, c, CHUNK, m)
            Kc = Kp.reshape(b, h, c, CHUNK, m)
            Vc = V.reshape(b, h, c, CHUNK, d)
            kv = jnp.einsum('bhclm,bhcld->bhcmd', Kc, Vc)
            ksum = Kc.sum(axis=3)
            kv_pre = jnp.cumsum(kv, axis=2) - kv
            ks_pre = jnp.cumsum(ksum, axis=2) - ksum
            scores = jnp.einsum('bhcim,bhcjm->bhcij', Qc, Kc)
            mask = jnp.tril(jnp.ones((CHUNK, CHUNK), bool))
            scores = jnp.where(mask, scores, 0.0)
            num = jnp.einsum('bhcij,bhcjd->bhcid', scores, Vc) + jnp.einsum('bhcim,bhcmd->bhcid', Qc, kv_pre)
            den = scores.sum(-1) + jnp.einsum('bhcim,bhcm->bhci', Qc, ks_pre)
            out = num / (den[..., None] + ATT_EPS)
            return out.reshape(b, h, s, d)

        def _forward(x, Wq, bq, Wk, bk, Wv, bv, Wo, bo, omega, g1, be1, W1, bf1, W2, bf2, g2, be2):
            bsz, slen, _ = x.shape
            out = x
            for l in range(N_LAYER):

                def proj(W, bvec):
                    y = jnp.einsum('bsd,de->bse', out, W) + bvec
                    return y.reshape(bsz, slen, N_HEAD, D_HEAD).transpose(0, 2, 1, 3)
                q = proj(Wq[l], bq[l])
                k = proj(Wk[l], bk[l])
                v = proj(Wv[l], bv[l])
                Qp = _favor_phi(q, omega[l])
                Kp = _favor_phi(k, omega[l])
                a = _causal_linear_attention(Qp, Kp, v)
                a = a.transpose(0, 2, 1, 3).reshape(bsz, slen, D_MODEL)
                a = jnp.einsum('bsd,de->bse', a, Wo[l]) + bo[l]
                h1 = _layer_norm(out + a, g1[l], be1[l])
                y = jax.nn.relu(jnp.einsum('bsd,df->bsf', h1, W1[l]) + bf1[l])
                y = jnp.einsum('bsf,fd->bsd', y, W2[l]) + bf2[l]
                out = _layer_norm(h1 + y, g2[l], be2[l])
            return out
        return _forward(x, Wq, bq, Wk, bk, Wv, bv, Wo, bo, omega, g1, be1, W1, bf1, W2, bf2, g2, be2)

    def _L0_ffn_ref(x, Wr, W1, W2):
        import jax, jax.numpy as jnp
        import numpy as np
        B, T, C = (4, 256, 128)
        E, F, K = (8, 256, 2)
        Bb, Tt, Cc = x.shape
        flat = x.reshape(-1, Cc)
        N = flat.shape[0]
        logits = flat @ Wr.T
        weights, ids = jax.lax.top_k(logits, K)
        weights = jax.nn.softmax(weights, axis=-1)
        rows = jnp.arange(N)[:, None]
        router_weights = jnp.zeros((N, E), dtype=flat.dtype).at[rows, ids].add(weights)
        h = jnp.einsum('nc,efc->nef', flat, W1)
        val, gate = (h[..., :F], h[..., F:])
        act = val * jax.nn.silu(gate)
        expert_outputs = jnp.einsum('nef,ecf->nec', act, W2)
        out = jnp.einsum('nec,ne->nc', expert_outputs, router_weights)
        return out.reshape(Bb, Tt, Cc)

    def _L1_attn_ref(hidden_states, q_w, k_w, v_w, b_w, q_cw, k_cw, v_cw, fir_short_w, fir_long_w, mlp1_w, mlp1_b, mlp2_w, mlp2_b, logit_temp, conv_res_logit, norm_w, o_w):
        import jax, jax.numpy as jnp
        import numpy as np
        import math
        B, L, D = (2, 512, 128)
        H, DK, DV = (4, 32, 32)
        CHUNK = 32
        PROB_FLOOR = 0.02

        def _l2norm(x, eps=1e-06):
            return x * jax.lax.rsqrt(jnp.sum(x * x, -1, keepdims=True) + eps)

        def _silu(x):
            return x * jax.nn.sigmoid(x)

        def _short_conv(x, w):
            K = w.shape[-1]
            xp = jnp.pad(x, ((0, 0), (K - 1, 0), (0, 0)))
            y = sum((xp[:, j:j + x.shape[1], :] * w[:, j] for j in range(K)))
            return _silu(y)

        def _fir_conv(x, filt):
            b, l, h, d = x.shape
            K = filt.shape[-1]
            xf = jnp.pad(x.reshape(b, l, h * d).transpose(0, 2, 1), ((0, 0), (0, 0), (K - 1, 0)))
            w = filt.reshape(h * d, 1, K)
            y = jax.lax.conv_general_dilated(xf, w, (1,), 'VALID', dimension_numbers=('NCH', 'OIH', 'NCH'), feature_group_count=h * d)
            return y.transpose(0, 2, 1).reshape(b, l, h, d)

        def _delta_rule_chunkwise(q, k, v, beta, chunk=CHUNK):
            b, h, Lq, dk = q.shape
            dv = v.shape[-1]
            n = Lq // chunk
            q = _l2norm(q)
            k = _l2norm(k)
            v = v * beta[..., None]
            kb = k * beta[..., None]
            rs = lambda t: t.reshape(b, h, n, chunk, t.shape[-1])
            qc, kc, vc, kbc = (rs(q), rs(k), rs(v), rs(kb))
            strict_lower = jnp.tril(jnp.ones((chunk, chunk), bool), -1)
            M = jnp.where(strict_lower, jnp.einsum('bhncd,bhnmd->bhncm', kbc, kc), 0.0)
            eye = jnp.eye(chunk, dtype=q.dtype)
            T = jax.scipy.linalg.solve_triangular(eye + M, jnp.broadcast_to(eye, M.shape), lower=True, unit_diagonal=True)
            u = T @ vc
            w = T @ kbc
            incl_lower = jnp.tril(jnp.ones((chunk, chunk), bool), 0)

            def step(S, xs):
                q_i, k_i, u_i, w_i = xs
                attn = jnp.where(incl_lower, q_i @ k_i.swapaxes(-1, -2), 0.0)
                u_adj = u_i - w_i @ S
                out_i = q_i @ S + attn @ u_adj
                S = S + k_i.swapaxes(-1, -2) @ u_adj
                return (S, out_i)
            S0 = jnp.zeros((b, h, dk, dv), q.dtype)
            xs = tuple((jnp.moveaxis(t, 2, 0) for t in (qc, kc, u, w)))
            S, out = jax.lax.scan(step, S0, xs)
            out = jnp.moveaxis(out, 0, 2).reshape(b, h, Lq, dv)
            return (out, S)

        def _rmsnorm(x, w, eps=1e-05):
            return x * jax.lax.rsqrt(jnp.mean(x * x, -1, keepdims=True) + eps) * w

        def _per_head_stats(x):
            mean = jnp.mean(x, -1, keepdims=True)
            var = jnp.var(x, -1, keepdims=True)
            am = jnp.mean(jnp.abs(x), -1, keepdims=True)
            l2 = jnp.sqrt(jnp.sum(x * x, -1, keepdims=True))
            return jnp.concatenate([mean, var, am, l2], -1)

        def _forward(hidden_states, q_w, k_w, v_w, b_w, q_cw, k_cw, v_cw, fir_short_w, fir_long_w, mlp1_w, mlp1_b, mlp2_w, mlp2_b, logit_temp, conv_res_logit, norm_w, o_w):
            b, l, _ = hidden_states.shape
            q_in = _short_conv(hidden_states @ q_w.T, q_cw)
            k_in = _short_conv(hidden_states @ k_w.T, k_cw)
            v_in = _short_conv(hidden_states @ v_w.T, v_cw)
            q = q_in.reshape(b, l, H, DK)
            k = k_in.reshape(b, l, H, DK)
            v_direct = v_in.reshape(b, l, H, DV)
            beta = jnp.maximum(jax.nn.sigmoid(hidden_states @ b_w.T), 1e-06)
            delta_out, _S = _delta_rule_chunkwise(q.transpose(0, 2, 1, 3), k.transpose(0, 2, 1, 3), v_direct.transpose(0, 2, 1, 3), beta.transpose(0, 2, 1))
            delta_out = delta_out.transpose(0, 2, 1, 3)
            local_short = _fir_conv(v_direct, fir_short_w)
            local_long = _fir_conv(v_direct, fir_long_w)
            stats = jnp.concatenate([_per_head_stats(local_short), _per_head_stats(local_long), _per_head_stats(delta_out), _per_head_stats(v_direct)], -1)
            hs_exp = jnp.broadcast_to(hidden_states[:, :, None, :], (b, l, H, hidden_states.shape[-1]))
            gate_in = jnp.concatenate([hs_exp, stats], -1)
            h1 = jax.nn.gelu(gate_in @ mlp1_w.T + mlp1_b)
            logits = h1 @ mlp2_w.T + mlp2_b
            temp = jax.nn.softplus(logit_temp)
            p = jax.nn.softmax(logits / temp, -1)
            p = jnp.maximum(p, PROB_FLOOR)
            p = p / jnp.sum(p, -1, keepdims=True)
            o = p[..., 0:1] * local_short + p[..., 1:2] * local_long + p[..., 2:3] * delta_out + p[..., 3:4] * v_direct
            o = o + jax.nn.sigmoid(conv_res_logit)[None, None, :, None] * local_short
            o = _rmsnorm(o, norm_w)
            o = o.reshape(b, l, H * DV) @ o_w.T
            return o
        return _forward(hidden_states, q_w, k_w, v_w, b_w, q_cw, k_cw, v_cw, fir_short_w, fir_long_w, mlp1_w, mlp1_b, mlp2_w, mlp2_b, logit_temp, conv_res_logit, norm_w, o_w)

    def _L1_ffn_ref(x, gate_w, lb_bias, w1, w2, cfc, cproj):
        import jax, jax.numpy as jnp
        import numpy as np
        E = 8
        K = 2
        D = 128
        H = 128
        B, T = (2, 128)
        Bx, Tx, Dx = x.shape
        logits = jnp.einsum('btd,ed->bte', x, gate_w)
        _, idx = jax.lax.top_k(logits + lb_bias, K)
        sel_logits = jnp.take_along_axis(logits, idx, axis=-1)
        w = jax.nn.sigmoid(sel_logits)
        w = w / (jnp.sum(w, axis=-1, keepdims=True) + 1e-06)
        xf = x.reshape(-1, Dx)
        idxf = idx.reshape(-1, K)
        wf = w.reshape(-1, K)
        onehot = jax.nn.one_hot(idxf, E, dtype=wf.dtype)
        we = jnp.einsum('nke,nk->ne', onehot, wf)
        hidden = jnp.square(jax.nn.relu(jnp.einsum('nd,ehd->neh', xf, w1)))
        expert_out = jnp.einsum('neh,edh->ned', hidden, w2)
        moe_out = jnp.einsum('ned,ne->nd', expert_out, we).reshape(Bx, Tx, Dx)
        sh = jnp.square(jax.nn.relu(jnp.einsum('btd,hd->bth', x, cfc)))
        shared = jnp.einsum('bth,dh->btd', sh, cproj)
        return moe_out + shared
    x = L0_attn_x
    x = x + _L0_attn_ref(_layernorm(x, axis=-1), L0_attn_Wq, L0_attn_bq, L0_attn_Wk, L0_attn_bk, L0_attn_Wv, L0_attn_bv, L0_attn_Wo, L0_attn_bo, L0_attn_omega, L0_attn_g1, L0_attn_be1, L0_attn_W1, L0_attn_bf1, L0_attn_W2, L0_attn_bf2, L0_attn_g2, L0_attn_be2)
    x = x + _L0_ffn_ref(_layernorm(x, axis=-1), L0_ffn_Wr, L0_ffn_W1, L0_ffn_W2)
    x = x + _L1_attn_ref(_layernorm(x, axis=-1), L1_attn_q_w, L1_attn_k_w, L1_attn_v_w, L1_attn_b_w, L1_attn_q_cw, L1_attn_k_cw, L1_attn_v_cw, L1_attn_fir_short_w, L1_attn_fir_long_w, L1_attn_mlp1_w, L1_attn_mlp1_b, L1_attn_mlp2_w, L1_attn_mlp2_b, L1_attn_logit_temp, L1_attn_conv_res_logit, L1_attn_norm_w, L1_attn_o_w)
    x = x + _L1_ffn_ref(_layernorm(x, axis=-1), L1_ffn_gate_w, L1_ffn_lb_bias, L1_ffn_w1, L1_ffn_w2, L1_ffn_cfc, L1_ffn_cproj)
    return x

_drawn_inputs = setup_inputs


def setup_inputs(seed=0):
    import zlib

    import numpy as np

    out = dict(_drawn_inputs(seed))
    spreads = {'L0_attn_bq': (0.0, 0.1),
     'L0_attn_bk': (0.0, 0.1),
     'L0_attn_bv': (0.0, 0.1),
     'L0_attn_bo': (0.0, 0.1),
     'L0_attn_g1': (1.0, 0.2),
     'L0_attn_be1': (0.0, 0.1),
     'L0_attn_bf1': (0.0, 0.1),
     'L0_attn_bf2': (0.0, 0.1),
     'L0_attn_g2': (1.0, 0.2),
     'L0_attn_be2': (0.0, 0.1),
     'L1_attn_mlp1_b': (0.0, 0.8),
     'L1_attn_conv_res_logit': (-2.0, 0.6),
     'L1_attn_norm_w': (1.0, 0.6),
     'L1_ffn_lb_bias': (0.0, 0.8)}
    factors = {'L1_attn_q_w': 8.0,
     'L1_attn_k_w': 8.0,
     'L1_attn_b_w': 8.0,
     'L1_attn_q_cw': 8.0,
     'L1_attn_k_cw': 8.0,
     'L1_attn_fir_short_w': 8.0,
     'L1_attn_fir_long_w': 8.0,
     'L1_attn_mlp1_w': 8.0,
     'L1_attn_mlp2_w': 8.0,
     'L1_ffn_gate_w': 8.0,
     'L1_ffn_w1': 8.0,
     'L1_ffn_w2': 8.0,
     'L1_ffn_cfc': 7.008,
     'L1_ffn_cproj': 6.462}
    for name, (base, spread) in spreads.items():
        noise = np.random.default_rng([zlib.crc32(name.encode()), seed]).standard_normal(out[name].shape)
        drawn = base * np.exp(spread * noise) if base else spread * noise
        out[name] = jnp.asarray(drawn.astype(out[name].dtype))
    for name, factor in factors.items():
        out[name] = (out[name] * factor).astype(out[name].dtype)
    return out
```

```python
from contextlib import ExitStack

import concourse.bass as bass
from concourse import mybir

F32 = mybir.dt.float32
U32 = mybir.dt.uint32
ALU = mybir.AluOpType
ACT = mybir.ActivationFunctionType
AX = mybir.AxisListType

P = 128
D = 128
TILES = 4
G = TILES * P
SEQ = 256


class Space:

    def __init__(self, nc, ctx, tag):
        self.nc, self.ctx, self.tag = nc, ctx, tag
        self.sems = []

    def sb(self, name, shape, dt=F32):
        return self.ctx.enter_context(self.nc.sbuf_tensor(f"{self.tag}_{name}", shape, dt))

    def ps(self, name):
        return self.ctx.enter_context(self.nc.psum_tensor(f"{self.tag}_{name}", [P, 512], F32))

    def sem(self, name):
        handle = self.ctx.enter_context(self.nc.semaphore(f"{self.tag}_{name}"))
        self.sems.append(handle.num)
        return handle

    def block(self):
        self.ctx.callback(self.clear)
        return self.ctx.enter_context(self.nc.Block())

    def clear(self):
        nums = sorted(self.sems)
        starts = [n for n in nums if n - 1 not in nums]
        ends = [n + 1 for n in nums if n + 1 not in nums]
        with self.nc.Block() as block:
            @block.gpsimd
            def _(pool):
                for first, end in zip(starts, ends):
                    pool.sem_clear(range(first, end))


def apart(eng, passes):
    eng.sem_inc(passes, 1)


def load_tokens(nc, x_dram, resid, normed, ident, ngroups):
    with ExitStack() as ctx:
        s = Space(nc, ctx, "ld")
        loaded = [s.sem(f"loaded{g}") for g in range(ngroups)]
        zeroed, ident_ready = s.sem("zeroed"), s.sem("ident_ready")
        block = s.block()

        @block.sync
        def _(sp):
            for g in range(ngroups):
                sp.dma_start(resid[:, g * TILES:(g + 1) * TILES, :],
                             x_dram[g * G:(g + 1) * G, :].rearrange("(t p) c -> p t c", p=P)
                             ).then_inc(loaded[g], 16)
            for g in range(ngroups):
                sp.wait_ge(loaded[g], 16)

        @block.gpsimd
        def _(pool):
            pool.memset(ident[:, :], 0.0).then_inc(zeroed, 1)
            pool.wait_ge(zeroed, 1)
            pool.affine_select(out=ident[:, :], in_=ident[:, :], compare_op=ALU.not_equal, fill=1.0,
                               base=0, pattern=[[-1, P]], channel_multiplier=1).then_inc(ident_ready, 1)


def residual_norm(nc, tag, resid, update, normed, ngroups):
    with ExitStack() as ctx:
        s = Space(nc, ctx, tag)
        row = s.sb("row", [P, TILES, D])
        st6 = s.sb("st6", [P, TILES, 6])
        mv = s.sb("mv", [P, TILES, 2])
        veps = s.sb("veps", [P, TILES])
        mhalf = s.sb("mhalf", [P, TILES])
        rstd = s.sb("rstd", [P, TILES])
        const_ready, fetched, summed = s.sem("const_ready"), s.sem("fetched"), s.sem("summed")
        stats, var_ready, rstd_ready, done = s.sem("stats"), s.sem("var_ready"), s.sem("rstd_ready"), s.sem("done")
        stored, passes = s.sem("stored"), s.sem("passes")
        block = s.block()

        @block.gpsimd
        def _(pool):
            pool.memset(mhalf[:, :], -0.5).then_inc(const_ready, 1)
            pool.wait_ge(const_ready, 1)
            with pool.Fori(0, ngroups) as g:
                pool.wait_ge(var_ready, g + 1)
                pool.tensor_tensor(rstd[:, :], veps[:, :], mhalf[:, :], ALU.pow).then_inc(rstd_ready, 1)

        @block.vector
        def _(dve):
            with dve.Fori(0, ngroups) as g:
                tiles = bass.ds(g * TILES, TILES)
                if update is None:
                    dve.tensor_copy(row[:, :, :], resid[:, tiles, :]).then_inc(summed, 1)
                else:
                    dve.tensor_tensor(row[:, :, :], resid[:, tiles, :], update[:, tiles, :],
                                      ALU.add).then_inc(summed, 1)
                dve.wait_ge(summed, g + 1)
                if update is not None:
                    apart(dve, passes)
                    dve.tensor_copy(resid[:, tiles, :], row[:, :, :]).then_inc(stored, 1)
                for t in range(TILES):
                    dve.bn_stats(st6[:, t, :], row[:, t, :]).then_inc(stats, 1)
                dve.wait_ge(stats, g * 2 * TILES + TILES)
                apart(dve, passes)
                for t in range(TILES):
                    dve.bn_aggr(mv[:, t, :], st6[:, t, :]).then_inc(stats, 1)
                dve.wait_ge(stats, (g + 1) * 2 * TILES)
                dve.tensor_scalar(veps[:, :], mv[:, :, 1], 1e-5, None, ALU.add).then_inc(var_ready, 1)
                dve.wait_ge(rstd_ready, g + 1)
                for t in range(TILES):
                    last = dve.tensor_scalar(row[:, t, :], row[:, t, :], mv[:, t, 0:1], rstd[:, t:t + 1],
                                             ALU.subtract, ALU.mult).then_inc(fetched, 1)
                dve.wait_ge(fetched, (g + 1) * TILES)
                apart(dve, passes)
                dve.tensor_copy(normed[:, tiles, :], row[:, :, :]).then_inc(done, 1)
                dve.wait_ge(done, g + 1)


NL = 6
NH = 16
DH = 8
MF = 16
DFF = 512
FB = DFF // P
C_WQ, C_WK, C_WV, C_WO, C_W1, C_W2 = 0, 128, 256, 384, 512, 1024
C_BV, C_BO, C_G1, C_BE1, C_BF2, C_G2, C_BE2 = (1536 + 128 * i for i in range(7))
C_OM = 1536 + 7 * 128
C_BQ = C_OM + DH
C_BK, C_G1C, C_BE1C, C_BF1C = C_BQ + 1, C_BQ + 2, C_BQ + 3, C_BQ + 4
NPAR = C_BF1C + FB


def encoder(nc, a, x, ident, nlayers=NL, ngroups=8):
    with ExitStack() as ctx:
        s = Space(nc, ctx, "enc")
        params = s.sb("params", [P, nlayers, NPAR])
        w = s.sb("w", [P, NPAR])
        om = s.sb("om", [P, 2, P])
        nb = s.sb("nb", [P, 2, P])
        own = s.sb("own", [P, NH])
        negown = s.sb("negown", [P, NH])
        hm = s.sb("hm", [P, 8])
        ones = s.sb("ones", [P, P])
        cm = s.sb("cm", [P, P])
        bm = s.sb("bm", [P, 2, 4, 2, 2, DH])
        mhalf = s.sb("mhalf", [P, TILES])
        xg = s.sb("xg", [P, G])
        xb = s.sb("xb", [P, G])
        xT = s.sb("xT", [P, G])
        q = s.sb("q", [P, G])
        k = s.sb("k", [P, G])
        qsq = s.sb("qsq", [P, G])
        ksq = s.sb("ksq", [P, G])
        vx = s.sb("vx", [P, TILES, NH, 32])
        vc = s.sb("vc", [P, 2, NH // 2, 32])
        qf = s.sb("qf", [P, 2, G])
        kf = s.sb("kf", [P, 2, G])
        qx = s.sb("qx", [P, 2, 8, G])
        kt = s.sb("kt", [P, 2, 2, P])
        st = s.sb("st", [P, 2, 2, P])
        sm = s.sb("sm", [P, 4, 4, P])
        osb = s.sb("osb", [P, 2, 2 * P])
        den = s.sb("den", [P, 2, NH])
        at = s.sb("at", [P, TILES, D])
        aT = s.sb("aT", [P, G])
        h = s.sb("h", [P, TILES, D])
        y1 = s.sb("y1", [P, TILES, D])
        h1 = s.sb("h1", [P, TILES, D])
        h1T = s.sb("h1T", [P, G])
        hid = s.sb("hid", [P, FB, G])
        st6 = s.sb("st6", [P, TILES, 6])
        mv = s.sb("mv", [P, TILES, 2])
        veps = s.sb("veps", [P, TILES])
        rstd = s.sb("rstd", [P, TILES])

        b_t, b_1, b_2, b_tok = (s.ps(n) for n in ("b_t", "b_1", "b_2", "b_tok"))
        b_o = [s.ps("b_o0"), s.ps("b_o1")]
        b_sc = [s.ps("b_sc0"), s.ps("b_sc1")]

        loaded = s.sem("loaded")
        const, masks_ready, w_ready, om_ready = (s.sem(n) for n in ("const", "masks_ready", "w_ready", "om_ready"))
        xg_ready, xb_ready, sq_ready, vc_ready, h1_ready, rstd_ready = (
            s.sem(n) for n in ("xg_ready", "xb_ready", "sq_ready", "vc_ready", "h1_ready", "rstd_ready"))
        xt_done, qk_done, v_done, phi_done, kt_done, st_done, sc_done, av_done, ot_done, at_done, wo_done, \
            ht_done, hid_done, ffn_done = (s.sem(n) for n in (
                "xt_done", "qk_done", "v_done", "phi_done", "kt_done", "st_done", "sc_done", "av_done",
                "ot_done", "at_done", "wo_done", "ht_done", "hid_done", "ffn_done"))
        qk_ready, v_ready, qx_ready, st_ready, sm_ready, den_step, a_ready, h_ready, ln_step, var_ready, \
            y1_ready, h2_ready, x_ready = (s.sem(n) for n in (
                "qk_ready", "v_ready", "qx_ready", "st_ready", "sm_ready", "den_step", "a_ready", "h_ready",
                "ln_step", "var_ready", "y1_ready", "h2_ready", "x_ready"))
        xT_ready, f_ready, kt_ready, o_ready, aT_ready, h1T_ready, hid_ready = (
            s.sem(n) for n in ("xT_ready", "f_ready", "kt_ready", "o_ready", "aT_ready", "h1T_ready", "hid_ready"))
        passes = s.sem("passes")
        pw = s.sem("pw")
        pw2 = s.sem("pw2")
        block = s.block()

        @block.sync
        def _(sp):
            sp.dma_start(params[:, :, 0:C_BV], a["enc_mats"][:, 0:nlayers, :]).then_inc(loaded, 16)
            sp.dma_start(params[:, :, C_BV:C_OM],
                         a["enc_rows"][0:nlayers].unsqueeze(0).to_broadcast([P, nlayers, C_OM - C_BV])
                         ).then_inc(loaded, 16)
            sp.dma_start(params[:, :, C_BQ:NPAR], a["enc_cols"][:, 0:nlayers, :]).then_inc(loaded, 16)
            for hd in range(NH):
                sp.dma_start(params[hd * DH:(hd + 1) * DH, :, C_OM:C_OM + DH],
                             a["L0_attn_omega"][0:nlayers].rearrange("l d m -> d l m")).then_inc(loaded, 16)
            sp.wait_ge(loaded, 16 * (3 + NH))

        @block.gpsimd
        def _(pool):
            n = 0

            def step(ins):
                nonlocal n
                n += 1
                ins.then_inc(const, 1)
                pool.wait_ge(const, n)

            step(pool.memset(ones[:, :], 1.0))
            step(pool.memset(mhalf[:, :], -0.5))
            step(pool.memset(cm[:, :], 1.0 / MF))
            step(pool.affine_select(out=cm[:, :], in_=cm[:, :], compare_op=ALU.is_ge, fill=0.0, base=0,
                                    pattern=[[1, P]], channel_multiplier=-1))
            step(pool.affine_select(out=own[:, :], in_=ones[:, 0:NH], compare_op=ALU.is_ge, fill=0.0, base=0,
                                    pattern=[[-DH, NH]], channel_multiplier=1))
            step(pool.affine_select(out=own[:, :], in_=own[:, :], compare_op=ALU.is_ge, fill=0.0, base=DH - 1,
                                    pattern=[[DH, NH]], channel_multiplier=-1))
            step(pool.affine_select(out=hm[:, :], in_=ones[:, 0:8], compare_op=ALU.is_ge, fill=0.0, base=0,
                                    pattern=[[-MF, 8]], channel_multiplier=1))
            step(pool.affine_select(out=hm[:, :], in_=hm[:, :], compare_op=ALU.is_ge, fill=0.0, base=MF - 1,
                                    pattern=[[MF, 8]], channel_multiplier=-1))
            step(pool.memset(vx[:, :, :, :], 0.0))
            for par in (0, 1):
                step(pool.memset(vx[:, :, par::2, 16 + DH * par:24 + DH * par], 1.0))
            pool.memset(vc[:, :, :, 16:32], 1.0).then_inc(masks_ready, 1)

            with pool.Fori(0, nlayers) as l:
                pool.wait_ge(w_ready, l + 1)
                pool.wait_ge(x_ready, l * ngroups)
                apart(pool, passes)
                with pool.Fori(0, ngroups) as g:
                    it = l * ngroups + g
                    pool.wait_ge(h_ready, it)
                    pool.tensor_copy(xg[:, :].rearrange("p (t c) -> p t c", t=TILES),
                                     x[:, bass.ds(g * TILES, TILES), :]).then_inc(xg_ready, 1)
                    pool.wait_ge(xg_ready, it + 1)
                    for i, (sq, v) in enumerate(((qsq, q), (ksq, k))):
                        pool.wait_ge(qk_ready, 2 * it + i + 1)
                        pool.tensor_tensor(sq[:, :], v[:, :], v[:, :], ALU.mult).then_inc(sq_ready, 1)
                    pool.wait_ge(v_ready, it + 1)
                    apart(pool, passes)
                    for i in range(2):
                        for par in (0, 1):
                            pool.tensor_copy(vc[:, i, :, DH * par:DH * par + DH],
                                             vx[:, 2 * i, par::2, DH * par:DH * par + DH]).then_inc(vc_ready, 1)
                    pool.tensor_tensor(
                        xb[:, :].rearrange("p (t c) -> p t c", t=TILES),
                        xg[:, :].rearrange("p (t c) -> p t c", t=TILES),
                        w[:, C_BO:C_BO + D].unsqueeze(1).to_broadcast([P, TILES, D]), ALU.add).then_inc(xb_ready, 1)
                    pool.wait_ge(var_ready, 2 * it + 1)
                    pool.tensor_tensor(rstd[:, :], veps[:, :], mhalf[:, :], ALU.pow).then_inc(rstd_ready, 1)
                    pool.wait_ge(y1_ready, TILES * (it + 1))
                    for i, (src, c, op) in enumerate(((y1, C_G1, ALU.mult), (h1, C_BE1, ALU.add), (h1, C_BF2, ALU.add))):
                        if i:
                            pool.wait_ge(h1_ready, 3 * it + i)
                        pool.tensor_tensor(h1[:, :, :], src[:, :, :],
                                           w[:, c:c + D].unsqueeze(1).to_broadcast([P, TILES, D]),
                                           op).then_inc(h1_ready, 1)
                    pool.wait_ge(var_ready, 2 * it + 2)
                    pool.tensor_tensor(rstd[:, :], veps[:, :], mhalf[:, :], ALU.pow).then_inc(rstd_ready, 1)

        @block.tensor
        def _(pe):
            pe.wait_ge(masks_ready, 1)
            with pe.Fori(0, nlayers) as l:
                pe.wait_ge(om_ready, 2 * l + 2)
                apart(pe, passes)
                with pe.Fori(0, ngroups) as g:
                    it = l * ngroups + g
                    pe.wait_ge(xg_ready, it + 1)
                    for t in range(TILES):
                        last = pe.transpose(b_t[:, t * P:(t + 1) * P], xg[:, t * P:(t + 1) * P], ident[:, :])
                    last.then_inc(xt_done, 1)
                    pe.wait_ge(xT_ready, it + 1)
                    for c, b in ((C_WQ, b_1), (C_WK, b_2)):
                        pe.matmul(b[:, :], w[:, c:c + D], xT[:, :], start=True, stop=True).then_inc(qk_done, 1)
                    pe.wait_ge(h2_ready, it)
                    for t in range(TILES):
                        last = pe.matmul(b_tok[:, t * D:(t + 1) * D], xT[:, t * P:(t + 1) * P], w[:, C_WV:C_WV + D],
                                         start=True, stop=True)
                    last.then_inc(v_done, 1)
                    for i, (f, b, lin, sq) in enumerate(((0, b_1, q, qsq), (1, b_2, q, qsq),
                                                         (0, b_t, k, ksq), (1, b_1, k, ksq))):
                        if i == 0:
                            pe.wait_ge(qk_ready, 2 * it + 1)
                        if i == 1:
                            pe.wait_ge(qk_ready, 2 * it + 2)
                        if i == 3:
                            pe.wait_ge(f_ready, 4 * it + 1)
                        pe.matmul(b[:, :], om[:, f, :], lin[:, :], start=True, stop=False)
                        pe.wait_ge(sq_ready, 2 * it + (1 if i < 2 else 2))
                        pe.matmul(b[:, :], nb[:, f, :], sq[:, :], start=False, stop=True).then_inc(phi_done, 1)
                    pe.wait_ge(f_ready, 4 * it + 4)
                    for i in range(2):
                        for f in range(2):
                            last = pe.transpose(b_2[:, (2 * i + f) * P:(2 * i + f + 1) * P],
                                                kf[:, f, 2 * i * P:(2 * i + 1) * P], ident[:, :])
                    last.then_inc(kt_done, 1)

                    def scores(c):
                        t, f, n = c // 4, c // 2 % 2, c % 4
                        if c < 4:
                            pe.wait_ge(qx_ready, 16 * it + 4 * (n + 1))
                        if c >= 2:
                            pe.wait_ge(sm_ready, 16 * it + c - 1)
                        for b in range(4):
                            last = pe.matmul(
                                b_sc[c % 2][32 * b:32 * b + 32, :].rearrange("p (h i) -> p h i", h=4)[:, :, 32 * b:P],
                                kf[:, f, t * P + 32 * b:t * P + 32 * b + 32],
                                qx[:, f, 4 * (n % 2):4 * (n % 2) + 4, t * P + 32 * b:(t + 1) * P],
                                start=True, stop=True)
                        last.then_inc(sc_done, 1)

                    def combine(c):
                        t, f, n = c // 4, c // 2 % 2, c % 4
                        if n == 0 and t >= 2:
                            pe.wait_ge(o_ready, TILES * it + t - 1)
                        if n == 0 and t == 1:
                            pe.wait_ge(st_ready, it + 1)
                        pe.wait_ge(sm_ready, 16 * it + c + 1)
                        for pair in (2 * n, 2 * n + 1):
                            o = b_o[t % 2][32 * (pair % 4):32 * (pair % 4) + 32,
                                           (pair // 4) * P:(pair // 4 + 1) * P]
                            for j in (0, 1):
                                hd = 2 * pair + j
                                last = pe.matmul(o, vx[:, t, hd, :], sm[:, c % 4, hd % 4, :],
                                                 start=(pair < 4 and j == 0), stop=(j == 1 and t % 2 == 0),
                                                 skip_group_check=True)
                            if t % 2:
                                last = pe.matmul(o, st[:, t // 2, f, 32 * (pair % 4):32 * (pair % 4) + 32],
                                          qf[:, f, t * P:(t + 1) * P], start=False, stop=True, skip_group_check=True)
                        last.then_inc(av_done, 1)

                    def turn(t):
                        pe.wait_ge(o_ready, TILES * it + t + 1)
                        if t == 0:
                            pass
                        else:
                            pe.wait_ge(a_ready, TILES * it + t)
                        for i in range(2):
                            last = pe.transpose(b_2[:, i * P:(i + 1) * P], osb[:, t % 2, i * P:(i + 1) * P], ident[:, :])
                        last.then_inc(ot_done, 1)

                    def turn_back(t):
                        pe.wait_ge(a_ready, TILES * it + t + 1)
                        pe.transpose(b_t[:, t * P:(t + 1) * P], at[:, t, :], ident[:, :]).then_inc(at_done, 1)

                    for c in range(4 * TILES + 3):
                        if c < 4 * TILES:
                            scores(c)
                        if c == 1:
                            pe.wait_ge(kt_ready, it + 1)
                            pe.wait_ge(vc_ready, 4 * it + 4)
                            for i in range(2):
                                for f in range(2):
                                    last = pe.matmul(b_tok[:, (2 * i + f) * P:(2 * i + f + 1) * P], kt[:, i, f, :],
                                                     vc[:, i, 4 * f:4 * f + 4, :], start=True, stop=True)
                            last.then_inc(st_done, 1)
                        if 1 <= c <= 4 * TILES:
                            combine(c - 1)
                        if c >= 5 and c % 4 == 1:
                            turn(c // 4 - 1)
                        if c >= 6 and c % 4 == 2:
                            turn_back(c // 4 - 1)
                    pe.wait_ge(aT_ready, it + 1)
                    for t in range(TILES):
                        last = pe.matmul(b_tok[:, t * D:(t + 1) * D], aT[:, t * P:(t + 1) * P], w[:, C_WO:C_WO + D],
                                         start=True, stop=True)
                    last.then_inc(wo_done, 1)
                    pe.wait_ge(y1_ready, TILES * (it + 1))
                    for t in range(TILES):
                        last = pe.transpose(b_t[:, t * P:(t + 1) * P], y1[:, t, :], ident[:, :])
                    last.then_inc(ht_done, 1)
                    pe.wait_ge(h1T_ready, it + 1)
                    for f in range(FB):
                        if f >= 2:
                            pe.wait_ge(hid_ready, FB * it + f - 1)
                        pe.matmul((b_1, b_2)[f % 2][:, :], w[:, C_W1 + f * P:C_W1 + (f + 1) * P], h1T[:, :],
                                  start=True, stop=True).then_inc(hid_done, 1)
                    pe.wait_ge(hid_ready, FB * (it + 1))
                    for t in range(TILES):
                        for f in range(FB):
                            last = pe.matmul(b_tok[:, t * D:(t + 1) * D], hid[:, f, t * P:(t + 1) * P],
                                             w[:, C_W2 + f * D:C_W2 + (f + 1) * D], start=(f == 0), stop=(f == FB - 1))
                    last.then_inc(ffn_done, 1)

        @block.scalar
        def _(act):
            act.wait_ge(loaded, 16 * (3 + NH))
            with act.Fori(0, nlayers) as l:
                act.wait_ge(x_ready, l * ngroups)
                act.activation(w[:, :], params[:, bass.ds(l, 1), :].rearrange("p a b -> p (a b)"),
                               ACT.Copy).then_inc(w_ready, 1)
                with act.Fori(0, ngroups) as g:
                    it = l * ngroups + g
                    act.wait_ge(xt_done, it + 1)
                    act.activation(xT[:, :], b_t[:, :], ACT.Copy).then_inc(xT_ready, 1)
                    for i, (f, b, dst) in enumerate(((0, b_1, qf), (1, b_2, qf), (0, b_t, kf), (1, b_1, kf))):
                        act.wait_ge(phi_done, 4 * it + i + 1)
                        act.activation(dst[:, f, :], b[:, :], ACT.Exp).then_inc(f_ready, 1)
                    act.wait_ge(kt_done, it + 1)
                    act.activation(kt[:, :, :, :].rearrange("p a b c -> p (a b c)"), b_2[:, :],
                                   ACT.Copy).then_inc(kt_ready, 1)
                    for t in range(TILES):
                        act.wait_ge(av_done, 16 * it + 4 * (t + 1))
                        act.activation(osb[:, t % 2, :], b_o[t % 2][:, 0:2 * P],
                                       ACT.Copy).then_inc(o_ready, 1)
                    act.wait_ge(at_done, TILES * (it + 1))
                    act.activation(aT[:, :], b_t[:, :], ACT.Copy).then_inc(aT_ready, 1)
                    act.wait_ge(ht_done, it + 1)
                    act.activation(h1T[:, :], b_t[:, :], ACT.Identity, scale=w[:, C_G1C:C_G1C + 1],
                                   bias=w[:, C_BE1C:C_BE1C + 1]).then_inc(h1T_ready, 1)
                    for f in range(FB):
                        act.wait_ge(hid_done, FB * it + f + 1)
                        act.activation(hid[:, f, :], (b_1, b_2)[f % 2][:, :], ACT.Relu,
                                       bias=w[:, C_BF1C + f:C_BF1C + f + 1]).then_inc(hid_ready, 1)

        @block.vector
        def _(dve):
            scale = float(DH) ** -0.25
            dve.wait_ge(masks_ready, 1)
            for i in range(2):
                dve.memset(b_sc[i][:, :], 0.0).then_inc(pw, 1)
            dve.tensor_scalar(negown[:, :], own[:, :], -1.0, None, ALU.mult).then_inc(pw, 1)
            dve.tensor_scalar(nb[:, :, :].rearrange("p f (h m) -> p (f h) m", m=MF),
                              own[:, :].unsqueeze(2).to_broadcast([P, NH, MF]), -0.5, None, ALU.mult).then_inc(pw, 1)
            for kind in range(2):
                dve.tensor_scalar(bm[:, 0, :, kind, :, :],
                                  hm[:, :].rearrange("p (a b) -> p a b", a=4).unsqueeze(3).to_broadcast([P, 4, 2, DH]),
                                  1.0 / MF, None, ALU.mult).then_inc(pw, 1)
            dve.wait_ge(pw, 6)
            with dve.Fori(0, nlayers) as l:
                dve.wait_ge(w_ready, l + 1)
                for sign, o in ((0, own), (1, negown)):
                    dve.tensor_tensor(
                        om[:, :, :].rearrange("p f (h m) -> p (f h) m", m=MF)[:, :, DH * sign:DH * sign + DH],
                        w[:, C_OM:C_OM + DH].unsqueeze(1).to_broadcast([P, NH, DH]),
                        o[:, :].unsqueeze(2).to_broadcast([P, NH, DH]), ALU.mult).then_inc(om_ready, 1)
                with dve.Fori(0, ngroups) as g:
                    it = l * ngroups + g
                    for i, (dst, b, c) in enumerate(((q, b_1, C_BQ), (k, b_2, C_BK))):
                        dve.wait_ge(qk_done, 2 * it + i + 1)
                        dve.tensor_scalar(dst[:, :], b[:, :], w[:, c:c + 1], scale, ALU.add,
                                          ALU.mult).then_inc(qk_ready, 1)
                    dve.wait_ge(v_done, it + 1)
                    for par in (0, 1):
                        last = dve.tensor_tensor(
                            vx[:, :, par::2, DH * par:DH * par + DH],
                            b_tok[:, :].rearrange("p (t a b d) -> p t a b d", t=TILES, a=8, b=2)[:, :, :, par, :],
                            w[:, C_BV:C_BV + D].rearrange("p (a b d) -> p a b d", a=8, b=2)[:, :, par, :]
                            .unsqueeze(1).to_broadcast([P, TILES, 8, DH]), ALU.add)
                    last.then_inc(v_ready, 1)
                    for f in range(2):
                        dve.wait_ge(f_ready, 4 * it + f + 1)
                        for hd in range(8):
                            dve.tensor_scalar(qx[:, f, hd, :], qf[:, f, :], hm[:, hd:hd + 1], None,
                                              ALU.mult).then_inc(qx_ready, 1)

                    def mask(c):
                        dve.wait_ge(sc_done, 16 * it + c + 1)
                        if c >= 4:
                            dve.wait_ge(av_done, 16 * it + c - 3)
                        dve.tensor_tensor(sm[:, c % 4, :, :], b_sc[c % 2][:, :].rearrange("p (h i) -> p h i", h=4),
                                          cm[:, :].unsqueeze(1).to_broadcast([P, 4, P]), ALU.mult).then_inc(sm_ready, 1)

                    def normalise(t):
                        dve.wait_ge(ot_done, TILES * it + t + 1)
                        o = b_2[:, 0:256].rearrange("p (a k j d) -> p a k j d", k=2, j=2, d=DH)
                        dve.tensor_scalar(den[:, 0, :].rearrange("p (a j) -> p a j", j=2), o[:, :, 1, :, 0],
                                          1e-6, None, ALU.add).then_inc(den_step, 1)
                        dve.wait_ge(den_step, 2 * (TILES * it + t) + 1)
                        dve.reciprocal(den[:, 1, :], den[:, 0, :]).then_inc(den_step, 1)
                        dve.wait_ge(den_step, 2 * (TILES * it + t) + 2)
                        dve.tensor_tensor(at[:, t, :].rearrange("p (a j d) -> p a j d", j=2, d=DH), o[:, :, 0, :, :],
                                          den[:, 1, :].rearrange("p (a j) -> p a j", j=2).unsqueeze(3)
                                          .to_broadcast([P, 8, 2, DH]), ALU.mult).then_inc(a_ready, 1)

                    for c in range(4 * TILES):
                        mask(c)
                        if c == 1:
                            dve.wait_ge(st_done, it + 1)
                            dve.tensor_tensor(
                                st[:, :, :, :].rearrange("p i f c -> p (i f) c"),
                                b_tok[:, :].rearrange("p (i c) -> p i c", i=4),
                                bm[:, 0, :, :, :, :].rearrange("p a k j d -> p (a k j d)").unsqueeze(1)
                                .to_broadcast([P, 4, P]), ALU.mult).then_inc(st_ready, 1)
                        if c >= 5 and c % 4 == 1:
                            normalise(c // 4 - 1)
                    normalise(TILES - 1)

                    def layer_norm(src, dst, k0, done):
                        base = (2 * it + k0) * 2 * TILES
                        for t in range(TILES):
                            dve.bn_stats(st6[:, t, :], src[:, t, :]).then_inc(ln_step, 1)
                        dve.wait_ge(ln_step, base + TILES)
                        apart(dve, passes)
                        for t in range(TILES):
                            dve.bn_aggr(mv[:, t, :], st6[:, t, :]).then_inc(ln_step, 1)
                        dve.wait_ge(ln_step, base + 2 * TILES)
                        dve.tensor_scalar(veps[:, :], mv[:, :, 1], 1e-5, None, ALU.add).then_inc(var_ready, 1)
                        dve.wait_ge(rstd_ready, 2 * it + k0 + 1)
                        for t in range(TILES):
                            dve.tensor_scalar(dst[:, t, :], src[:, t, :], mv[:, t, 0:1], rstd[:, t:t + 1],
                                              ALU.subtract, ALU.mult).then_inc(done, 1)

                    dve.wait_ge(wo_done, it + 1)
                    dve.wait_ge(xb_ready, it + 1)
                    dve.tensor_tensor(h[:, :, :].rearrange("p t c -> p (t c)"), b_tok[:, :], xb[:, :],
                                      ALU.add).then_inc(h_ready, 1)
                    dve.wait_ge(h_ready, it + 1)
                    layer_norm(h, y1, 0, y1_ready)
                    dve.wait_ge(ffn_done, it + 1)
                    dve.wait_ge(h1_ready, 3 * it + 3)
                    dve.tensor_tensor(h[:, :, :].rearrange("p t c -> p (t c)"), b_tok[:, :],
                                      h1[:, :, :].rearrange("p t c -> p (t c)"), ALU.add).then_inc(h2_ready, 1)
                    dve.wait_ge(h2_ready, it + 1)
                    layer_norm(h, h, 1, pw2)
                    dve.wait_ge(pw2, 5 * it + TILES)
                    dve.tensor_tensor(h[:, :, :], h[:, :, :], w[:, C_G2:C_G2 + D].unsqueeze(1).to_broadcast([P, TILES, D]),
                                      ALU.mult).then_inc(pw2, 1)
                    dve.wait_ge(pw2, 5 * it + TILES + 1)
                    dve.tensor_tensor(x[:, bass.ds(g * TILES, TILES), :], h[:, :, :],
                                      w[:, C_BE2:C_BE2 + D].unsqueeze(1).to_broadcast([P, TILES, D]),
                                      ALU.add).then_inc(x_ready, 1)


NE = 8


def mixture(nc, tag, x, ident, ngroups, experts, blocks, up_dram, down_dram, router_dram, bias_dram):
    gated = bias_dram is None
    ways = 2 if gated else 1
    units = [(e, f) for e in range(experts) for f in range(blocks)]
    U = len(units)
    with ExitStack() as ctx:
        s = Space(nc, ctx, tag)
        up = s.sb("up", [P, experts, ways, blocks, P])
        down = s.sb("down", [P, experts, blocks, D])
        wr = s.sb("wr", [P, NE])
        bias = s.sb("bias", [P, NE])
        xg = s.sb("xg", [P, G])
        xT = s.sb("xT", [P, G])
        act = s.sb("act", [P, 2, G])
        hid = s.sb("hid", [P, 3, G])
        acc = s.sb("acc", [P, TILES, D])
        index = s.sb("index", [P, NE])
        lg = s.sb("lg", [P, TILES, NE])
        lb = s.sb("lb", [P, TILES, NE])
        top = s.sb("top", [P, TILES, 8])
        tidx = s.sb("tidx", [P, TILES, 8], U32)
        tif = s.sb("tif", [P, TILES, 8])
        eq1 = s.sb("eq1", [P, TILES, NE])
        eq2 = s.sb("eq2", [P, TILES, NE])
        score = s.sb("score", [P, TILES, NE])
        total = s.sb("total", [P, 2, TILES])
        rw = s.sb("rw", [P, TILES, experts])
        b_t, b_r = s.ps("b_t"), s.ps("b_r")
        b_v = [s.ps("b_v0"), s.ps("b_v1")]
        b_g = [s.ps("b_g0"), s.ps("b_g1")] if gated else b_v
        b_y = [s.ps("b_y0"), s.ps("b_y1")]
        loaded, const_ready = s.sem("loaded"), s.sem("const_ready")
        xg_ready, xt_done, xT_ready, lg_done, route, route_act, score_ready, rw_ready = (s.sem(n) for n in (
            "xg_ready", "xt_done", "xT_ready", "lg_done", "route", "route_act", "score_ready", "rw_ready"))
        up_done, act_ready, hid_ready, down_done, acc_ready, stored = (s.sem(n) for n in (
            "up_done", "act_ready", "hid_ready", "down_done", "acc_ready", "stored"))
        acc_step, chain, passes = s.sem("acc_step"), s.sem("chain"), s.sem("passes")
        block = s.block()
        NLOAD = 3 if gated else 4

        @block.sync
        def _(sp):
            sp.dma_start(wr[:, :], router_dram).then_inc(loaded, 16)
            sp.dma_start(up[:, :, :, :, :], up_dram).then_inc(loaded, 16)
            sp.dma_start(down[:, :, :, :], down_dram).then_inc(loaded, 16)
            if not gated:
                sp.dma_start(bias[:, :], bias_dram.unsqueeze(0).to_broadcast([P, NE])).then_inc(loaded, 16)
            sp.wait_ge(loaded, 16 * NLOAD)

        @block.gpsimd
        def _(pool):
            for e in range(NE):
                pool.memset(index[:, e:e + 1], float(e)).then_inc(const_ready, 1)
            pool.memset(rw[:, :, :], 1.0).then_inc(const_ready, 1)

            def fetch(g, n):
                pool.tensor_copy(xg[:, :].rearrange("p (t c) -> p t c", t=TILES),
                                 x[:, bass.ds(g * TILES, TILES), :]).then_inc(xg_ready, 1)

            fetch(0, 0)
            with pool.Fori(0, ngroups - 1) as g:
                pool.wait_ge(xt_done, g + 1)
                fetch(g + 1, g + 1)
                pool.wait_ge(acc_ready, g + 1)
                pool.tensor_copy(x[:, bass.ds(g * TILES, TILES), :], acc[:, :, :]).then_inc(stored, 1)
            pool.wait_ge(acc_ready, ngroups)
            pool.tensor_copy(x[:, (ngroups - 1) * TILES:ngroups * TILES, :], acc[:, :, :]).then_inc(stored, 1)

        @block.tensor
        def _(pe):
            def turn(g):
                pe.wait_ge(xg_ready, g + 1)
                for t in range(TILES):
                    last = pe.transpose(b_t[:, t * P:(t + 1) * P], xg[:, t * P:(t + 1) * P], ident[:, :])
                last.then_inc(xt_done, 1)

            def logits(g):
                pe.wait_ge(xT_ready, g + 1)
                for t in range(TILES):
                    last = pe.matmul(b_r[:, t * NE:(t + 1) * NE], xT[:, t * P:(t + 1) * P], wr[:, :],
                                     start=True, stop=True)
                last.then_inc(lg_done, 1)

            def expand(g, u):
                e, f = units[u]
                if u >= 2:
                    pe.wait_ge(hid_ready, g * U + u - 1)
                for i in reversed(range(ways)):
                    last = pe.matmul((b_v, b_g)[i][u % 2][:, :], up[:, e, i, f, :], xT[:, :], start=True, stop=True)
                last.then_inc(up_done, 1)

            def contract(g, u):
                e, f = units[u]
                pe.wait_ge(hid_ready, g * U + u + 1)
                if f == 0:
                    pe.wait_ge(acc_step, (g * experts + max(e - 1, 0)) * TILES)
                for t in range(TILES):
                    last = pe.matmul(b_y[e % 2][:, t * D:(t + 1) * D], hid[:, u % 3, t * P:(t + 1) * P],
                                     down[:, e, f, :], start=(f == 0 and t == 0), stop=(f == blocks - 1),
                                     skip_group_check=True)
                last.then_inc(down_done, 1)

            def group(g, ahead):
                for u in range(U + 2):
                    if u < U:
                        expand(g, u)
                    elif u == U and ahead:
                        turn(g + 1)
                    if u >= 2:
                        contract(g, u - 2)
                if ahead:
                    logits(g + 1)

            pe.wait_ge(loaded, 16 * NLOAD)
            turn(0)
            logits(0)
            with pe.Fori(0, ngroups - 1) as g:
                group(g, True)
            group(ngroups - 1, False)

        @block.scalar
        def _(act_e):
            def copy_x(g):
                act_e.wait_ge(xt_done, g + 1)
                act_e.activation(xT[:, :], b_t[:, :], ACT.Copy).then_inc(xT_ready, 1)

            def group(g, ahead):
                for u in range(U):
                    if u == 2:
                        act_e.wait_ge(route, g + 1)
                        act_e.activation(score[:, :, :], score[:, :, :],
                                         ACT.Exp if gated else ACT.Sigmoid).then_inc(route_act, 1)
                    act_e.wait_ge(up_done, g * U + u + 1)
                    if u >= 2:
                        act_e.wait_ge(hid_ready, g * U + u - 1)
                    act_e.activation(act[:, u % 2, :], b_g[u % 2][:, :],
                                     ACT.Silu if gated else ACT.Relu).then_inc(act_ready, 1)
                if ahead:
                    copy_x(g + 1)

            copy_x(0)
            with act_e.Fori(0, ngroups - 1) as g:
                group(g, True)
            group(ngroups - 1, False)

        @block.vector
        def _(dve):
            def router(g):
                n = NR * g

                def link(ins):
                    nonlocal n
                    n = n + 1
                    ins.then_inc(chain, 1)
                    dve.wait_ge(chain, n)
                    apart(dve, passes)

                dve.wait_ge(lg_done, g + 1)
                link(dve.tensor_copy(lg[:, :, :].rearrange("p t e -> p (t e)"), b_r[:, 0:TILES * NE]))
                if gated:
                    pick = lg
                else:
                    pick = lb
                    link(dve.tensor_tensor(lb[:, :, :], lg[:, :, :], bias[:, :].unsqueeze(1).to_broadcast([P, TILES, NE]),
                                           ALU.add))
                for t in range(TILES):
                    link(dve.max(top[:, t, :], pick[:, t, :]))
                for t in range(TILES):
                    link(dve.max_index(tidx[:, t, :], top[:, t, :], pick[:, t, :]))
                if gated:
                    dve.tensor_tensor(score[:, :, :], lg[:, :, :], top[:, :, 0:1].to_broadcast([P, TILES, NE]),
                                      ALU.subtract).then_inc(route, 1)
                else:
                    dve.tensor_copy(score[:, :, :], lg[:, :, :]).then_inc(route, 1)
                link(dve.tensor_copy(tif[:, :, :], tidx[:, :, :]))
                for i, eq in enumerate((eq1, eq2)):
                    link(dve.tensor_tensor(eq[:, :, :], index[:, :].unsqueeze(1).to_broadcast([P, TILES, NE]),
                                           tif[:, :, i:i + 1].to_broadcast([P, TILES, NE]), ALU.is_equal))
                link(dve.tensor_tensor(eq1[:, :, :], eq1[:, :, :], eq2[:, :, :], ALU.add))
                dve.wait_ge(route_act, g + 1)
                link(dve.tensor_tensor(eq1[:, :, :], eq1[:, :, :], score[:, :, :], ALU.mult))
                link(dve.tensor_reduce(total[:, 0, :], eq1[:, :, :], AX.X, ALU.add))
                if not gated:
                    link(dve.tensor_scalar(total[:, 0, :], total[:, 0, :], 1e-6, None, ALU.add))
                link(dve.reciprocal(total[:, 1, :], total[:, 0, :]))
                link(dve.tensor_tensor(rw[:, :, 0:NE], eq1[:, :, :], total[:, 1, :].unsqueeze(2)
                                       .to_broadcast([P, TILES, NE]), ALU.mult))

            NR = 17 if gated else 19

            def product(g, u):
                dve.wait_ge(act_ready, g * U + u + 1)
                if u >= 3:
                    dve.wait_ge(down_done, g * U + u - 2)
                dve.tensor_tensor(hid[:, u % 3, :], b_v[u % 2][:, :], act[:, u % 2, :], ALU.mult).then_inc(hid_ready, 1)

            def gather(g, e):
                dve.wait_ge(down_done, g * U + (e + 1) * blocks)
                if e == 0:
                    dve.wait_ge(stored, g)
                else:
                    dve.wait_ge(acc_step, (g * experts + e) * TILES)
                for t in range(TILES):
                    y, wt = b_y[e % 2][:, t * D:(t + 1) * D], rw[:, t, e:e + 1]
                    if e == 0:
                        dve.tensor_scalar(acc[:, t, :], y, wt, None, ALU.mult).then_inc(acc_step, 1)
                    else:
                        dve.scalar_tensor_tensor(out=acc[:, t, :], in0=y, scalar=wt, in1=acc[:, t, :],
                                                 op0=ALU.mult, op1=ALU.add).then_inc(acc_step, 1)

            def group(g):
                product(g, 0)
                product(g, 1)
                router(g)
                for u in range(2, U + 3):
                    if u < U:
                        product(g, u)
                    if u >= 3 and units[u - 3][1] == blocks - 1:
                        gather(g, units[u - 3][0])
                dve.wait_ge(acc_step, (g + 1) * experts * TILES)
                dve.tensor_copy(total[:, 0, 0:1], total[:, 1, 0:1]).then_inc(acc_ready, 1)

            dve.wait_ge(const_ready, NE + 1)
            dve.wait_ge(loaded, 16 * NLOAD)
            with dve.Fori(0, ngroups) as g:
                group(g)


HD = 4
DK = 32
LEVELS = 7
TAPS, SHORT, LONG = 4, 5, 64


def delta_mixer(nc, a, x, ident, nseq, v_r, short_tm, delta_tm):
    S2 = 2 * P
    NC = SHORT + 3
    with ExitStack() as ctx:
        s = Space(nc, ctx, "dlt")
        wqkv = s.sb("wqkv", [P, 3, D])
        bw = s.sb("bw", [P, HD])
        taps = s.sb("taps", [P, 3, TAPS])
        ftaps = s.sb("ftaps", [P, SHORT])
        ones = s.sb("ones", [P, P])
        hmask = s.sb("hmask", [P, HD])
        strict = s.sb("strict", [P, P])
        causal = s.sb("causal", [P, P])
        blocks = s.sb("blocks", [P, LEVELS + 1, P])
        couple = s.sb("couple", [P, LEVELS, P])
        mhalf = s.sb("mhalf", [P, 4 * HD])
        xg = s.sb("xg", [P, S2])
        xT = s.sb("xT", [P, S2])
        pad = s.sb("pad", [P, 3, TAPS - 1 + S2])
        conv = s.sb("conv", [P, 3, S2])
        qk = s.sb("qk", [P, 2, S2])
        vpad = s.sb("vpad", [P, SHORT - 1 + S2])
        sf = s.sb("sf", [P, S2])
        beta = s.sb("beta", [P, 2, 2, HD])
        qk_tm = s.sb("qk_tm", [P, 2, 2, D])
        vs_tm = s.sb("vs_tm", [P, 2, 2, D])
        sq = s.sb("sq", [P, 2, 2, D])
        ss = s.sb("ss", [P, 2, 4 * HD])
        rn = s.sb("rn", [P, 4 * HD])
        qkn = s.sb("qkn", [P, 2, 2, D])
        kb = s.sb("kb", [P, 2, D])
        vb = s.sb("vb", [P, 2, D])
        qknT = s.sb("qknT", [P, 2, S2])
        qkx = s.sb("qkx", [P, 2, 2, HD, P])
        M = s.sb("M", [P, 2, HD, P])
        MT = s.sb("MT", [P, 2, HD, P])
        AT = s.sb("AT", [P, 2, HD, P])
        CT = s.sb("CT", [P, 2, 2, HD, P])
        X = s.sb("X", [P, 2, HD, P])
        Y = s.sb("Y", [P, 2, HD, P])
        PX = s.sb("PX", [P, 2, HD, P])
        uwT = s.sb("uwT", [P, 3, P])
        u = s.sb("u", [P, 2, D])
        state = s.sb("state", [P, D])
        ua = s.sb("ua", [P, D])
        oT = s.sb("oT", [P, S2])
        B = [s.ps(f"b{i}") for i in range(8)]
        bP, bY, bX = (B[5], B[6]), (B[1], B[2]), (B[7], B[0])
        (loaded, const, const_ready, xg_ready, xt_done, xT_ready, proj_done, pad_ready, beta_sig, dchain, conv_ready,
         silu_ready, sf_ready, tm_done, tm_ready, sq_ready, rn_ready, ss_ready, qkn_ready, qknt_done, qknT_ready,
         qkx_ready, kk_done, at_done, m_ready, at_ready, mt_done, mt_ready, ct_ready, xt2_done, x_ready, p_done,
         p_ready, yy_done, y_ready, uw_done, uw_ready, ut_done, u_ready, st_done, state_ready, ws_done, ua_ready,
         ot_done, oT_ready, o_done, o_ready, kept) = (s.sem(n) for n in (
             "loaded const const_ready xg_ready xt_done xT_ready proj_done pad_ready beta_sig dchain conv_ready "
             "silu_ready sf_ready tm_done tm_ready sq_ready rn_ready ss_ready qkn_ready qknt_done qknT_ready "
             "qkx_ready kk_done at_done m_ready at_ready mt_done mt_ready ct_ready xt2_done x_ready p_done "
             "p_ready yy_done y_ready uw_done uw_ready ut_done u_ready st_done state_ready ws_done ua_ready "
             "ot_done oT_ready o_done o_ready kept").split())
        block = s.block()

        @block.sync
        def _(sp):
            for dst, src in ((wqkv[:, :, :], a["dlt_wqkv"]), (bw[:, :], a["dlt_bw"]), (taps[:, :, :], a["dlt_taps"]),
                             (ftaps[:, :], a["dlt_short"])):
                sp.dma_start(dst, src).then_inc(loaded, 16)
            sp.wait_ge(loaded, 64)

        @block.gpsimd
        def _(pool):
            n = 0

            def step(ins):
                nonlocal n
                n += 1
                ins.then_inc(const, 1)
                pool.wait_ge(const, n)

            def in_blocks(dst, size, count, src):
                w = dst.shape[-1] // count
                d3 = dst.rearrange("p (a r) -> p a r", a=count)
                s3 = src.rearrange("p (a r) -> p a r", a=count)
                step(pool.affine_select(out=d3, in_=s3, compare_op=ALU.is_ge, fill=0.0, base=0,
                                        pattern=[[-size, count], [0, w]], channel_multiplier=1))
                step(pool.affine_select(out=d3, in_=d3, compare_op=ALU.is_ge, fill=0.0, base=size - 1,
                                        pattern=[[size, count], [0, w]], channel_multiplier=-1))

            step(pool.memset(ones[:, :], 1.0))
            step(pool.memset(mhalf[:, :], -0.5))
            step(pool.memset(pad[:, :, 0:TAPS - 1], 0.0))
            step(pool.memset(vpad[:, 0:SHORT - 1], 0.0))
            step(pool.affine_select(out=strict[:, :], in_=ones[:, :], compare_op=ALU.is_gt, fill=0.0, base=0,
                                    pattern=[[-1, P]], channel_multiplier=1))
            step(pool.affine_select(out=causal[:, :], in_=ones[:, :], compare_op=ALU.is_ge, fill=0.0, base=0,
                                    pattern=[[1, P]], channel_multiplier=-1))
            in_blocks(hmask[:, :], DK, HD, ones[:, 0:HD])
            for l in range(LEVELS + 1):
                in_blocks(blocks[:, l, :], 2 ** l, P >> l, ones[:, :])
            for l in range(LEVELS):
                step(pool.tensor_tensor(couple[:, l, :], blocks[:, l + 1, :], blocks[:, l, :], ALU.subtract))
            pool.memset(ua[:, :], 0.0).then_inc(const_ready, 1)
            with pool.Fori(0, nseq) as q:
                pool.wait_ge(xt_done, q)
                pool.tensor_copy(xg[:, :].rearrange("p (t c) -> p t c", t=2),
                                 x[:, bass.ds(q * 2, 2), :]).then_inc(xg_ready, 1)
                pool.wait_ge(tm_ready, 2 * q + 1)
                pool.tensor_tensor(sq[:, :, :, :], qk_tm[:, :, :, :], qk_tm[:, :, :, :], ALU.mult).then_inc(sq_ready, 1)
                pool.wait_ge(ss_ready, q + 1)
                pool.tensor_tensor(rn[:, :], ss[:, 1, :], mhalf[:, :], ALU.pow).then_inc(rn_ready, 1)
                pool.wait_ge(tm_ready, 2 * q + 2)
                for t in range(2):
                    pool.tensor_copy(v_r[:, bass.ds(q + (1 - t) * nseq, 1), :], vs_tm[:, 0, t:t + 1, :]).then_inc(kept, 1)
                pool.tensor_copy(short_tm[:, bass.ds(q * 2, 2), :], vs_tm[:, 1, :, :]).then_inc(kept, 1)
                for l in range(LEVELS):
                    for t in range(2):
                        if l == 0:
                            pool.wait_ge(mt_ready, 2 * q + t + 1)
                        if l >= 2:
                            pool.wait_ge(y_ready if l == 2 else p_ready,
                                         (2 * LEVELS * q + t + 1) if l == 2 else (2 * (LEVELS - 1) * q + 2 * (l - 3) + t + 1))
                        pool.tensor_tensor(CT[:, t, l % 2, :, :], MT[:, t, :, :],
                                           couple[:, l, :].unsqueeze(1).to_broadcast([P, HD, P]),
                                           ALU.mult).then_inc(ct_ready, 1)

        @block.tensor
        def _(pe):
            pe.wait_ge(const_ready, 1)
            pe.wait_ge(loaded, 64)
            with pe.Fori(0, nseq) as q:
                pe.wait_ge(xg_ready, q + 1)
                for t in range(2):
                    last = pe.transpose(B[0][:, t * P:(t + 1) * P], xg[:, t * P:(t + 1) * P], ident[:, :])
                last.then_inc(xt_done, 1)
                pe.wait_ge(xT_ready, q + 1)
                for i in range(3):
                    last = pe.matmul(B[1 + i // 2][:, (i % 2) * S2:(i % 2 + 1) * S2], wqkv[:, i, :], xT[:, :],
                                     start=True, stop=True)
                    if i == 1:
                        last.then_inc(proj_done, 1)
                for t in range(2):
                    last = pe.matmul(B[2][:, S2 + t * HD:S2 + (t + 1) * HD], xT[:, t * P:(t + 1) * P], bw[:, :],
                                     start=True, stop=True)
                last.then_inc(proj_done, 1)
                pe.wait_ge(silu_ready, 3 * q + 2)
                for i in range(4):
                    last = pe.transpose(B[3][:, i * P:(i + 1) * P], qk[:, i // 2, (i % 2) * P:(i % 2 + 1) * P], ident[:, :])
                last.then_inc(tm_done, 1)
                pe.wait_ge(silu_ready, 3 * q + 3)
                for t in range(2):
                    pe.transpose(B[4][:, t * P:(t + 1) * P],
                                 vpad[:, SHORT - 1 + t * P:SHORT - 1 + (t + 1) * P], ident[:, :])
                pe.wait_ge(sf_ready, q + 1)
                for t in range(2):
                    last = pe.transpose(B[4][:, (2 + t) * P:(3 + t) * P], sf[:, t * P:(t + 1) * P], ident[:, :])
                last.then_inc(tm_done, 1)
                pe.wait_ge(qkn_ready, q + 1)
                for i in range(4):
                    last = pe.transpose(B[0][:, i * P:(i + 1) * P], qkn[:, i // 2, i % 2, :], ident[:, :])
                last.then_inc(qknt_done, 1)
                pe.wait_ge(qkx_ready, q * 2 * HD + 2 * HD)
                for t in range(2):
                    pe.matmul(B[5 + t][:, :], qknT[:, 1, t * P:(t + 1) * P], qkx[:, 1, t, :, :],
                              start=True, stop=True).then_inc(kk_done, 1)
                for t in range(2):
                    pe.matmul(B[1 + t][:, :], qknT[:, 1, t * P:(t + 1) * P], qkx[:, 0, t, :, :],
                              start=True, stop=True).then_inc(at_done, 1)
                for t in range(2):
                    pe.wait_ge(m_ready, 2 * q + t + 1)
                    for h in range(HD):
                        last = pe.transpose(B[3 + t][:, h * P:(h + 1) * P], M[:, t, h, :], ident[:, :])
                    last.then_inc(mt_done, 1)
                for l in range(LEVELS):
                    if l:
                        for t in range(2):
                            pe.wait_ge(x_ready, 2 * (LEVELS - 1) * q + 2 * (l - 1) + t + 1)
                            pe.wait_ge(ct_ready, 2 * LEVELS * q + 2 * l + t + 1)
                            for h in range(HD):
                                last = pe.matmul(bP[t][:, h * P:(h + 1) * P], CT[:, t, l % 2, h, :], X[:, t, h, :],
                                                 start=True, stop=True)
                            last.then_inc(p_done, 1)
                        for t in range(2):
                            pe.wait_ge(p_ready, 2 * (LEVELS - 1) * q + 2 * (l - 1) + t + 1)
                            if l == 1:
                                pe.wait_ge(at_ready, 2 * q + t + 1)
                            for h in range(HD):
                                last = pe.matmul(bY[t][:, h * P:(h + 1) * P], PX[:, t, h, :], Y[:, t, h, :],
                                                 start=True, stop=True)
                            last.then_inc(yy_done, 1)
                    if l < LEVELS - 1:
                        for t in range(2):
                            pe.wait_ge(y_ready, 2 * LEVELS * q + 2 * l + t + 1)
                            for h in range(HD):
                                last = pe.transpose(bX[t][:, h * P:(h + 1) * P], Y[:, t, h, :], ident[:, :])
                            last.then_inc(xt2_done, 1)
                for i, (src, t) in enumerate(((vb, 0), (vb, 1), (kb, 1))):
                    pe.wait_ge(y_ready, 2 * LEVELS * q + 2 * (LEVELS - 1) + t + 1)
                    for h in range(HD):
                        last = pe.matmul(B[3][DK * h:DK * (h + 1), i * P:(i + 1) * P], src[:, t, DK * h:DK * (h + 1)],
                                         Y[:, t, h, :], start=True, stop=True)
                last.then_inc(uw_done, 1)
                pe.wait_ge(uw_ready, q + 1)
                for t in range(2):
                    last = pe.transpose(B[4][:, t * P:(t + 1) * P], uwT[:, t, :], ident[:, :])
                last.then_inc(ut_done, 1)
                pe.wait_ge(u_ready, q + 1)
                pe.matmul(B[5][:, 0:D], qkn[:, 1, 0, :], u[:, 0, :], start=True, stop=True).then_inc(st_done, 1)
                for h in range(HD):
                    pe.matmul(B[7][DK * h:DK * (h + 1), 0:P], u[:, 0, DK * h:DK * (h + 1)], AT[:, 0, h, :],
                              start=True, stop=True)
                pe.wait_ge(state_ready, q + 1)
                pe.matmul(B[6][:, 0:D], uwT[:, 2, :], state[:, :], start=True, stop=True).then_inc(ws_done, 1)
                pe.matmul(B[7][:, P:S2], state[:, :], qknT[:, 0, P:S2], start=True, stop=False, skip_group_check=True)
                pe.wait_ge(ua_ready, q + 1)
                for h in range(HD):
                    last = pe.matmul(B[7][DK * h:DK * (h + 1), P:S2], ua[:, DK * h:DK * (h + 1)], AT[:, 1, h, :],
                                     start=False, stop=True, skip_group_check=True)
                last.then_inc(ot_done, 1)
                pe.wait_ge(oT_ready, q + 1)
                for t in range(2):
                    last = pe.transpose(B[0][:, t * P:(t + 1) * P], oT[:, t * P:(t + 1) * P], ident[:, :])
                last.then_inc(o_done, 1)
                pe.wait_ge(o_ready, q + 1)

        @block.scalar
        def _(act):
            act.wait_ge(const_ready, 1)
            with act.Fori(0, nseq) as q:
                act.wait_ge(xt_done, q + 1)
                act.activation(xT[:, :], B[0][:, 0:S2], ACT.Copy).then_inc(xT_ready, 1)
                act.wait_ge(proj_done, 2 * q + 1)
                act.activation(pad[:, 0:2, TAPS - 1:], B[1][:, :].rearrange("p (i n) -> p i n", i=2),
                               ACT.Copy).then_inc(pad_ready, 1)
                act.wait_ge(proj_done, 2 * q + 2)
                act.activation(pad[:, 2, TAPS - 1:], B[2][:, 0:S2], ACT.Copy).then_inc(pad_ready, 1)
                act.activation(beta[:, 0, :, :].rearrange("p t h -> p (t h)"), B[2][:, S2:S2 + 2 * HD],
                               ACT.Sigmoid).then_inc(beta_sig, 1)
                for i in range(3):
                    act.wait_ge(conv_ready, 3 * TAPS * q + 3 * (TAPS - 1) + i + 1)
                    act.activation(qk[:, i, :] if i < 2 else vpad[:, SHORT - 1:], conv[:, i, :],
                                   ACT.Silu).then_inc(silu_ready, 1)
                act.wait_ge(tm_done, 2 * q + 1)
                act.activation(qk_tm[:, :, :, :].rearrange("p i t c -> p (i t c)"), B[3][:, :], ACT.Copy).then_inc(tm_ready, 1)
                act.wait_ge(tm_done, 2 * q + 2)
                act.wait_ge(kept, 3 * q)
                act.activation(vs_tm[:, :, :, :].rearrange("p i t c -> p (i t c)"), B[4][:, :], ACT.Copy).then_inc(tm_ready, 1)
                act.wait_ge(qknt_done, q + 1)
                act.activation(qknT[:, :, :].rearrange("p i n -> p (i n)"), B[0][:, :], ACT.Copy).then_inc(qknT_ready, 1)
                for t in range(2):
                    act.wait_ge(mt_done, 2 * q + t + 1)
                    act.activation(MT[:, t, :, :].rearrange("p h n -> p (h n)"), B[3 + t][:, :], ACT.Copy).then_inc(mt_ready, 1)
                for l in range(LEVELS):
                    if l:
                        for t in range(2):
                            act.wait_ge(p_done, 2 * (LEVELS - 1) * q + 2 * (l - 1) + t + 1)
                            act.activation(PX[:, t, :, :].rearrange("p h n -> p (h n)"), bP[t][:, :],
                                           ACT.Copy).then_inc(p_ready, 1)
                    if l < LEVELS - 1:
                        for t in range(2):
                            act.wait_ge(xt2_done, 2 * (LEVELS - 1) * q + 2 * l + t + 1)
                            act.activation(X[:, t, :, :].rearrange("p h n -> p (h n)"), bX[t][:, :],
                                           ACT.Copy).then_inc(x_ready, 1)
                act.wait_ge(uw_done, q + 1)
                act.activation(uwT[:, :, :].rearrange("p i n -> p (i n)"), B[3][:, 0:3 * P], ACT.Copy).then_inc(uw_ready, 1)
                act.wait_ge(ut_done, q + 1)
                act.activation(u[:, :, :].rearrange("p t n -> p (t n)"), B[4][:, 0:S2], ACT.Copy).then_inc(u_ready, 1)
                act.wait_ge(ot_done, q + 1)
                act.activation(oT[:, :], B[7][:, 0:S2], ACT.Copy).then_inc(oT_ready, 1)
                act.wait_ge(o_done, q + 1)
                act.activation(delta_tm[:, bass.ds(q * 2, 2), :], B[0][:, 0:S2].rearrange("p (t c) -> p t c", t=2),
                               ACT.Copy).then_inc(o_ready, 1)

        @block.vector
        def _(dve):
            dve.wait_ge(const_ready, 1)
            dve.wait_ge(loaded, 64)
            with dve.Fori(0, nseq) as q:
                for j in range(TAPS):
                    for i in range(3):
                        if j == 0:
                            dve.wait_ge(pad_ready, 2 * q + 1 + i // 2)
                            dve.tensor_scalar(conv[:, i, :], pad[:, i, 0:S2], taps[:, i, 0:1], None,
                                              ALU.mult).then_inc(conv_ready, 1)
                        else:
                            dve.wait_ge(conv_ready, 3 * TAPS * q + 3 * (j - 1) + i + 1)
                            dve.scalar_tensor_tensor(out=conv[:, i, :], in0=pad[:, i, j:j + S2],
                                                     scalar=taps[:, i, j:j + 1], in1=conv[:, i, :],
                                                     op0=ALU.mult, op1=ALU.add).then_inc(conv_ready, 1)
                dve.wait_ge(beta_sig, q + 1)
                dve.tensor_scalar(beta[:, 1, :, :], beta[:, 0, :, :], 1e-6, None, ALU.max).then_inc(dchain, 1)
                dve.wait_ge(silu_ready, 3 * q + 3)
                for j in range(SHORT):
                    if j == 0:
                        ins = dve.tensor_scalar(sf[:, :], vpad[:, 0:S2], ftaps[:, 0:1], None, ALU.mult)
                    else:
                        dve.wait_ge(dchain, NC * q + 1 + j)
                        ins = dve.scalar_tensor_tensor(out=sf[:, :], in0=vpad[:, j:j + S2], scalar=ftaps[:, j:j + 1],
                                                       in1=sf[:, :], op0=ALU.mult, op1=ALU.add)
                    ins.then_inc(dchain if j < SHORT - 1 else sf_ready, 1)
                dve.wait_ge(sq_ready, q + 1)
                dve.tensor_reduce(ss[:, 0, :], sq[:, :, :, :].rearrange("p i t (h c) -> p (i t h) c", h=HD),
                                  AX.X, ALU.add).then_inc(dchain, 1)
                dve.wait_ge(dchain, NC * q + SHORT + 1)
                dve.tensor_scalar(ss[:, 1, :], ss[:, 0, :], 1e-6, None, ALU.add).then_inc(ss_ready, 1)
                dve.wait_ge(tm_ready, 2 * q + 2)
                bt = beta[:, 1, :, :].unsqueeze(3).to_broadcast([P, 2, HD, DK])
                dve.wait_ge(rn_ready, q + 1)
                dve.tensor_tensor(qkn[:, :, :, :].rearrange("p i t (h c) -> p (i t h) c", h=HD),
                                  qk_tm[:, :, :, :].rearrange("p i t (h c) -> p (i t h) c", h=HD),
                                  rn[:, :].unsqueeze(2).to_broadcast([P, 4 * HD, DK]), ALU.mult).then_inc(qkn_ready, 1)
                dve.tensor_tensor(vb[:, :, :].rearrange("p t (h c) -> p t h c", h=HD),
                                  vs_tm[:, 0, :, :].rearrange("p t (h c) -> p t h c", h=HD), bt,
                                  ALU.mult).then_inc(dchain, 1)
                dve.wait_ge(qkn_ready, q + 1)
                dve.tensor_tensor(kb[:, :, :].rearrange("p t (h c) -> p t h c", h=HD),
                                  qkn[:, 1, :, :].rearrange("p t (h c) -> p t h c", h=HD), bt,
                                  ALU.mult).then_inc(dchain, 1)
                dve.wait_ge(qknT_ready, q + 1)
                for i in (1, 0):
                    for h in range(HD):
                        dve.tensor_scalar(qkx[:, i, :, h, :], qknT[:, i, :].rearrange("p (t n) -> p t n", t=2),
                                          hmask[:, h:h + 1], None, ALU.mult).then_inc(qkx_ready, 1)
                for t in range(2):
                    dve.wait_ge(kk_done, 2 * q + t + 1)
                    for h in range(HD):
                        last = dve.scalar_tensor_tensor(out=M[:, t, h, :], in0=B[5 + t][:, h * P:(h + 1) * P],
                                                        scalar=beta[:, 1, t, h:h + 1], in1=strict[:, :],
                                                        op0=ALU.mult, op1=ALU.mult)
                    last.then_inc(m_ready, 1)
                for t in range(2):
                    dve.wait_ge(at_done, 2 * q + t + 1)
                    dve.tensor_tensor(AT[:, t, :, :], B[1 + t][:, :].rearrange("p (h n) -> p h n", h=HD),
                                      causal[:, :].unsqueeze(1).to_broadcast([P, HD, P]), ALU.mult).then_inc(at_ready, 1)
                for t in range(2):
                    dve.wait_ge(ct_ready, 2 * LEVELS * q + t + 1)
                    dve.scalar_tensor_tensor(out=Y[:, t, :, :], in0=CT[:, t, 0, :, :], scalar=-1.0,
                                             in1=ident[:, :].unsqueeze(1).to_broadcast([P, HD, P]),
                                             op0=ALU.mult, op1=ALU.add).then_inc(y_ready, 1)
                for l in range(1, LEVELS):
                    for t in range(2):
                        dve.wait_ge(yy_done, 2 * (LEVELS - 1) * q + 2 * (l - 1) + t + 1)
                        dve.tensor_tensor(Y[:, t, :, :], Y[:, t, :, :],
                                          bY[t][:, :].rearrange("p (h n) -> p h n", h=HD),
                                          ALU.subtract).then_inc(y_ready, 1)
                dve.wait_ge(st_done, q + 1)
                dve.tensor_tensor(state[:, :], B[5][:, 0:D], blocks[:, 5, :], ALU.mult).then_inc(state_ready, 1)
                dve.wait_ge(ws_done, q + 1)
                dve.tensor_tensor(ua[:, :], u[:, 1, :], B[6][:, 0:D], ALU.subtract).then_inc(ua_ready, 1)


def long_filter(nc, a, ident, nseq, v_r, long_r):
    CH = 8
    NS2 = 2 * nseq
    W = P + LONG
    FW = 2 * P + LONG
    taps = a["dlt_long"]
    with ExitStack() as ctx:
        s = Space(nc, ctx, "fir")
        tz = s.sb("tz", [P, 2, CH, W])
        vcol = s.sb("vcol", [P, 2, CH, NS2])
        vrev = s.sb("vrev", [P, 2, CH, NS2])
        flip = s.sb("flip", [P, P])
        o4 = s.sb("o4", [P, 2, 2 * P])
        bF = [s.ps("bF0"), s.ps("bF1")]
        bT = [s.ps("bT0"), s.ps("bT1")]
        bV = [s.ps("bV0"), s.ps("bV1")]
        tz_loaded = [s.sem("tz_loaded0"), s.sem("tz_loaded1")]
        flip_ready, vcol_ready, flipped, vrev_ready, fir_done, o4_ready, turn_done, kept = (s.sem(n) for n in (
            "flip_ready", "vcol_ready", "flipped", "vrev_ready", "fir_done", "o4_ready", "turn_done", "kept"))
        block = s.block()
        turns = D // CH

        @block.sync
        def _(sp):
            with sp.Fori(0, turns // 2) as i:
                for half in range(2):
                    sp.wait_ge(fir_done, 2 * i)
                    src = taps[bass.ds((2 * i + half) * CH, CH), 0:W]
                    src = bass.AP(tensor=taps.tensor, offset=src.offset + 1, ap=[[1, P], [FW, CH], [1, W]])
                    sp.dma_start(tz[:, half, :, :], src).then_inc(tz_loaded[half], 16)
            for half in range(2):
                sp.wait_ge(tz_loaded[half], 16 * (turns // 2))

        @block.gpsimd
        def _(pool):
            pool.memset(flip[:, :], 0.0).then_inc(flip_ready, 1)
            pool.wait_ge(flip_ready, 1)
            pool.affine_select(out=flip[:, :], in_=flip[:, :], compare_op=ALU.not_equal, fill=1.0, base=1 - P,
                               pattern=[[1, P]], channel_multiplier=1).then_inc(flip_ready, 1)
            with pool.Fori(0, turns // 2) as i:
                for half in range(2):
                    pool.wait_ge(flipped, 2 * i)
                    pool.tensor_copy(vcol[:, half, :, :].rearrange("p c s -> p s c"),
                                     v_r[:, :, bass.ds((2 * i + half) * CH, CH)]).then_inc(vcol_ready, 1)

        @block.tensor
        def _(pe):
            def turn_over(i, half):
                pe.wait_ge(o4_ready, 2 * i + half + 1)
                for j in range(2):
                    last = pe.transpose(bT[half][:, j * P:(j + 1) * P], o4[:, half, j * P:(j + 1) * P], ident[:, :])
                last.then_inc(turn_done, 1)

            pe.wait_ge(flip_ready, 2)
            with pe.Fori(0, turns // 2) as i:
                for half in range(2):
                    pe.wait_ge(vcol_ready, 2 * i + half + 1)
                    pe.wait_ge(vrev_ready, 2 * i)
                    pe.matmul(bV[half][:, 0:CH * NS2], flip[:, :], vcol[:, half, :, :],
                              start=True, stop=True).then_inc(flipped, 1)
                for half in range(2):
                    pe.wait_ge(tz_loaded[half], 16 * i + 16)
                    pe.wait_ge(vrev_ready, 2 * i + half + 1)
                    pe.wait_ge(o4_ready, 2 * i)
                    for c in range(CH):
                        o = bF[half][32 * (c % 4):32 * (c % 4) + NS2, (c // 4) * P:(c // 4 + 1) * P]
                        pe.matmul(o, vrev[:, half, c, :], tz[:, half, c, 0:P], start=(c < 4), stop=False,
                                  skip_group_check=True)
                        last = pe.matmul(bF[half][32 * (c % 4):32 * (c % 4) + nseq, (c // 4) * P:(c // 4) * P + LONG],
                                         vrev[:, half, c, nseq:NS2], tz[:, half, c, P:W], start=False, stop=True,
                                         skip_group_check=True)
                    last.then_inc(fir_done, 1)
                    if half == 1:
                        turn_over(i, 0)
                turn_over(i, 1)

        @block.scalar
        def _(act):
            with act.Fori(0, turns // 2) as i:
                for half in range(2):
                    act.wait_ge(flipped, 2 * i + half + 1)
                    act.wait_ge(fir_done, 2 * i)
                    act.activation(vrev[:, half, :, :].rearrange("p c s -> p (c s)"), bV[half][:, 0:CH * NS2],
                                   ACT.Copy).then_inc(vrev_ready, 1)
                for half in range(2):
                    act.wait_ge(fir_done, 2 * i + half + 1)
                    act.wait_ge(turn_done, 2 * i)
                    act.activation(o4[:, half, :], bF[half][:, 0:2 * P], ACT.Copy).then_inc(o4_ready, 1)
                for half in range(2):
                    act.wait_ge(turn_done, 2 * i + half + 1)
                    act.activation(long_r[:, :, bass.ds((2 * i + half) * CH, CH)],
                                   bT[half][:, 0:2 * P].rearrange("p (c s) -> p s c", c=CH)[:, 0:NS2, :],
                                   ACT.Copy).then_inc(kept, 1)


def gate_and_project(nc, a, x, ident, ngroups, v_r, short_tm, long_r, delta_tm):
    NSTR = 4
    NC = 24
    HT = TILES * HD
    nseq = 2 * ngroups
    with ExitStack() as ctx:
        s = Space(nc, ctx, "gate")
        w1a = s.sb("w1a", [P, P])
        w1b = s.sb("w1b", [P, HD, P])
        w2 = s.sb("w2", [P, 32])
        ow = s.sb("ow", [P, 2, D])
        col = s.sb("col", [P, 3])
        tmp = s.sb("tmp", [P, 8])
        cr = s.sb("cr", [P, 2, HD])
        mhalf = s.sb("mhalf", [P, 64])
        half = s.sb("half", [P, 64])
        xg = s.sb("xg", [P, G])
        xT = s.sb("xT", [P, G])
        S = s.sb("S", [P, NSTR, TILES, D])
        cen = s.sb("cen", [P, NSTR, TILES, D])
        red = s.sb("red", [P, 6, 64])
        stz = s.sb("stz", [P, TILES, P])
        stT = s.sb("stT", [P, G])
        hg = s.sb("hg", [P, 2, G])
        lT = s.sb("lT", [P, G])
        lt = s.sb("lt", [P, HT, 4])
        pr = s.sb("pr", [P, 4, HT, 4])
        red2 = s.sb("red2", [P, 6, HT])
        mix = s.sb("mix", [P, 4, G])
        o = s.sb("o", [P, G])
        osq = s.sb("osq", [P, G])
        oT = s.sb("oT", [P, G])
        b_x, b_s, b_h0, b_h1, b_l, b_lt, b_o, b_y = (s.ps(n) for n in (
            "b_x", "b_s", "b_h0", "b_h1", "b_l", "b_lt", "b_o", "b_y"))
        b_h = (b_h0, b_h1)
        (loaded, setup_p, setup_v, setup_a, zeroed, xg_ready, s_ready, xt_done, xT_ready, chain, cen_ready, sq_ready,
         l2_in, l2_ready, st_ready, stt_done, stT_ready, h_done, hg_ready, l_done, lT_ready, lt_done, e_in, e_ready,
         prod_in, prod_ready, osq_ready, rms_in, rms_ready, o_ready, ot_done, oT_ready, y_done, x_ready, mixed) = (
            s.sem(n) for n in (
                "loaded setup_p setup_v setup_a zeroed xg_ready s_ready xt_done xT_ready chain cen_ready sq_ready "
                "l2_in l2_ready st_ready stt_done stT_ready h_done hg_ready l_done lT_ready lt_done e_in e_ready "
                "prod_in prod_ready osq_ready rms_in rms_ready o_ready ot_done oT_ready y_done x_ready mixed").split())
        block = s.block()
        NLOAD = 4 + 2 + 2 * HD + 2

        @block.sync
        def _(sp):
            sp.wait_ge(zeroed, 3)
            sp.dma_start(w1a[:, :], a["gate_w1a"]).then_inc(loaded, 16)
            sp.dma_start(w2[:, 0:4], a["gate_w2"]).then_inc(loaded, 16)
            sp.dma_start(ow[:, 0, :], a["gate_ow"]).then_inc(loaded, 16)
            sp.dma_start(col[:, 0:2], a["gate_cols"]).then_inc(loaded, 16)
            sp.dma_start(cr[:, 0, :], a["gate_res"].unsqueeze(0).to_broadcast([P, HD])).then_inc(loaded, 16)
            sp.dma_start(tmp[:, 0:1], a["gate_temp"].unsqueeze(0).to_broadcast([P, 1])).then_inc(loaded, 16)
            for h in range(HD):
                sp.dma_start(w1b[16 * h:16 * h + 16, h, :], a["gate_w1b"]).then_inc(loaded, 16)
                sp.dma_start(col[DK * h:DK * h + 4, 2:3], a["gate_b2"].rearrange("(p o) -> p o", o=1)).then_inc(loaded, 16)
            sp.wait_ge(loaded, 16 * (NLOAD - 2))

        @block.gpsimd
        def _(pool):
            pool.memset(w1b[:, :, :], 0.0).then_inc(zeroed, 1)
            pool.memset(w2[:, :], 0.0).then_inc(zeroed, 1)
            pool.memset(col[:, :], 0.0).then_inc(zeroed, 1)
            pool.memset(stz[:, :, :], 0.0).then_inc(setup_p, 1)
            pool.memset(mhalf[:, :], -0.5).then_inc(setup_p, 1)
            pool.memset(half[:, :], 0.5).then_inc(setup_p, 1)
            pool.wait_ge(setup_p, 3)
            with pool.Fori(0, ngroups) as g:
                pool.wait_ge(mixed, g)
                pool.wait_ge(xt_done, g)
                tiles = bass.ds(g * TILES, TILES)
                pool.tensor_copy(xg[:, :].rearrange("p (t c) -> p t c", t=TILES), x[:, tiles, :]).then_inc(xg_ready, 1)
                pool.tensor_copy(S[:, 0, :, :], short_tm[:, tiles, :]).then_inc(s_ready, 1)
                pool.wait_ge(l2_in, g + 1)
                pool.tensor_tensor(red[:, 5, :], red[:, 4, :], half[:, :], ALU.pow).then_inc(l2_ready, 1)
                pool.wait_ge(prod_in, g + 1)
                for i in (2, 3):
                    pool.tensor_tensor(mix[:, i, :].rearrange("p (t c) -> p t c", c=DK),
                                       S[:, i, :, :].rearrange("p t (h c) -> p (t h) c", c=DK),
                                       pr[:, 3, :, i:i + 1].to_broadcast([P, HT, DK]), ALU.mult).then_inc(prod_ready, 1)
                pool.wait_ge(rms_in, g + 1)
                pool.tensor_tensor(red2[:, 5, :], red2[:, 4, :], mhalf[:, 0:HT], ALU.pow).then_inc(rms_ready, 1)

        @block.tensor
        def _(pe):
            pe.wait_ge(loaded, 16 * (NLOAD - 2))
            pe.wait_ge(setup_v, 6)
            with pe.Fori(0, ngroups) as g:
                pe.wait_ge(xg_ready, g + 1)
                for t in range(TILES):
                    last = pe.transpose(b_x[:, t * P:(t + 1) * P], xg[:, t * P:(t + 1) * P], ident[:, :])
                last.then_inc(xt_done, 1)
                pe.wait_ge(st_ready, 4 * g + 4)
                for t in range(TILES):
                    last = pe.transpose(b_s[:, t * P:(t + 1) * P], stz[:, t, :], ident[:, :])
                last.then_inc(stt_done, 1)
                pe.wait_ge(xT_ready, g + 1)
                for h in range(HD + 1):
                    if h < HD:
                        if h >= 2:
                            pe.wait_ge(hg_ready, HD * g + h - 1)
                        pe.matmul(b_h[h % 2][:, :], w1a[:, :], xT[:, :], start=True, stop=False)
                        if h == 0:
                            pe.wait_ge(stT_ready, g + 1)
                        pe.matmul(b_h[h % 2][:, :], w1b[:, h, :], stT[:, :], start=False, stop=True).then_inc(h_done, 1)
                    if h >= 1:
                        pe.wait_ge(hg_ready, HD * g + h)
                        last = pe.matmul(b_l[32 * (h - 1):32 * h, :], w2[:, :], hg[:, (h - 1) % 2, :],
                                         start=True, stop=True).then_inc(l_done, 1)
                pe.wait_ge(lT_ready, g + 1)
                for t in range(TILES):
                    last = pe.transpose(b_lt[:, t * P:(t + 1) * P], lT[:, t * P:(t + 1) * P], ident[:, :])
                last.then_inc(lt_done, 1)
                pe.wait_ge(o_ready, g + 1)
                for t in range(TILES):
                    last = pe.transpose(b_o[:, t * P:(t + 1) * P], o[:, t * P:(t + 1) * P], ident[:, :])
                last.then_inc(ot_done, 1)
                pe.wait_ge(oT_ready, g + 1)
                for t in range(TILES):
                    last = pe.matmul(b_y[:, t * D:(t + 1) * D], oT[:, t * P:(t + 1) * P], ow[:, 1, :],
                                     start=True, stop=True)
                last.then_inc(y_done, 1)
                pe.wait_ge(x_ready, g + 1)

        @block.scalar
        def _(act):
            act.wait_ge(loaded, 16 * (NLOAD - 2))
            act.wait_ge(setup_v, 2)
            act.activation(tmp[:, 3:4], tmp[:, 2:3], ACT.Exp, scale=-1.0).then_inc(setup_a, 1)
            act.wait_ge(setup_a, 1)
            act.activation(tmp[:, 4:5], tmp[:, 3:4], ACT.Ln, bias=1.0).then_inc(setup_a, 1)
            act.activation(cr[:, 1, :], cr[:, 0, :], ACT.Sigmoid).then_inc(setup_a, 1)
            with act.Fori(0, ngroups) as g:
                tiles = bass.ds(g * TILES, TILES)
                act.wait_ge(mixed, g)
                act.activation(S[:, 2, :, :], delta_tm[:, tiles, :], ACT.Copy).then_inc(s_ready, 1)
                for src, i in ((v_r, 3), (long_r, 1)):
                    for b in range(2):
                        act.activation(S[:, i, 1 - b::2, :], src[:, bass.ds(b * nseq + 2 * g, 2), :],
                                       ACT.Copy).then_inc(s_ready, 1)
                act.wait_ge(xt_done, g + 1)
                act.activation(xT[:, :], b_x[:, :], ACT.Copy).then_inc(xT_ready, 1)
                act.wait_ge(cen_ready, g + 1)
                act.activation(cen[:, :, :, :], cen[:, :, :, :], ACT.Square).then_inc(sq_ready, 1)
                act.wait_ge(stt_done, g + 1)
                act.activation(stT[:, :], b_s[:, :], ACT.Copy).then_inc(stT_ready, 1)
                for h in range(HD):
                    act.wait_ge(h_done, HD * g + h + 1)
                    if h >= 2:
                        act.wait_ge(l_done, HD * g + h - 1)
                    act.activation(hg[:, h % 2, :], b_h[h % 2][:, :], ACT.Gelu_apprx_tanh,
                                   bias=col[:, 0:1]).then_inc(hg_ready, 1)
                act.wait_ge(l_done, HD * (g + 1))
                act.activation(lT[:, :], b_l[:, :], ACT.Identity, bias=col[:, 2:3]).then_inc(lT_ready, 1)
                act.wait_ge(e_in, g + 1)
                act.activation(pr[:, 1, :, :], pr[:, 0, :, :], ACT.Exp, scale=tmp[:, 6:7]).then_inc(e_ready, 1)
                act.wait_ge(ot_done, g + 1)
                act.activation(oT[:, :], b_o[:, :], ACT.Copy).then_inc(oT_ready, 1)
                act.wait_ge(y_done, g + 1)
                act.activation(x[:, tiles, :], b_y[:, :].rearrange("p (t c) -> p t c", t=TILES),
                               ACT.Copy).then_inc(x_ready, 1)

        @block.vector
        def _(dve):
            dve.wait_ge(loaded, 16 * (NLOAD - 2))
            dve.wait_ge(setup_p, 3)
            dve.tensor_scalar(tmp[:, 1:2], tmp[:, 0:1], -1.0, None, ALU.mult).then_inc(setup_v, 1)
            dve.wait_ge(setup_v, 1)
            dve.tensor_tensor(tmp[:, 2:3], tmp[:, 0:1], tmp[:, 1:2], ALU.max).then_inc(setup_v, 1)
            dve.wait_ge(setup_a, 3)
            dve.tensor_scalar(tmp[:, 7:8], tmp[:, 0:1], 0.0, None, ALU.max).then_inc(setup_v, 1)
            dve.wait_ge(setup_v, 3)
            dve.tensor_tensor(tmp[:, 5:6], tmp[:, 7:8], tmp[:, 4:5], ALU.add).then_inc(setup_v, 1)
            dve.wait_ge(setup_v, 4)
            dve.reciprocal(tmp[:, 6:7], tmp[:, 5:6]).then_inc(setup_v, 1)
            dve.tensor_scalar(ow[:, 1, :], ow[:, 0, :], col[:, 1:2], None, ALU.mult).then_inc(setup_v, 1)
            dve.wait_ge(setup_v, 6)
            with dve.Fori(0, ngroups) as g:
                n = NC * g

                def link(ins):
                    nonlocal n
                    n = n + 1
                    ins.then_inc(chain, 1)
                    dve.wait_ge(chain, n)

                rows = S[:, :, :, :].rearrange("p s t (h c) -> p (s t h) c", c=DK)
                crow = cen[:, :, :, :].rearrange("p s t (h c) -> p (s t h) c", c=DK)
                stat = stz[:, :, 0:HD * 16].rearrange("p t (h s k) -> p k s t h", h=HD, s=NSTR)

                def put(k, src):
                    v = src.rearrange("p (s t h) -> p s t h", s=NSTR, t=TILES)
                    for i in range(NSTR):
                        last = dve.tensor_copy(stat[:, k, i, :, :], v[:, i, :, :])
                    last.then_inc(st_ready, 1)

                dve.wait_ge(s_ready, 6 * g + 6)
                dve.wait_ge(stt_done, g)
                link(dve.tensor_reduce(red[:, 0, :], rows, AX.X, ALU.add))
                link(dve.tensor_scalar(red[:, 1, :], red[:, 0, :], 1.0 / DK, None, ALU.mult))
                dve.tensor_tensor(crow, rows, red[:, 1, :].unsqueeze(2).to_broadcast([P, 64, DK]),
                                  ALU.subtract).then_inc(cen_ready, 1)
                link(dve.tensor_reduce(red[:, 0, :], rows, AX.X, ALU.add, apply_absolute_value=True))
                link(dve.tensor_scalar(red[:, 0, :], red[:, 0, :], 1.0 / DK, None, ALU.mult))
                put(0, red[:, 1, :])
                put(2, red[:, 0, :])
                dve.wait_ge(sq_ready, g + 1)
                link(dve.tensor_reduce(red[:, 2, :], crow, AX.X, ALU.add))
                link(dve.tensor_scalar(red[:, 3, :], red[:, 2, :], 1.0 / DK, None, ALU.mult))
                link(dve.tensor_tensor(red[:, 4, :], red[:, 1, :], red[:, 1, :], ALU.mult))
                link(dve.tensor_tensor(red[:, 4, :], red[:, 4, :], red[:, 3, :], ALU.add))
                dve.tensor_scalar(red[:, 4, :], red[:, 4, :], float(DK), None, ALU.mult).then_inc(l2_in, 1)
                put(1, red[:, 3, :])
                dve.wait_ge(l2_ready, g + 1)
                put(3, red[:, 5, :])
                dve.wait_ge(lt_done, g + 1)
                lo = b_lt[:, :].rearrange("p (a e) -> p a e", e=32)[:, :, 0:4]
                link(dve.tensor_copy(lt[:, :, :], lo))
                link(dve.tensor_reduce(red2[:, 0, :], lt[:, :, :], AX.X, ALU.max))
                dve.tensor_tensor(pr[:, 0, :, :], lt[:, :, :], red2[:, 0, :].unsqueeze(2).to_broadcast([P, HT, 4]),
                                  ALU.subtract).then_inc(e_in, 1)
                dve.wait_ge(e_ready, g + 1)
                for i in (1, 2):
                    link(dve.tensor_reduce(red2[:, i, :], pr[:, i, :, :], AX.X, ALU.add))
                    link(dve.reciprocal(red2[:, 3, :], red2[:, i, :]))
                    link(dve.tensor_tensor(pr[:, i + 1, :, :], pr[:, i, :, :],
                                           red2[:, 3, :].unsqueeze(2).to_broadcast([P, HT, 4]), ALU.mult))
                    if i == 1:
                        link(dve.tensor_scalar(pr[:, 2, :, :], pr[:, 2, :, :], 0.02, None, ALU.max))
                dve.tensor_tensor(pr[:, 3, :, 0].rearrange("p (t h) -> p t h", h=HD),
                                  pr[:, 3, :, 0].rearrange("p (t h) -> p t h", h=HD),
                                  cr[:, 1, :].unsqueeze(1).to_broadcast([P, TILES, HD]), ALU.add).then_inc(prod_in, 1)
                dve.wait_ge(prod_in, g + 1)
                for i in (0, 1):
                    ins = dve.tensor_tensor(mix[:, i, :].rearrange("p (t c) -> p t c", c=DK),
                                            S[:, i, :, :].rearrange("p t (h c) -> p (t h) c", c=DK),
                                            pr[:, 3, :, i:i + 1].to_broadcast([P, HT, DK]), ALU.mult)
                    link(ins)
                link(dve.tensor_tensor(o[:, :], mix[:, 0, :], mix[:, 1, :], ALU.add))
                for i in (2, 3):
                    dve.wait_ge(prod_ready, 2 * g + i - 1)
                    link(dve.tensor_tensor(o[:, :], o[:, :], mix[:, i, :], ALU.add))
                dve.tensor_copy(red2[:, 0, 0:1], red2[:, 1, 0:1]).then_inc(mixed, 1)
                link(dve.tensor_tensor(osq[:, :], o[:, :], o[:, :], ALU.mult))
                link(dve.tensor_reduce(red2[:, 3, :], osq[:, :].rearrange("p (a c) -> p a c", c=DK), AX.X, ALU.add))
                dve.tensor_scalar(red2[:, 4, :], red2[:, 3, :], 1.0 / DK, 1e-5, ALU.mult, ALU.add).then_inc(rms_in, 1)
                dve.wait_ge(rms_ready, g + 1)
                dve.tensor_tensor(o[:, :].rearrange("p (a c) -> p a c", c=DK), o[:, :].rearrange("p (a c) -> p a c", c=DK),
                                  red2[:, 5, :].unsqueeze(2).to_broadcast([P, HT, DK]), ALU.mult).then_inc(o_ready, 1)


def lay_out(i):
    import numpy as np

    def A(n):
        return np.asarray(i["L0_attn_" + n])

    nl = A("Wq").shape[0]
    out = {}
    mats = [A(n).transpose(1, 0, 2) for n in ("Wq", "Wk", "Wv", "Wo", "W1")]
    mats.append(A("W2").reshape(nl, FB, P, D).transpose(2, 0, 1, 3).reshape(P, nl, FB * D))
    out["enc_mats"] = np.ascontiguousarray(np.concatenate(mats, axis=2))
    out["enc_rows"] = np.ascontiguousarray(np.concatenate(
        [A(n) for n in ("bv", "bo", "g1", "be1", "bf2", "g2", "be2")], axis=1))
    cols = [A(n).T[:, :, None] for n in ("bq", "bk", "g1", "be1")]
    cols.append(A("bf1").reshape(nl, FB, P).transpose(2, 0, 1))
    out["enc_cols"] = np.ascontiguousarray(np.concatenate(cols, axis=2))
    out["L0_attn_omega"] = A("omega")
    w1, w2, wr = (np.asarray(i["L0_ffn_" + n]) for n in ("W1", "W2", "Wr"))
    out["moe0_up"] = np.ascontiguousarray(w1.reshape(NE, 2, 2, P, D).transpose(4, 0, 1, 2, 3))
    out["moe0_down"] = np.ascontiguousarray(w2.reshape(NE, D, 2, P).transpose(3, 0, 2, 1))
    out["moe0_router"] = np.ascontiguousarray(wr.T)
    w1, w2, cf, cp, gw = (np.asarray(i["L1_ffn_" + n]) for n in ("w1", "w2", "cfc", "cproj", "gate_w"))
    out["moe1_up"] = np.ascontiguousarray(np.concatenate([w1, cf[None]]).transpose(2, 0, 1)[:, :, None, None, :])
    out["moe1_down"] = np.ascontiguousarray(np.concatenate([w2, cp[None]]).transpose(2, 0, 1)[:, :, None, :])
    out["moe1_router"] = np.ascontiguousarray(gw.T)
    w = [np.asarray(i[f"L1_attn_{n}_w"]).T[:, None, :] for n in "qkv"]
    out["dlt_wqkv"] = np.ascontiguousarray(np.concatenate(w, axis=1))
    out["dlt_bw"] = np.ascontiguousarray(np.asarray(i["L1_attn_b_w"]).T)
    out["dlt_taps"] = np.ascontiguousarray(np.stack([np.asarray(i[f"L1_attn_{n}_cw"]) for n in "qkv"], axis=1))
    out["dlt_short"] = np.asarray(i["L1_attn_fir_short_w"]).reshape(D, SHORT)
    f = np.asarray(i["L1_attn_fir_long_w"]).reshape(D, LONG)[:, ::-1]
    out["dlt_long"] = np.ascontiguousarray(np.pad(f, ((0, 0), (P, P))))
    w1 = np.asarray(i["L1_attn_mlp1_w"]).T
    out["gate_w1a"], out["gate_w1b"] = np.ascontiguousarray(w1[:D]), np.ascontiguousarray(w1[D:])
    out["gate_w2"] = np.ascontiguousarray(np.asarray(i["L1_attn_mlp2_w"]).T)
    out["gate_ow"] = np.ascontiguousarray(np.asarray(i["L1_attn_o_w"]).T)
    out["gate_cols"] = np.ascontiguousarray(np.stack(
        [np.asarray(i["L1_attn_mlp1_b"]), np.tile(np.asarray(i["L1_attn_norm_w"]), HD)], axis=1))
    out["gate_res"] = np.asarray(i["L1_attn_conv_res_logit"])
    out["gate_temp"] = np.asarray(i["L1_attn_logit_temp"])
    out["gate_b2"] = np.asarray(i["L1_attn_mlp2_b"])
    out["moe1_bias"] = np.asarray(i["L1_ffn_lb_bias"])
    return out


def store_tokens(nc, resid, update, out, ngroups):
    with ExitStack() as ctx:
        s = Space(nc, ctx, "out")
        row = s.sb("row", [P, ngroups, TILES, D])
        summed, stored = s.sem("summed"), s.sem("stored")
        block = s.block()

        @block.vector
        def _(dve):
            for g in range(ngroups):
                tiles = slice(g * TILES, (g + 1) * TILES)
                dve.tensor_tensor(row[:, g, :, :], resid[:, tiles, :], update[:, tiles, :],
                                  ALU.add).then_inc(summed, 1)

        @block.sync
        def _(sp):
            for g in range(ngroups):
                sp.wait_ge(summed, g + 1)
                sp.dma_start(out[g * G:(g + 1) * G, :].rearrange("(t p) c -> p t c", p=P),
                             row[:, g, :, :]).then_inc(stored, 16)
            sp.wait_ge(stored, 16 * ngroups)


def program(nc, a, out):
    ntok = a["x"].shape[0]
    ngroups, nseq, tiles = ntok // G, ntok // SEQ, ntok // P
    with ExitStack() as ctx:
        s = Space(nc, ctx, "top")
        resid, x = s.sb("resid", [P, tiles, D]), s.sb("x", [P, tiles, D])
        ident = s.sb("ident", [P, P])
        load_tokens(nc, a["x"], resid, x, ident, ngroups)
        residual_norm(nc, "n0", resid, None, x, ngroups)
        encoder(nc, a, x, ident)
        residual_norm(nc, "n1", resid, x, x, ngroups)
        mixture(nc, "moe0", x, ident, ngroups, NE, 2, a["moe0_up"], a["moe0_down"], a["moe0_router"], None)
        residual_norm(nc, "n2", resid, x, x, ngroups)
        with ExitStack() as inner:
            streams = Space(nc, inner, "str")
            v_r, short_tm, long_r, delta_tm = (streams.sb(n, [P, tiles, D]) for n in ("v", "short", "long", "delta"))
            delta_mixer(nc, a, x, ident, nseq, v_r, short_tm, delta_tm)
            long_filter(nc, a, ident, nseq, v_r, long_r)
            gate_and_project(nc, a, x, ident, ngroups, v_r, short_tm, long_r, delta_tm)
        residual_norm(nc, "n3", resid, x, x, ngroups)
        mixture(nc, "moe1", x, ident, ngroups, NE + 1, 1, a["moe1_up"], a["moe1_down"], a["moe1_router"],
                a["moe1_bias"])
        store_tokens(nc, resid, x, out, ngroups)


def kernel(**inputs):
    import numpy as np
    import concourse.bacc as bacc
    from concourse.bass_utils import run_bass_kernel_spmd

    laid = lay_out(inputs)
    x = np.asarray(inputs["L0_attn_x"])
    laid["x"] = np.ascontiguousarray(x.reshape(-1, D))
    nc = bacc.Bacc("TRN2", target_bir_lowering=False, num_devices=1)
    arrays = {f"in_{n}": v for n, v in laid.items()}
    a = {n: nc.dram_tensor(f"in_{n}", v.shape, mybir.dt.from_np(v.dtype), kind="ExternalInput").ap()
         for n, v in laid.items()}
    out = nc.dram_tensor("out_y", laid["x"].shape, F32, kind="ExternalOutput").ap()
    program(nc, a, out)
    r = run_bass_kernel_spmd(nc, [arrays], core_ids=[0])
    return r.results[0]["out_y"].reshape(x.shape)
```

```python
from contextlib import ExitStack

import concourse.bass as bass
from concourse import mybir

F32 = mybir.dt.float32
U32 = mybir.dt.uint32
ALU = mybir.AluOpType
ACT = mybir.ActivationFunctionType
AX = mybir.AxisListType

P = 128
D = 128
TILES = 4
G = TILES * P
SEQ = 256


class Space:

    def __init__(self, nc, ctx, tag):
        self.nc, self.ctx, self.tag = nc, ctx, tag
        self.sems = []

    def sb(self, name, shape, dt=F32):
        return self.ctx.enter_context(self.nc.sbuf_tensor(f"{self.tag}_{name}", shape, dt))

    def ps(self, name):
        return self.ctx.enter_context(self.nc.psum_tensor(f"{self.tag}_{name}", [P, 512], F32))

    def sem(self, name):
        handle = self.ctx.enter_context(self.nc.semaphore(f"{self.tag}_{name}"))
        self.sems.append(handle.num)
        return handle

    def block(self):
        self.ctx.callback(self.clear)
        return self.ctx.enter_context(self.nc.Block())

    def clear(self):
        nums = sorted(self.sems)
        starts = [n for n in nums if n - 1 not in nums]
        ends = [n + 1 for n in nums if n + 1 not in nums]
        with self.nc.Block() as block:
            @block.gpsimd
            def _(pool):
                for first, end in zip(starts, ends):
                    pool.sem_clear(range(first, end))


def apart(eng, passes):
    eng.sem_inc(passes, 1)


def load_tokens(nc, x_dram, resid, ident, ngroups):
    with ExitStack() as ctx:
        s = Space(nc, ctx, "ld")
        loaded = [s.sem(f"loaded{g}") for g in range(ngroups)]
        zeroed, ident_ready = s.sem("zeroed"), s.sem("ident_ready")
        block = s.block()

        @block.sync
        def _(sp):
            for g in range(ngroups):
                sp.dma_start(resid[:, g * TILES:(g + 1) * TILES, :],
                             x_dram[g * G:(g + 1) * G, :].rearrange("(t p) c -> p t c", p=P)
                             ).then_inc(loaded[g], 16)
            for g in range(ngroups):
                sp.wait_ge(loaded[g], 16)

        @block.gpsimd
        def _(pool):
            pool.memset(ident[:, :], 0.0).then_inc(zeroed, 1)
            pool.wait_ge(zeroed, 1)
            pool.affine_select(out=ident[:, :], in_=ident[:, :], compare_op=ALU.not_equal, fill=1.0,
                               base=0, pattern=[[-1, P]], channel_multiplier=1).then_inc(ident_ready, 1)


def residual_norm(nc, tag, resid, update, normed, ngroups):
    with ExitStack() as ctx:
        s = Space(nc, ctx, tag)
        row = s.sb("row", [P, 2, TILES, D])
        st6 = s.sb("st6", [P, TILES, 6])
        mv = s.sb("mv", [P, 2, TILES, 2])
        veps = s.sb("veps", [P, 2, TILES])
        mhalf = s.sb("mhalf", [P, TILES])
        rstd = s.sb("rstd", [P, 2, TILES])
        const_ready, summed, stats, var_ready, rstd_ready, normed_ready, stored, passes = (s.sem(n) for n in (
            "const_ready", "summed", "stats", "var_ready", "rstd_ready", "normed_ready", "stored", "passes"))
        block = s.block()

        @block.gpsimd
        def _(pool):
            pool.memset(mhalf[:, :], -0.5).then_inc(const_ready, 1)
            pool.wait_ge(const_ready, 1)
            with pool.Fori(0, ngroups // 2) as i:
                for b in range(2):
                    pool.wait_ge(var_ready, 2 * i + b + 1)
                    pool.tensor_tensor(rstd[:, b, :], veps[:, b, :], mhalf[:, :], ALU.pow).then_inc(rstd_ready, 1)

        @block.scalar
        def _(act):
            if update is not None:
                with act.Fori(0, ngroups // 2) as i:
                    for b in range(2):
                        act.wait_ge(summed, 2 * i + b + 1)
                        act.activation(resid[:, bass.ds((2 * i + b) * TILES, TILES), :], row[:, b, :, :],
                                       ACT.Copy).then_inc(stored, 1)

        @block.vector
        def _(dve):
            def moments(g, b, reused):
                tiles = bass.ds(g * TILES, TILES)
                if reused:
                    dve.wait_ge(normed_ready, TILES * (g - 1))
                    if update is not None:
                        dve.wait_ge(stored, g - 1)
                if update is None:
                    dve.tensor_copy(row[:, b, :, :], resid[:, tiles, :]).then_inc(summed, 1)
                else:
                    dve.tensor_tensor(row[:, b, :, :], resid[:, tiles, :], update[:, tiles, :],
                                      ALU.add).then_inc(summed, 1)
                dve.wait_ge(summed, g + 1)
                apart(dve, passes)
                for t in range(TILES):
                    dve.bn_stats(st6[:, t, :], row[:, b, t, :]).then_inc(stats, 1)
                dve.wait_ge(stats, g * 2 * TILES + TILES)
                apart(dve, passes)
                for t in range(TILES):
                    dve.bn_aggr(mv[:, b, t, :], st6[:, t, :]).then_inc(stats, 1)
                dve.wait_ge(stats, (g + 1) * 2 * TILES)
                dve.tensor_scalar(veps[:, b, :], mv[:, b, :, 1], 1e-5, None, ALU.add).then_inc(var_ready, 1)

            def scale(g, b):
                dve.wait_ge(rstd_ready, g + 1)
                for t in range(TILES):
                    dve.tensor_scalar(normed[:, bass.ds(g * TILES + t, 1), :].rearrange("p a c -> p (a c)"),
                                      row[:, b, t, :], mv[:, b, t, 0:1], rstd[:, b, t:t + 1],
                                      ALU.subtract, ALU.mult).then_inc(normed_ready, 1)

            moments(0, 0, False)
            moments(1, 1, False)
            scale(0, 0)
            with dve.Fori(0, ngroups // 2 - 1) as i:
                moments(2 * i + 2, 0, True)
                scale(2 * i + 1, 1)
                moments(2 * i + 3, 1, True)
                scale(2 * i + 2, 0)
            scale(ngroups - 1, 1)


NL = 6
NH = 16
DH = 8
MF = 16
DFF = 512
FB = DFF // P
C_WQ, C_WK, C_WV, C_WO, C_W1, C_W2 = 0, 128, 256, 384, 512, 1024
C_BV, C_BO, C_G1, C_BE1, C_BF2, C_G2, C_BE2 = (1536 + 128 * i for i in range(7))
C_OM = 1536 + 7 * 128
C_BQ = C_OM + DH
C_BK, C_G1C, C_BE1C, C_BF1C = C_BQ + 1, C_BQ + 2, C_BQ + 3, C_BQ + 4
NPAR = C_BF1C + FB


def encoder(nc, a, x, ident, nlayers=NL, ngroups=8):
    with ExitStack() as ctx:
        s = Space(nc, ctx, "enc")
        params = s.sb("params", [P, nlayers, NPAR])
        w = s.sb("w", [P, NPAR])
        om = s.sb("om", [P, 2, P])
        nb = s.sb("nb", [P, 2, P])
        own = s.sb("own", [P, NH])
        negown = s.sb("negown", [P, NH])
        hm = s.sb("hm", [P, 8])
        ones = s.sb("ones", [P, P])
        cm = s.sb("cm", [P, P])
        bm = s.sb("bm", [P, 2, 4, 2, 2, DH])
        mhalf = s.sb("mhalf", [P, TILES])
        xg = s.sb("xg", [P, G])
        xb = s.sb("xb", [P, G])
        xT = s.sb("xT", [P, G])
        q = s.sb("q", [P, G])
        k = s.sb("k", [P, G])
        qsq = s.sb("qsq", [P, G])
        ksq = s.sb("ksq", [P, G])
        vx = s.sb("vx", [P, TILES, NH, 32])
        vc = s.sb("vc", [P, 2, NH // 2, 32])
        qf = s.sb("qf", [P, 2, G])
        kf = s.sb("kf", [P, 2, G])
        qx = s.sb("qx", [P, 2, 8, G])
        kt = s.sb("kt", [P, 2, 2, P])
        st = s.sb("st", [P, 2, 2, P])
        sm = s.sb("sm", [P, 4, 4, P])
        osb = s.sb("osb", [P, 2, 2 * P])
        den = s.sb("den", [P, 2, NH])
        at = s.sb("at", [P, TILES, D])
        aT = s.sb("aT", [P, G])
        h = s.sb("h", [P, TILES, D])
        y1 = s.sb("y1", [P, TILES, D])
        h1 = s.sb("h1", [P, TILES, D])
        h1T = s.sb("h1T", [P, G])
        hid = s.sb("hid", [P, FB, G])
        h2 = s.sb("h2", [P, TILES, D])
        y2 = s.sb("y2", [P, TILES, D])
        beb = s.sb("beb", [P, D])
        st6 = s.sb("st6", [P, TILES, 6])
        mv = s.sb("mv", [P, 2, TILES, 2])
        veps = s.sb("veps", [P, 2, TILES])
        rstd = s.sb("rstd", [P, 2, TILES])

        b_t, b_1, b_2, b_tok = (s.ps(n) for n in ("b_t", "b_1", "b_2", "b_tok"))
        b_o = [s.ps("b_o0"), s.ps("b_o1")]
        b_sc = [s.ps("b_sc0"), s.ps("b_sc1")]

        loaded = s.sem("loaded")
        const, masks_ready, w_ready, om_ready = (s.sem(n) for n in ("const", "masks_ready", "w_ready", "om_ready"))
        xg_ready, xb_ready, sq_ready, vc_ready, h1_ready, rstd_ready = (
            s.sem(n) for n in ("xg_ready", "xb_ready", "sq_ready", "vc_ready", "h1_ready", "rstd_ready"))
        xt_done, qk_done, v_done, phi_done, kt_done, st_done, sc_done, av_done, ot_done, at_done, wo_done, \
            ht_done, hid_done, ffn_done = (s.sem(n) for n in (
                "xt_done", "qk_done", "v_done", "phi_done", "kt_done", "st_done", "sc_done", "av_done",
                "ot_done", "at_done", "wo_done", "ht_done", "hid_done", "ffn_done"))
        qk_ready, v_ready, qx_ready, st_ready, sm_ready, den_step, a_ready, h_ready, ln_step, var_ready, \
            y1_ready, h2_ready, x_ready = (s.sem(n) for n in (
                "qk_ready", "v_ready", "qx_ready", "st_ready", "sm_ready", "den_step", "a_ready", "h_ready",
                "ln_step", "var_ready", "y1_ready", "h2_ready", "x_ready"))
        xT_ready, f_ready, kt_ready, o_ready, aT_ready, h1T_ready, hid_ready = (
            s.sem(n) for n in ("xT_ready", "f_ready", "kt_ready", "o_ready", "aT_ready", "h1T_ready", "hid_ready"))
        qx1_ready, y2_step, bias_ready = s.sem("qx1_ready"), s.sem("y2_step"), s.sem("bias_ready")
        passes = s.sem("passes")
        dve_const = s.sem("dve_const")
        block = s.block()

        @block.sync
        def _(sp):
            sp.dma_start(params[:, :, 0:C_BV], a["enc_mats"][:, 0:nlayers, :]).then_inc(loaded, 16)
            sp.dma_start(params[:, :, C_BV:C_OM],
                         a["enc_rows"][0:nlayers].unsqueeze(0).to_broadcast([P, nlayers, C_OM - C_BV])
                         ).then_inc(loaded, 16)
            sp.dma_start(params[:, :, C_BQ:NPAR], a["enc_cols"][:, 0:nlayers, :]).then_inc(loaded, 16)
            for hd in range(NH):
                sp.dma_start(params[hd * DH:(hd + 1) * DH, :, C_OM:C_OM + DH],
                             a["L0_attn_omega"][0:nlayers].rearrange("l d m -> d l m")).then_inc(loaded, 16)
            sp.wait_ge(loaded, 16 * (3 + NH))

        @block.gpsimd
        def _(pool):
            n = 0

            def step(ins):
                nonlocal n
                n += 1
                ins.then_inc(const, 1)
                pool.wait_ge(const, n)

            step(pool.memset(ones[:, :], 1.0))
            step(pool.memset(mhalf[:, :], -0.5))
            step(pool.memset(cm[:, :], 1.0 / MF))
            step(pool.affine_select(out=cm[:, :], in_=cm[:, :], compare_op=ALU.is_ge, fill=0.0, base=0,
                                    pattern=[[1, P]], channel_multiplier=-1))
            step(pool.affine_select(out=own[:, :], in_=ones[:, 0:NH], compare_op=ALU.is_ge, fill=0.0, base=0,
                                    pattern=[[-DH, NH]], channel_multiplier=1))
            step(pool.affine_select(out=own[:, :], in_=own[:, :], compare_op=ALU.is_ge, fill=0.0, base=DH - 1,
                                    pattern=[[DH, NH]], channel_multiplier=-1))
            step(pool.affine_select(out=hm[:, :], in_=ones[:, 0:8], compare_op=ALU.is_ge, fill=0.0, base=0,
                                    pattern=[[-MF, 8]], channel_multiplier=1))
            step(pool.affine_select(out=hm[:, :], in_=hm[:, :], compare_op=ALU.is_ge, fill=0.0, base=MF - 1,
                                    pattern=[[MF, 8]], channel_multiplier=-1))
            step(pool.memset(vx[:, :, :, :], 0.0))
            for par in (0, 1):
                step(pool.memset(vx[:, :, par::2, 16 + DH * par:24 + DH * par], 1.0))
            pool.memset(vc[:, :, :, 16:32], 1.0).then_inc(masks_ready, 1)

            def residual(it):
                pool.wait_ge(xg_ready, it + 1)
                pool.tensor_tensor(
                    xb[:, :].rearrange("p (t c) -> p t c", t=TILES),
                    xg[:, :].rearrange("p (t c) -> p t c", t=TILES),
                    w[:, C_BO:C_BO + D].unsqueeze(1).to_broadcast([P, TILES, D]), ALU.add).then_inc(xb_ready, 1)

            def first_norm(it):
                pool.wait_ge(var_ready, 2 * it + 1)
                pool.tensor_tensor(rstd[:, 0, :], veps[:, 0, :], mhalf[:, :], ALU.pow).then_inc(rstd_ready, 1)

            def values(it):
                pool.wait_ge(v_ready, it + 1)
                apart(pool, passes)
                for i in range(2):
                    for par in (0, 1):
                        pool.tensor_copy(vc[:, i, :, DH * par:DH * par + DH],
                                         vx[:, 2 * i, par::2, DH * par:DH * par + DH]).then_inc(vc_ready, 1)

            def ffn_side(it, g):
                pool.wait_ge(y1_ready, TILES * (it + 1))
                pool.tensor_tensor(h1[:, :, :], y1[:, :, :], w[:, C_G1:C_G1 + D].unsqueeze(1).to_broadcast([P, TILES, D]),
                                   ALU.mult).then_inc(h1_ready, 1)
                pool.wait_ge(h1_ready, 2 * it + 1)
                pool.tensor_tensor(h1[:, :, :], h1[:, :, :], beb[:, :].unsqueeze(1).to_broadcast([P, TILES, D]),
                                   ALU.add).then_inc(h1_ready, 1)
                pool.wait_ge(var_ready, 2 * it + 2)
                pool.tensor_tensor(rstd[:, 1, :], veps[:, 1, :], mhalf[:, :], ALU.pow).then_inc(rstd_ready, 1)
                pool.wait_ge(rstd_ready, 2 * it + 2)
                apart(pool, passes)
                for t in range(TILES):
                    pool.tensor_scalar(y2[:, t, :], h2[:, t, :], mv[:, 1, t, 0:1], rstd[:, 1, t:t + 1],
                                       ALU.subtract, ALU.mult).then_inc(y2_step, 1)
                pool.wait_ge(y2_step, 5 * it + TILES)
                pool.tensor_tensor(y2[:, :, :], y2[:, :, :], w[:, C_G2:C_G2 + D].unsqueeze(1).to_broadcast([P, TILES, D]),
                                   ALU.mult).then_inc(y2_step, 1)
                pool.wait_ge(y2_step, 5 * it + TILES + 1)
                pool.tensor_tensor(x[:, bass.ds(g * TILES, TILES), :], y2[:, :, :],
                                   w[:, C_BE2:C_BE2 + D].unsqueeze(1).to_broadcast([P, TILES, D]),
                                   ALU.add).then_inc(x_ready, 1)

            pool.sem_inc(x_ready, 1)
            with pool.Fori(0, nlayers) as l:
                pool.wait_ge(w_ready, l + 1)
                pool.tensor_tensor(beb[:, :], w[:, C_BE1:C_BE1 + D], w[:, C_BF2:C_BF2 + D],
                                   ALU.add).then_inc(bias_ready, 1)
                pool.wait_ge(bias_ready, l + 1)
                first = l * ngroups
                residual(first)
                values(first)
                with pool.Fori(0, ngroups - 1) as g:
                    it = first + g
                    first_norm(it)
                    residual(it + 1)
                    values(it + 1)
                    ffn_side(it, g)
                last_it = first + (ngroups - 1)
                first_norm(last_it)
                ffn_side(last_it, ngroups - 1)

        @block.tensor
        def _(pe):
            def turn_input(it):
                pe.wait_ge(xg_ready, it + 1)
                for t in range(TILES):
                    last = pe.transpose(b_1[:, t * P:(t + 1) * P], xg[:, t * P:(t + 1) * P], ident[:, :])
                last.then_inc(xt_done, 1)

            def project(it):
                pe.wait_ge(xT_ready, it + 1)
                for c, b in ((C_WQ, b_1), (C_WK, b_tok)):
                    pe.matmul(b[:, :], w[:, c:c + D], xT[:, :], start=True, stop=True).then_inc(qk_done, 1)

            def values(it):
                for t in range(TILES):
                    last = pe.matmul(b_t[:, t * D:(t + 1) * D], xT[:, t * P:(t + 1) * P], w[:, C_WV:C_WV + D],
                                     start=True, stop=True)
                last.then_inc(v_done, 1)

            def exponents(it, i):
                f, b, lin, sq = ((0, b_1, q, qsq), (0, b_o[0], k, ksq), (1, b_2, q, qsq), (1, b_1, k, ksq))[i]
                if i < 2:
                    pe.wait_ge(qk_ready, 2 * it + i + 1)
                if i == 3:
                    pe.wait_ge(f_ready, 4 * it + 1)
                pe.matmul(b[:, :], om[:, f, :], lin[:, :], start=True, stop=False)
                pe.wait_ge(sq_ready, 2 * it + i % 2 + 1)
                pe.matmul(b[:, :], nb[:, f, :], sq[:, :], start=False, stop=True).then_inc(phi_done, 1)

            def turn_keys(it):
                pe.wait_ge(f_ready, 4 * it + 4)
                for i in range(2):
                    for f in range(2):
                        last = pe.transpose(b_2[:, (2 * i + f) * P:(2 * i + f + 1) * P],
                                            kf[:, f, 2 * i * P:(2 * i + 1) * P], ident[:, :])
                last.then_inc(kt_done, 1)

            def scores(it, c):
                t, f, n = c // 4, c // 2 % 2, c % 4
                if c < 4:
                    pe.wait_ge(qx_ready if n < 2 else qx1_ready, 8 * it + 4 * (n % 2 + 1))
                if c >= 2:
                    pe.wait_ge(sm_ready, 16 * it + c - 1)
                for b in range(4):
                    last = pe.matmul(
                        b_sc[c % 2][32 * b:32 * b + 32, :].rearrange("p (h i) -> p h i", h=4)[:, :, 32 * b:P],
                        kf[:, f, t * P + 32 * b:t * P + 32 * b + 32],
                        qx[:, f, 4 * (n % 2):4 * (n % 2) + 4, t * P + 32 * b:(t + 1) * P],
                        start=True, stop=True)
                last.then_inc(sc_done, 1)

            def combine(it, c):
                t, f, n = c // 4, c // 2 % 2, c % 4
                if n == 0 and t >= 2:
                    pe.wait_ge(o_ready, TILES * it + t - 1)
                if n == 0 and t == 1:
                    pe.wait_ge(st_ready, it + 1)
                pe.wait_ge(sm_ready, 16 * it + c + 1)
                for pair in (2 * n, 2 * n + 1):
                    o = b_o[t % 2][32 * (pair % 4):32 * (pair % 4) + 32,
                                   (pair // 4) * P:(pair // 4 + 1) * P]
                    for j in (0, 1):
                        hd = 2 * pair + j
                        last = pe.matmul(o, vx[:, t, hd, :], sm[:, c % 4, hd % 4, :],
                                         start=(pair < 4 and j == 0), stop=(j == 1 and t % 2 == 0),
                                         skip_group_check=True)
                    if t % 2:
                        last = pe.matmul(o, st[:, t // 2, f, 32 * (pair % 4):32 * (pair % 4) + 32],
                                  qf[:, f, t * P:(t + 1) * P], start=False, stop=True, skip_group_check=True)
                last.then_inc(av_done, 1)

            def turn(it, t):
                pe.wait_ge(o_ready, TILES * it + t + 1)
                if t == 0:
                    pass
                else:
                    pe.wait_ge(a_ready, TILES * it + t)
                for i in range(2):
                    last = pe.transpose(b_2[:, i * P:(i + 1) * P], osb[:, t % 2, i * P:(i + 1) * P], ident[:, :])
                last.then_inc(ot_done, 1)

            def turn_back(it, t):
                pe.wait_ge(a_ready, TILES * it + t + 1)
                pe.transpose(b_t[:, t * P:(t + 1) * P], at[:, t, :], ident[:, :]).then_inc(at_done, 1)

            def states(it):
                pe.wait_ge(kt_ready, it + 1)
                pe.wait_ge(vc_ready, 4 * it + 4)
                for i in range(2):
                    for f in range(2):
                        last = pe.matmul(b_t[:, (2 * i + f) * P:(2 * i + f + 1) * P], kt[:, i, f, :],
                                         vc[:, i, 4 * f:4 * f + 4, :], start=True, stop=True)
                last.then_inc(st_done, 1)

            def out_projection(it):
                pe.wait_ge(aT_ready, it + 1)
                for t in range(TILES):
                    last = pe.matmul(b_tok[:, t * D:(t + 1) * D], aT[:, t * P:(t + 1) * P], w[:, C_WO:C_WO + D],
                                     start=True, stop=True)
                last.then_inc(wo_done, 1)

            def ffn(it, follows):
                pe.wait_ge(y1_ready, TILES * (it + 1))
                for t in range(TILES):
                    last = pe.transpose(b_o[0][:, t * P:(t + 1) * P], y1[:, t, :], ident[:, :])
                last.then_inc(ht_done, 1)
                if follows:
                    scores(it + 1, 1)
                pe.wait_ge(h1T_ready, it + 1)
                for f in range(FB):
                    if f >= 2:
                        pe.wait_ge(hid_ready, FB * it + f - 1)
                    pe.matmul(b_o[1 - f % 2][:, :], w[:, C_W1 + f * P:C_W1 + (f + 1) * P], h1T[:, :],
                              start=True, stop=True).then_inc(hid_done, 1)
                for f in range(FB):
                    pe.wait_ge(hid_ready, FB * it + f + 1)
                    for t in range(TILES):
                        last = pe.matmul(b_tok[:, t * D:(t + 1) * D], hid[:, f, t * P:(t + 1) * P],
                                         w[:, C_W2 + f * D:C_W2 + (f + 1) * D], start=(f == 0 and t == 0),
                                         stop=(f == FB - 1), skip_group_check=True)
                last.then_inc(ffn_done, 1)

            def group(it, follows):
                for c in range(4 * TILES + 1):
                    if 2 <= c < 4 * TILES:
                        scores(it, c)
                    if c == 1:
                        states(it)
                    if 1 <= c:
                        combine(it, c - 1)
                    if c in (6, 10, 14):
                        turn(it, c // 4 - 1)
                    if c in (8, 12, 16):
                        turn_back(it, c // 4 - 2)
                    if follows and c == 6:
                        turn_input(it + 1)
                    if follows and c == 8:
                        project(it + 1)
                if follows:
                    exponents(it + 1, 0)
                turn(it, TILES - 1)
                if follows:
                    exponents(it + 1, 1)
                turn_back(it, TILES - 1)
                if follows:
                    exponents(it + 1, 2)
                out_projection(it)
                if follows:
                    exponents(it + 1, 3)
                    values(it + 1)
                    turn_keys(it + 1)
                    scores(it + 1, 0)
                ffn(it, follows)

            pe.wait_ge(masks_ready, 1)
            with pe.Fori(0, nlayers) as l:
                pe.wait_ge(om_ready, 2 * l + 2)
                apart(pe, passes)
                first = l * ngroups
                turn_input(first)
                project(first)
                for i in range(4):
                    exponents(first, i)
                values(first)
                turn_keys(first)
                for c in range(2):
                    scores(first, c)
                with pe.Fori(0, ngroups - 1) as g:
                    group(first + g, True)
                group(first + (ngroups - 1), False)

        @block.scalar
        def _(act):
            def fetch(it, g):
                act.activation(xg[:, :].rearrange("p (t c) -> p t c", t=TILES), x[:, bass.ds(g * TILES, TILES), :],
                               ACT.Copy).then_inc(xg_ready, 1)

            def turned(it):
                act.wait_ge(xt_done, it + 1)
                act.activation(xT[:, :], b_1[:, :], ACT.Copy).then_inc(xT_ready, 1)

            def squares(it):
                for i, (sq, v) in enumerate(((qsq, q), (ksq, k))):
                    act.wait_ge(qk_ready, 2 * it + i + 1)
                    act.activation(sq[:, :], v[:, :], ACT.Square).then_inc(sq_ready, 1)

            def features(it, i):
                f, b, dst = ((0, b_1, qf), (0, b_o[0], kf), (1, b_2, qf), (1, b_1, kf))[i]
                act.wait_ge(phi_done, 4 * it + i + 1)
                act.activation(dst[:, f, :], b[:, :], ACT.Exp).then_inc(f_ready, 1)

            def expand(it, half):
                for hd in range(4 * half, 4 * half + 4):
                    act.activation(qx[:, 1, hd, :], qf[:, 1, :], ACT.Identity,
                                   scale=hm[:, hd:hd + 1]).then_inc(qx1_ready, 1)

            def keys(it):
                act.wait_ge(kt_done, it + 1)
                act.activation(kt[:, :, :, :].rearrange("p a b c -> p (a b c)"), b_2[:, :],
                               ACT.Copy).then_inc(kt_ready, 1)

            def outputs(it, t):
                act.wait_ge(av_done, 16 * it + 4 * (t + 1))
                act.activation(osb[:, t % 2, :], b_o[t % 2][:, 0:2 * P], ACT.Copy).then_inc(o_ready, 1)

            def group(it, g, follows):
                outputs(it, 0)
                if follows:
                    act.wait_ge(xb_ready, it + 1)
                    fetch(it + 1, g + 1)
                    turned(it + 1)
                outputs(it, 1)
                if follows:
                    squares(it + 1)
                outputs(it, 2)
                outputs(it, 3)
                if follows:
                    features(it + 1, 0)
                    features(it + 1, 1)
                act.wait_ge(at_done, TILES * (it + 1))
                act.activation(aT[:, :], b_t[:, :], ACT.Copy).then_inc(aT_ready, 1)
                if follows:
                    features(it + 1, 2)
                    features(it + 1, 3)
                    act.wait_ge(f_ready, 4 * it + 7)
                    expand(it + 1, 0)
                    keys(it + 1)
                act.wait_ge(ht_done, it + 1)
                act.activation(h1T[:, :], b_o[0][:, :], ACT.Identity, scale=w[:, C_G1C:C_G1C + 1],
                               bias=w[:, C_BE1C:C_BE1C + 1]).then_inc(h1T_ready, 1)
                for f in range(FB):
                    act.wait_ge(hid_done, FB * it + f + 1)
                    act.activation(hid[:, f, :], b_o[1 - f % 2][:, :], ACT.Relu,
                                   bias=w[:, C_BF1C + f:C_BF1C + f + 1]).then_inc(hid_ready, 1)
                if follows:
                    expand(it + 1, 1)

            act.wait_ge(loaded, 16 * (3 + NH))
            act.wait_ge(masks_ready, 1)
            with act.Fori(0, nlayers) as l:
                first = l * ngroups
                act.wait_ge(x_ready, first + 1)
                act.activation(w[:, :], params[:, bass.ds(l, 1), :].rearrange("p a b -> p (a b)"),
                               ACT.Copy).then_inc(w_ready, 1)
                fetch(first, 0)
                turned(first)
                squares(first)
                for i in range(4):
                    features(first, i)
                act.wait_ge(f_ready, 4 * first + 3)
                expand(first, 0)
                keys(first)
                expand(first, 1)
                with act.Fori(0, ngroups - 1) as g:
                    group(first + g, g, True)
                group(first + (ngroups - 1), ngroups - 1, False)

        @block.vector
        def _(dve):
            def queries_keys(it):
                for i, (dst, b, c) in enumerate(((q, b_1, C_BQ), (k, b_tok, C_BK))):
                    dve.wait_ge(qk_done, 2 * it + i + 1)
                    dve.tensor_scalar(dst[:, :], b[:, :], w[:, c:c + 1], scale, ALU.add,
                                      ALU.mult).then_inc(qk_ready, 1)

            def values(it):
                dve.wait_ge(v_done, it + 1)
                for par in (0, 1):
                    last = dve.tensor_tensor(
                        vx[:, :, par::2, DH * par:DH * par + DH],
                        b_t[:, :].rearrange("p (t a b d) -> p t a b d", t=TILES, a=8, b=2)[:, :, :, par, :],
                        w[:, C_BV:C_BV + D].rearrange("p (a b d) -> p a b d", a=8, b=2)[:, :, par, :]
                        .unsqueeze(1).to_broadcast([P, TILES, 8, DH]), ALU.add)
                last.then_inc(v_ready, 1)

            def expand(it, start, end):
                if start == 0:
                    dve.wait_ge(f_ready, 4 * it + 1)
                for hd in range(start, end):
                    dve.tensor_scalar(qx[:, 0, hd, :], qf[:, 0, :], hm[:, hd:hd + 1], None,
                                      ALU.mult).then_inc(qx_ready, 1)

            def mask(it, c):
                dve.wait_ge(sc_done, 16 * it + c + 1)
                if c >= 4:
                    dve.wait_ge(av_done, 16 * it + c - 3)
                dve.tensor_tensor(sm[:, c % 4, :, :], b_sc[c % 2][:, :].rearrange("p (h i) -> p h i", h=4),
                                  cm[:, :].unsqueeze(1).to_broadcast([P, 4, P]), ALU.mult).then_inc(sm_ready, 1)

            def normalise(it, t):
                dve.wait_ge(ot_done, TILES * it + t + 1)
                o = b_2[:, 0:256].rearrange("p (a k j d) -> p a k j d", k=2, j=2, d=DH)
                dve.tensor_scalar(den[:, 0, :].rearrange("p (a j) -> p a j", j=2), o[:, :, 1, :, 0],
                                  1e-6, None, ALU.add).then_inc(den_step, 1)
                dve.wait_ge(den_step, 2 * (TILES * it + t) + 1)
                dve.reciprocal(den[:, 1, :], den[:, 0, :]).then_inc(den_step, 1)
                dve.wait_ge(den_step, 2 * (TILES * it + t) + 2)
                dve.tensor_tensor(at[:, t, :].rearrange("p (a j d) -> p a j d", j=2, d=DH), o[:, :, 0, :, :],
                                  den[:, 1, :].rearrange("p (a j) -> p a j", j=2).unsqueeze(3)
                                  .to_broadcast([P, 8, 2, DH]), ALU.mult).then_inc(a_ready, 1)

            def moments(it, which, src):
                base = (2 * it + which) * 2 * TILES
                for t in range(TILES):
                    dve.bn_stats(st6[:, t, :], src[:, t, :]).then_inc(ln_step, 1)
                dve.wait_ge(ln_step, base + TILES)
                apart(dve, passes)
                for t in range(TILES):
                    dve.bn_aggr(mv[:, which, t, :], st6[:, t, :]).then_inc(ln_step, 1)
                dve.wait_ge(ln_step, base + 2 * TILES)
                dve.tensor_scalar(veps[:, which, :], mv[:, which, :, 1], 1e-5, None, ALU.add).then_inc(var_ready, 1)

            def group(it, follows):
                for c in range(4 * TILES):
                    if c >= 2:
                        mask(it, c)
                    if c == 1:
                        dve.wait_ge(st_done, it + 1)
                        dve.tensor_tensor(
                            st[:, :, :, :].rearrange("p i f c -> p (i f) c"),
                            b_t[:, :].rearrange("p (i c) -> p i c", i=4),
                            bm[:, 0, :, :, :, :].rearrange("p a k j d -> p (a k j d)").unsqueeze(1)
                            .to_broadcast([P, 4, P]), ALU.mult).then_inc(st_ready, 1)
                    if c >= 5 and c % 4 == 2:
                        normalise(it, c // 4 - 1)
                    if follows and c == 9:
                        queries_keys(it + 1)
                normalise(it, TILES - 1)
                if follows:
                    expand(it + 1, 0, 6)
                dve.wait_ge(wo_done, it + 1)
                dve.wait_ge(xb_ready, it + 1)
                dve.tensor_tensor(h[:, :, :].rearrange("p t c -> p (t c)"), b_tok[:, :], xb[:, :],
                                  ALU.add).then_inc(h_ready, 1)
                dve.wait_ge(h_ready, it + 1)
                moments(it, 0, h)
                if follows:
                    expand(it + 1, 6, 8)
                dve.wait_ge(rstd_ready, 2 * it + 1)
                for t in range(TILES):
                    dve.tensor_scalar(y1[:, t, :], h[:, t, :], mv[:, 0, t, 0:1], rstd[:, 0, t:t + 1],
                                      ALU.subtract, ALU.mult).then_inc(y1_ready, 1)
                if follows:
                    values(it + 1)
                    mask(it + 1, 0)
                    mask(it + 1, 1)
                dve.wait_ge(ffn_done, it + 1)
                dve.wait_ge(h1_ready, 2 * it + 2)
                dve.tensor_tensor(h2[:, :, :].rearrange("p t c -> p (t c)"), b_tok[:, :],
                                  h1[:, :, :].rearrange("p t c -> p (t c)"), ALU.add).then_inc(h2_ready, 1)
                dve.wait_ge(h2_ready, it + 1)
                moments(it, 1, h2)

            scale = float(DH) ** -0.25
            dve.wait_ge(masks_ready, 1)
            for i in range(2):
                dve.memset(b_sc[i][:, :], 0.0).then_inc(dve_const, 1)
            dve.tensor_scalar(negown[:, :], own[:, :], -1.0, None, ALU.mult).then_inc(dve_const, 1)
            dve.tensor_scalar(nb[:, :, :].rearrange("p f (h m) -> p (f h) m", m=MF),
                              own[:, :].unsqueeze(2).to_broadcast([P, NH, MF]), -0.5, None, ALU.mult).then_inc(dve_const, 1)
            for kind in range(2):
                dve.tensor_scalar(bm[:, 0, :, kind, :, :],
                                  hm[:, :].rearrange("p (a b) -> p a b", a=4).unsqueeze(3).to_broadcast([P, 4, 2, DH]),
                                  1.0 / MF, None, ALU.mult).then_inc(dve_const, 1)
            dve.wait_ge(dve_const, 6)
            with dve.Fori(0, nlayers) as l:
                dve.wait_ge(w_ready, l + 1)
                for sign, o in ((0, own), (1, negown)):
                    dve.tensor_tensor(
                        om[:, :, :].rearrange("p f (h m) -> p (f h) m", m=MF)[:, :, DH * sign:DH * sign + DH],
                        w[:, C_OM:C_OM + DH].unsqueeze(1).to_broadcast([P, NH, DH]),
                        o[:, :].unsqueeze(2).to_broadcast([P, NH, DH]), ALU.mult).then_inc(om_ready, 1)
                first = l * ngroups
                queries_keys(first)
                expand(first, 0, 8)
                values(first)
                mask(first, 0)
                mask(first, 1)
                with dve.Fori(0, ngroups - 1) as g:
                    group(first + g, True)
                group(first + (ngroups - 1), False)


NE = 8


def mixture(nc, tag, x, ident, ngroups, experts, blocks, up_dram, down_dram, router_dram, bias_dram):
    gated = bias_dram is None
    ways = 2 if gated else 1
    units = [(e, f) for e in range(experts) for f in range(blocks)]
    U = len(units)
    with ExitStack() as ctx:
        s = Space(nc, ctx, tag)
        up = s.sb("up", [P, experts, ways, blocks, P])
        down = s.sb("down", [P, experts, blocks, D])
        wr = s.sb("wr", [P, NE])
        bias = s.sb("bias", [P, NE])
        xg = s.sb("xg", [P, G])
        xT = s.sb("xT", [P, G])
        act = s.sb("act", [P, 2, G])
        hid = s.sb("hid", [P, 3, G])
        acc = s.sb("acc", [P, TILES, D])
        index = s.sb("index", [P, NE])
        lg = s.sb("lg", [P, TILES, NE])
        lb = s.sb("lb", [P, TILES, NE])
        top = s.sb("top", [P, TILES, 8])
        tidx = s.sb("tidx", [P, TILES, 8], U32)
        tif = s.sb("tif", [P, TILES, 8])
        eq1 = s.sb("eq1", [P, TILES, NE])
        eq2 = s.sb("eq2", [P, TILES, NE])
        score = s.sb("score", [P, TILES, NE])
        total = s.sb("total", [P, 2, TILES])
        rw = s.sb("rw", [P, TILES, experts])
        b_t, b_r = s.ps("b_t"), s.ps("b_r")
        b_v = [s.ps("b_v0"), s.ps("b_v1")]
        b_g = [s.ps("b_g0"), s.ps("b_g1")] if gated else b_v
        b_y = [s.ps("b_y0"), s.ps("b_y1")]
        loaded, const_ready = s.sem("loaded"), s.sem("const_ready")
        xg_ready, xt_done, xT_ready, lg_done, route, route_act, score_ready, rw_ready = (s.sem(n) for n in (
            "xg_ready", "xt_done", "xT_ready", "lg_done", "route", "route_act", "score_ready", "rw_ready"))
        up_done, act_ready, hid_ready, down_done, acc_ready, stored = (s.sem(n) for n in (
            "up_done", "act_ready", "hid_ready", "down_done", "acc_ready", "stored"))
        acc_step, chain, passes = s.sem("acc_step"), s.sem("chain"), s.sem("passes")
        block = s.block()
        NLOAD = 3 if gated else 4

        @block.sync
        def _(sp):
            sp.dma_start(wr[:, :], router_dram).then_inc(loaded, 16)
            sp.dma_start(up[:, :, :, :, :], up_dram).then_inc(loaded, 16)
            sp.dma_start(down[:, :, :, :], down_dram).then_inc(loaded, 16)
            if not gated:
                sp.dma_start(bias[:, :], bias_dram.unsqueeze(0).to_broadcast([P, NE])).then_inc(loaded, 16)
            sp.wait_ge(loaded, 16 * NLOAD)

        @block.gpsimd
        def _(pool):
            for e in range(NE):
                pool.memset(index[:, e:e + 1], float(e)).then_inc(const_ready, 1)
            pool.memset(rw[:, :, :], 1.0).then_inc(const_ready, 1)

            def fetch(g, n):
                pool.tensor_copy(xg[:, :].rearrange("p (t c) -> p t c", t=TILES),
                                 x[:, bass.ds(g * TILES, TILES), :]).then_inc(xg_ready, 1)

            fetch(0, 0)
            with pool.Fori(0, ngroups - 1) as g:
                pool.wait_ge(xt_done, g + 1)
                fetch(g + 1, g + 1)
                pool.wait_ge(acc_ready, g + 1)
                pool.tensor_copy(x[:, bass.ds(g * TILES, TILES), :], acc[:, :, :]).then_inc(stored, 1)
            pool.wait_ge(acc_ready, ngroups)
            pool.tensor_copy(x[:, (ngroups - 1) * TILES:ngroups * TILES, :], acc[:, :, :]).then_inc(stored, 1)

        @block.tensor
        def _(pe):
            def turn(g):
                pe.wait_ge(xg_ready, g + 1)
                for t in range(TILES):
                    last = pe.transpose(b_t[:, t * P:(t + 1) * P], xg[:, t * P:(t + 1) * P], ident[:, :])
                last.then_inc(xt_done, 1)

            def logits(g):
                pe.wait_ge(xT_ready, g + 1)
                for t in range(TILES):
                    last = pe.matmul(b_r[:, t * NE:(t + 1) * NE], xT[:, t * P:(t + 1) * P], wr[:, :],
                                     start=True, stop=True)
                last.then_inc(lg_done, 1)

            def expand(g, u):
                e, f = units[u]
                if u >= 2:
                    pe.wait_ge(hid_ready, g * U + u - 1)
                for i in reversed(range(ways)):
                    last = pe.matmul((b_v, b_g)[i][u % 2][:, :], up[:, e, i, f, :], xT[:, :], start=True, stop=True)
                last.then_inc(up_done, 1)

            def contract(g, u):
                e, f = units[u]
                pe.wait_ge(hid_ready, g * U + u + 1)
                if f == 0:
                    pe.wait_ge(acc_step, (g * experts + max(e - 1, 0)) * TILES)
                for t in range(TILES):
                    last = pe.matmul(b_y[e % 2][:, t * D:(t + 1) * D], hid[:, u % 3, t * P:(t + 1) * P],
                                     down[:, e, f, :], start=(f == 0 and t == 0), stop=(f == blocks - 1),
                                     skip_group_check=True)
                last.then_inc(down_done, 1)

            def group(g, ahead):
                for u in range(U + 2):
                    if u < U:
                        expand(g, u)
                    elif u == U and ahead:
                        turn(g + 1)
                    if u >= 2:
                        contract(g, u - 2)
                if ahead:
                    logits(g + 1)

            pe.wait_ge(loaded, 16 * NLOAD)
            turn(0)
            logits(0)
            with pe.Fori(0, ngroups - 1) as g:
                group(g, True)
            group(ngroups - 1, False)

        @block.scalar
        def _(act_e):
            def copy_x(g):
                act_e.wait_ge(xt_done, g + 1)
                act_e.activation(xT[:, :], b_t[:, :], ACT.Copy).then_inc(xT_ready, 1)

            def group(g, ahead):
                for u in range(U):
                    if u == 2:
                        act_e.wait_ge(route, g + 1)
                        act_e.activation(score[:, :, :], score[:, :, :],
                                         ACT.Exp if gated else ACT.Sigmoid).then_inc(route_act, 1)
                    act_e.wait_ge(up_done, g * U + u + 1)
                    if u >= 2:
                        act_e.wait_ge(hid_ready, g * U + u - 1)
                    act_e.activation(act[:, u % 2, :], b_g[u % 2][:, :],
                                     ACT.Silu if gated else ACT.Relu).then_inc(act_ready, 1)
                if ahead:
                    copy_x(g + 1)

            copy_x(0)
            with act_e.Fori(0, ngroups - 1) as g:
                group(g, True)
            group(ngroups - 1, False)

        @block.vector
        def _(dve):
            def router(g):
                n = NR * g

                def link(ins):
                    nonlocal n
                    n = n + 1
                    ins.then_inc(chain, 1)
                    dve.wait_ge(chain, n)
                    apart(dve, passes)

                dve.wait_ge(lg_done, g + 1)
                link(dve.tensor_copy(lg[:, :, :].rearrange("p t e -> p (t e)"), b_r[:, 0:TILES * NE]))
                if gated:
                    pick = lg
                else:
                    pick = lb
                    link(dve.tensor_tensor(lb[:, :, :], lg[:, :, :], bias[:, :].unsqueeze(1).to_broadcast([P, TILES, NE]),
                                           ALU.add))
                for t in range(TILES):
                    link(dve.max(top[:, t, :], pick[:, t, :]))
                for t in range(TILES):
                    link(dve.max_index(tidx[:, t, :], top[:, t, :], pick[:, t, :]))
                if gated:
                    dve.tensor_tensor(score[:, :, :], lg[:, :, :], top[:, :, 0:1].to_broadcast([P, TILES, NE]),
                                      ALU.subtract).then_inc(route, 1)
                else:
                    dve.tensor_copy(score[:, :, :], lg[:, :, :]).then_inc(route, 1)
                link(dve.tensor_copy(tif[:, :, :], tidx[:, :, :]))
                for i, eq in enumerate((eq1, eq2)):
                    link(dve.tensor_tensor(eq[:, :, :], index[:, :].unsqueeze(1).to_broadcast([P, TILES, NE]),
                                           tif[:, :, i:i + 1].to_broadcast([P, TILES, NE]), ALU.is_equal))
                link(dve.tensor_tensor(eq1[:, :, :], eq1[:, :, :], eq2[:, :, :], ALU.add))
                dve.wait_ge(route_act, g + 1)
                link(dve.tensor_tensor(eq1[:, :, :], eq1[:, :, :], score[:, :, :], ALU.mult))
                link(dve.tensor_reduce(total[:, 0, :], eq1[:, :, :], AX.X, ALU.add))
                if not gated:
                    link(dve.tensor_scalar(total[:, 0, :], total[:, 0, :], 1e-6, None, ALU.add))
                link(dve.reciprocal(total[:, 1, :], total[:, 0, :]))
                link(dve.tensor_tensor(rw[:, :, 0:NE], eq1[:, :, :], total[:, 1, :].unsqueeze(2)
                                       .to_broadcast([P, TILES, NE]), ALU.mult))

            NR = 17 if gated else 19

            def product(g, u):
                dve.wait_ge(act_ready, g * U + u + 1)
                if u >= 3:
                    dve.wait_ge(down_done, g * U + u - 2)
                dve.tensor_tensor(hid[:, u % 3, :], b_v[u % 2][:, :], act[:, u % 2, :], ALU.mult).then_inc(hid_ready, 1)

            def gather(g, e):
                dve.wait_ge(down_done, g * U + (e + 1) * blocks)
                if e == 0:
                    dve.wait_ge(stored, g)
                else:
                    dve.wait_ge(acc_step, (g * experts + e) * TILES)
                for t in range(TILES):
                    y, wt = b_y[e % 2][:, t * D:(t + 1) * D], rw[:, t, e:e + 1]
                    if e == 0:
                        dve.tensor_scalar(acc[:, t, :], y, wt, None, ALU.mult).then_inc(acc_step, 1)
                    else:
                        dve.scalar_tensor_tensor(out=acc[:, t, :], in0=y, scalar=wt, in1=acc[:, t, :],
                                                 op0=ALU.mult, op1=ALU.add).then_inc(acc_step, 1)

            def group(g):
                product(g, 0)
                product(g, 1)
                router(g)
                for u in range(2, U + 3):
                    if u < U:
                        product(g, u)
                    if u >= 3 and units[u - 3][1] == blocks - 1:
                        gather(g, units[u - 3][0])
                dve.wait_ge(acc_step, (g + 1) * experts * TILES)
                dve.tensor_copy(total[:, 0, 0:1], total[:, 1, 0:1]).then_inc(acc_ready, 1)

            dve.wait_ge(const_ready, NE + 1)
            dve.wait_ge(loaded, 16 * NLOAD)
            with dve.Fori(0, ngroups) as g:
                group(g)


HD = 4
DK = 32
LEVELS = 7
TAPS, SHORT, LONG = 4, 5, 64


def delta_mixer(nc, a, x, ident, nseq, v_r, short_tm, delta_tm):
    S2 = 2 * P
    NC = SHORT + 1
    with ExitStack() as ctx:
        s = Space(nc, ctx, "dlt")
        wqkv = s.sb("wqkv", [P, 3, D])
        bw = s.sb("bw", [P, HD])
        taps = s.sb("taps", [P, 3, TAPS])
        ftaps = s.sb("ftaps", [P, SHORT])
        ones = s.sb("ones", [P, P])
        hmask = s.sb("hmask", [P, HD])
        strict = s.sb("strict", [P, P])
        causal = s.sb("causal", [P, P])
        blocks = s.sb("blocks", [P, LEVELS + 1, P])
        couple = s.sb("couple", [P, LEVELS, P])
        mhalf = s.sb("mhalf", [P, 4 * HD])
        xg = s.sb("xg", [P, S2])
        xT = s.sb("xT", [P, S2])
        pad = s.sb("pad", [P, 3, TAPS - 1 + S2])
        conv = s.sb("conv", [P, 3, S2])
        qk = s.sb("qk", [P, 2, S2])
        vpad = s.sb("vpad", [P, SHORT - 1 + S2])
        sf = s.sb("sf", [P, S2])
        beta = s.sb("beta", [P, 2, 2, HD])
        qk_tm = s.sb("qk_tm", [P, 2, 2, D])
        vs_tm = s.sb("vs_tm", [P, 2, 2, D])
        sq = s.sb("sq", [P, 2, 2, D])
        ss = s.sb("ss", [P, 2, 4 * HD])
        rn = s.sb("rn", [P, 4 * HD])
        qkn = s.sb("qkn", [P, 2, 2, D])
        kb = s.sb("kb", [P, 2, D])
        vb = s.sb("vb", [P, 2, D])
        k0 = s.sb("k0", [P, D])
        qT1 = s.sb("qT1", [P, P])
        qknT = s.sb("qknT", [P, 2, S2])
        qkx = s.sb("qkx", [P, 2, 2, HD, P])
        M = s.sb("M", [P, 2, HD, P])
        MT = s.sb("MT", [P, 2, HD, P])
        AT = s.sb("AT", [P, 2, HD, P])
        CT = s.sb("CT", [P, 2, 2, HD, P])
        X = s.sb("X", [P, 2, HD, P])
        Y = s.sb("Y", [P, 2, HD, P])
        PX = s.sb("PX", [P, 2, HD, P])
        uwT = s.sb("uwT", [P, 3, P])
        u = s.sb("u", [P, 2, D])
        state = s.sb("state", [P, D])
        ua = s.sb("ua", [P, D])
        oT = s.sb("oT", [P, S2])
        B = [s.ps(f"b{i}") for i in range(8)]
        bP, bY, bX = (B[5], B[6]), (B[1], B[2]), (B[7], B[0])
        (loaded, const, const_ready, xg_ready, xt_done, xT_ready, proj_done, pad_ready, beta_sig, dchain, conv_ready,
         silu_ready, sf_ready, tm_done, tm_ready, sq_ready, rn_ready, ss_ready, qkn_ready, qknt_done, qknT_ready,
         qkx_ready, kk_done, at_done, m_ready, at_ready, mt_done, mt_ready, ct_ready, xt2_done, x_ready, p_done,
         p_ready, yy_done, y_ready, uw_done, uw_ready, ut_done, u_ready, st_done, state_ready, ws_done, ua_ready,
         ot_done, oT_ready, o_done, o_ready, kept, scaled, late_ready, passes) = (s.sem(n) for n in (
             "loaded const const_ready xg_ready xt_done xT_ready proj_done pad_ready beta_sig dchain conv_ready "
             "silu_ready sf_ready tm_done tm_ready sq_ready rn_ready ss_ready qkn_ready qknt_done qknT_ready "
             "qkx_ready kk_done at_done m_ready at_ready mt_done mt_ready ct_ready xt2_done x_ready p_done "
             "p_ready yy_done y_ready uw_done uw_ready ut_done u_ready st_done state_ready ws_done ua_ready "
             "ot_done oT_ready o_done o_ready kept scaled late_ready passes").split())
        block = s.block()

        @block.sync
        def _(sp):
            for dst, src in ((wqkv[:, :, :], a["dlt_wqkv"]), (bw[:, :], a["dlt_bw"]), (taps[:, :, :], a["dlt_taps"]),
                             (ftaps[:, :], a["dlt_short"])):
                sp.dma_start(dst, src).then_inc(loaded, 16)
            sp.wait_ge(loaded, 64)

        @block.gpsimd
        def _(pool):
            n = 0

            def step(ins):
                nonlocal n
                n += 1
                ins.then_inc(const, 1)
                pool.wait_ge(const, n)

            def in_blocks(dst, size, count, src):
                w = dst.shape[-1] // count
                d3 = dst.rearrange("p (a r) -> p a r", a=count)
                s3 = src.rearrange("p (a r) -> p a r", a=count)
                step(pool.affine_select(out=d3, in_=s3, compare_op=ALU.is_ge, fill=0.0, base=0,
                                        pattern=[[-size, count], [0, w]], channel_multiplier=1))
                step(pool.affine_select(out=d3, in_=d3, compare_op=ALU.is_ge, fill=0.0, base=size - 1,
                                        pattern=[[size, count], [0, w]], channel_multiplier=-1))

            step(pool.memset(ones[:, :], 1.0))
            step(pool.memset(mhalf[:, :], -0.5))
            step(pool.memset(pad[:, :, 0:TAPS - 1], 0.0))
            step(pool.memset(vpad[:, 0:SHORT - 1], 0.0))
            step(pool.affine_select(out=strict[:, :], in_=ones[:, :], compare_op=ALU.is_gt, fill=0.0, base=0,
                                    pattern=[[-1, P]], channel_multiplier=1))
            step(pool.affine_select(out=causal[:, :], in_=ones[:, :], compare_op=ALU.is_ge, fill=0.0, base=0,
                                    pattern=[[1, P]], channel_multiplier=-1))
            in_blocks(hmask[:, :], DK, HD, ones[:, 0:HD])
            for l in range(LEVELS + 1):
                in_blocks(blocks[:, l, :], 2 ** l, P >> l, ones[:, :])
            for l in range(LEVELS):
                step(pool.tensor_tensor(couple[:, l, :], blocks[:, l + 1, :], blocks[:, l, :], ALU.subtract))
            pool.memset(ua[:, :], 0.0).then_inc(const_ready, 1)
            def fetch(q):
                pool.tensor_copy(xg[:, :].rearrange("p (t c) -> p t c", t=2),
                                 x[:, bass.ds(q * 2, 2), :]).then_inc(xg_ready, 1)

            def norms(q):
                pool.wait_ge(tm_ready, 2 * q + 1)
                pool.tensor_tensor(sq[:, :, :, :], qk_tm[:, :, :, :], qk_tm[:, :, :, :], ALU.mult).then_inc(sq_ready, 1)
                pool.wait_ge(ss_ready, q + 1)
                pool.tensor_tensor(rn[:, :], ss[:, 1, :], mhalf[:, :], ALU.pow).then_inc(rn_ready, 1)
                pool.wait_ge(tm_ready, 2 * q + 2)
                apart(pool, passes)
                for t in range(2):
                    pool.tensor_copy(v_r[:, bass.ds(q + (1 - t) * nseq, 1), :], vs_tm[:, 0, t:t + 1, :]).then_inc(kept, 1)
                pool.tensor_copy(short_tm[:, bass.ds(q * 2, 2), :], vs_tm[:, 1, :, :]).then_inc(kept, 1)

            def couplings(q):
                for l in range(LEVELS):
                    for t in range(2):
                        if l == 0:
                            pool.wait_ge(mt_ready, 2 * q + t + 1)
                        if l >= 2:
                            pool.wait_ge(y_ready if l == 2 else p_ready,
                                         (2 * LEVELS * q + t + 1) if l == 2 else (2 * (LEVELS - 1) * q + 2 * (l - 3) + t + 1))
                        pool.tensor_tensor(CT[:, t, l % 2, :, :], MT[:, t, :, :],
                                           couple[:, l, :].unsqueeze(1).to_broadcast([P, HD, P]),
                                           ALU.mult).then_inc(ct_ready, 1)

            fetch(0)
            norms(0)
            with pool.Fori(0, nseq - 1) as q:
                pool.wait_ge(xt_done, q + 1)
                apart(pool, passes)
                fetch(q + 1)
                couplings(q)
                norms(q + 1)
            couplings(nseq - 1)

        @block.tensor
        def _(pe):
            pe.wait_ge(const_ready, 1)
            pe.wait_ge(loaded, 64)
            def turn_input(q):
                pe.wait_ge(xg_ready, q + 1)
                for t in range(2):
                    last = pe.transpose(B[3][:, t * P:(t + 1) * P], xg[:, t * P:(t + 1) * P], ident[:, :])
                last.then_inc(xt_done, 1)

            def project(q):
                pe.wait_ge(xT_ready, q + 1)
                for i in range(3):
                    last = pe.matmul(B[4 - i // 2][:, (i % 2) * S2:(i % 2 + 1) * S2], wqkv[:, i, :], xT[:, :],
                                     start=True, stop=True)
                    if i == 1:
                        last.then_inc(proj_done, 1)
                for t in range(2):
                    last = pe.matmul(B[3][:, S2 + t * HD:S2 + (t + 1) * HD], xT[:, t * P:(t + 1) * P], bw[:, :],
                                     start=True, stop=True)
                last.then_inc(proj_done, 1)

            def turn_qk(q):
                pe.wait_ge(silu_ready, 3 * q + 2)
                for i in range(4):
                    last = pe.transpose(B[4][:, i * P:(i + 1) * P], qk[:, i // 2, (i % 2) * P:(i % 2 + 1) * P], ident[:, :])
                last.then_inc(tm_done, 1)

            def turn_v(q):
                pe.wait_ge(silu_ready, 3 * q + 3)
                for t in range(2):
                    pe.transpose(B[3][:, t * P:(t + 1) * P],
                                 vpad[:, SHORT - 1 + t * P:SHORT - 1 + (t + 1) * P], ident[:, :])
                pe.wait_ge(sf_ready, q + 1)
                for t in range(2):
                    last = pe.transpose(B[3][:, (2 + t) * P:(3 + t) * P], sf[:, t * P:(t + 1) * P], ident[:, :])
                last.then_inc(tm_done, 1)

            def turn_normalised(q):
                pe.wait_ge(qkn_ready, q + 1)
                for i in range(4):
                    last = pe.transpose(B[4][:, i * P:(i + 1) * P], qkn[:, i // 2, i % 2, :], ident[:, :])
                last.then_inc(qknt_done, 1)

            def step(q, follows):
                pe.wait_ge(qkx_ready, q * 2 * HD + 2 * HD)
                for t in range(2):
                    pe.matmul(B[5 + t][:, :], qknT[:, 1, t * P:(t + 1) * P], qkx[:, 1, t, :, :],
                              start=True, stop=True).then_inc(kk_done, 1)
                for t in range(2):
                    pe.matmul(B[1 + t][:, :], qknT[:, 1, t * P:(t + 1) * P], qkx[:, 0, t, :, :],
                              start=True, stop=True).then_inc(at_done, 1)
                for t in range(2):
                    pe.wait_ge(m_ready, 2 * q + t + 1)
                    for h in range(HD):
                        last = pe.transpose(B[3 + t][:, h * P:(h + 1) * P], M[:, t, h, :], ident[:, :])
                    last.then_inc(mt_done, 1)
                for l in range(LEVELS):
                    if l:
                        for t in range(2):
                            pe.wait_ge(x_ready, 2 * (LEVELS - 1) * q + 2 * (l - 1) + t + 1)
                            pe.wait_ge(ct_ready, 2 * LEVELS * q + 2 * l + t + 1)
                            for h in range(HD):
                                last = pe.matmul(bP[t][:, h * P:(h + 1) * P], CT[:, t, l % 2, h, :], X[:, t, h, :],
                                                 start=True, stop=True)
                            last.then_inc(p_done, 1)
                        for t in range(2):
                            pe.wait_ge(p_ready, 2 * (LEVELS - 1) * q + 2 * (l - 1) + t + 1)
                            if l == 1:
                                pe.wait_ge(at_ready, 2 * q + t + 1)
                            for h in range(HD):
                                last = pe.matmul(bY[t][:, h * P:(h + 1) * P], PX[:, t, h, :], Y[:, t, h, :],
                                                 start=True, stop=True)
                            last.then_inc(yy_done, 1)
                    if l < LEVELS - 1:
                        for t in range(2):
                            pe.wait_ge(y_ready, 2 * LEVELS * q + 2 * l + t + 1)
                            for h in range(HD):
                                last = pe.transpose(bX[t][:, h * P:(h + 1) * P], Y[:, t, h, :], ident[:, :])
                            last.then_inc(xt2_done, 1)
                    if follows and l == 0:
                        turn_input(q + 1)
                    if follows and l == 1:
                        project(q + 1)
                    if follows and l == 4:
                        turn_qk(q + 1)
                    if follows and l == 5:
                        turn_v(q + 1)
                for i, (src, t) in enumerate(((vb, 0), (vb, 1), (kb, 1))):
                    pe.wait_ge(y_ready, 2 * LEVELS * q + 2 * (LEVELS - 1) + t + 1)
                    for h in range(HD):
                        last = pe.matmul(B[5][DK * h:DK * (h + 1), i * P:(i + 1) * P], src[:, t, DK * h:DK * (h + 1)],
                                         Y[:, t, h, :], start=True, stop=True)
                last.then_inc(uw_done, 1)
                pe.wait_ge(uw_ready, q + 1)
                for t in range(2):
                    last = pe.transpose(B[6][:, t * P:(t + 1) * P], uwT[:, t, :], ident[:, :])
                last.then_inc(ut_done, 1)
                if follows:
                    turn_normalised(q + 1)
                pe.wait_ge(u_ready, q + 1)
                pe.wait_ge(late_ready, 2 * q + 2)
                pe.matmul(B[1][:, 0:D], k0[:, :], u[:, 0, :], start=True, stop=True).then_inc(st_done, 1)
                for h in range(HD):
                    pe.matmul(B[7][DK * h:DK * (h + 1), 0:P], u[:, 0, DK * h:DK * (h + 1)], AT[:, 0, h, :],
                              start=True, stop=True)
                pe.wait_ge(state_ready, q + 1)
                pe.matmul(B[2][:, 0:D], uwT[:, 2, :], state[:, :], start=True, stop=True).then_inc(ws_done, 1)
                pe.matmul(B[7][:, P:S2], state[:, :], qT1[:, :], start=True, stop=False, skip_group_check=True)
                pe.wait_ge(ua_ready, q + 1)
                for h in range(HD):
                    last = pe.matmul(B[7][DK * h:DK * (h + 1), P:S2], ua[:, DK * h:DK * (h + 1)], AT[:, 1, h, :],
                                     start=False, stop=True, skip_group_check=True)
                last.then_inc(ot_done, 1)
                pe.wait_ge(oT_ready, q + 1)
                for t in range(2):
                    last = pe.transpose(B[0][:, t * P:(t + 1) * P], oT[:, t * P:(t + 1) * P], ident[:, :])
                last.then_inc(o_done, 1)
                pe.wait_ge(o_ready, q + 1)

            turn_input(0)
            project(0)
            turn_qk(0)
            turn_v(0)
            turn_normalised(0)
            with pe.Fori(0, nseq - 1) as q:
                step(q, True)
            step(nseq - 1, False)

        @block.scalar
        def _(act):
            act.wait_ge(const_ready, 1)
            def turned(q):
                act.wait_ge(xt_done, q + 1)
                act.activation(xT[:, :], B[3][:, 0:S2], ACT.Copy).then_inc(xT_ready, 1)

            def projected(q):
                act.wait_ge(proj_done, 2 * q + 1)
                act.activation(pad[:, 0:2, TAPS - 1:], B[4][:, :].rearrange("p (i n) -> p i n", i=2),
                               ACT.Copy).then_inc(pad_ready, 1)
                act.wait_ge(proj_done, 2 * q + 2)
                act.activation(pad[:, 2, TAPS - 1:], B[3][:, 0:S2], ACT.Copy).then_inc(pad_ready, 1)
                act.activation(beta[:, 0, :, :].rearrange("p t h -> p (t h)"), B[3][:, S2:S2 + 2 * HD],
                               ACT.Sigmoid).then_inc(beta_sig, 1)

            def silus(q):
                for i in range(3):
                    act.wait_ge(conv_ready, 3 * TAPS * q + 3 * (TAPS - 1) + i + 1)
                    act.activation(qk[:, i, :] if i < 2 else vpad[:, SHORT - 1:], conv[:, i, :],
                                   ACT.Silu).then_inc(silu_ready, 1)

            def turned_qk(q):
                act.wait_ge(tm_done, 2 * q + 1)
                act.activation(qk_tm[:, :, :, :].rearrange("p i t c -> p (i t c)"), B[4][:, :], ACT.Copy).then_inc(tm_ready, 1)

            def turned_v(q, kept_before):
                act.wait_ge(tm_done, 2 * q + 2)
                if kept_before:
                    act.wait_ge(kept, 3 * q)
                    act.wait_ge(scaled, 2 * q)
                act.activation(vs_tm[:, :, :, :].rearrange("p i t c -> p (i t c)"), B[3][:, :], ACT.Copy).then_inc(tm_ready, 1)

            def turned_normalised(q):
                act.wait_ge(qknt_done, q + 1)
                act.activation(qknT[:, :, :].rearrange("p i n -> p (i n)"), B[4][:, :], ACT.Copy).then_inc(qknT_ready, 1)

            def step(q, follows):
                act.activation(k0[:, :], qkn[:, 1, 0, :], ACT.Copy).then_inc(late_ready, 1)
                act.wait_ge(qknT_ready, q + 1)
                act.activation(qT1[:, :], qknT[:, 0, P:S2], ACT.Copy).then_inc(late_ready, 1)
                for t in range(2):
                    act.wait_ge(mt_done, 2 * q + t + 1)
                    act.activation(MT[:, t, :, :].rearrange("p h n -> p (h n)"), B[3 + t][:, :], ACT.Copy).then_inc(mt_ready, 1)
                for l in range(LEVELS):
                    if l:
                        for t in range(2):
                            act.wait_ge(p_done, 2 * (LEVELS - 1) * q + 2 * (l - 1) + t + 1)
                            act.activation(PX[:, t, :, :].rearrange("p h n -> p (h n)"), bP[t][:, :],
                                           ACT.Copy).then_inc(p_ready, 1)
                    if l < LEVELS - 1:
                        for t in range(2):
                            act.wait_ge(xt2_done, 2 * (LEVELS - 1) * q + 2 * l + t + 1)
                            act.activation(X[:, t, :, :].rearrange("p h n -> p (h n)"), bX[t][:, :],
                                           ACT.Copy).then_inc(x_ready, 1)
                    if follows and l == 0:
                        turned(q + 1)
                    if follows and l == 1:
                        projected(q + 1)
                    if follows and l == 3:
                        silus(q + 1)
                    if follows and l == 5:
                        turned_qk(q + 1)
                    if follows and l == 6:
                        turned_v(q + 1, True)
                act.wait_ge(uw_done, q + 1)
                act.activation(uwT[:, :, :].rearrange("p i n -> p (i n)"), B[5][:, 0:3 * P], ACT.Copy).then_inc(uw_ready, 1)
                act.wait_ge(ut_done, q + 1)
                act.activation(u[:, :, :].rearrange("p t n -> p (t n)"), B[6][:, 0:S2], ACT.Copy).then_inc(u_ready, 1)
                if follows:
                    turned_normalised(q + 1)
                act.wait_ge(ot_done, q + 1)
                act.activation(oT[:, :], B[7][:, 0:S2], ACT.Copy).then_inc(oT_ready, 1)
                act.wait_ge(o_done, q + 1)
                act.activation(delta_tm[:, bass.ds(q * 2, 2), :], B[0][:, 0:S2].rearrange("p (t c) -> p t c", t=2),
                               ACT.Copy).then_inc(o_ready, 1)

            turned(0)
            projected(0)
            silus(0)
            turned_qk(0)
            turned_v(0, False)
            turned_normalised(0)
            with act.Fori(0, nseq - 1) as q:
                step(q, True)
            step(nseq - 1, False)

        @block.vector
        def _(dve):
            dve.wait_ge(const_ready, 1)
            dve.wait_ge(loaded, 64)
            def convolve(q, steps):
                for j in steps:
                    for i in range(3):
                        if j == 0:
                            dve.wait_ge(pad_ready, 2 * q + 1 + i // 2)
                            dve.tensor_scalar(conv[:, i, :], pad[:, i, 0:S2], taps[:, i, 0:1], None,
                                              ALU.mult).then_inc(conv_ready, 1)
                        else:
                            dve.wait_ge(conv_ready, 3 * TAPS * q + 3 * (j - 1) + i + 1)
                            dve.scalar_tensor_tensor(out=conv[:, i, :], in0=pad[:, i, j:j + S2],
                                                     scalar=taps[:, i, j:j + 1], in1=conv[:, i, :],
                                                     op0=ALU.mult, op1=ALU.add).then_inc(conv_ready, 1)

            def short_filter(q):
                dve.wait_ge(beta_sig, q + 1)
                dve.tensor_scalar(beta[:, 1, :, :], beta[:, 0, :, :], 1e-6, None, ALU.max).then_inc(dchain, 1)
                dve.wait_ge(silu_ready, 3 * q + 3)
                for j in range(SHORT):
                    if j == 0:
                        ins = dve.tensor_scalar(sf[:, :], vpad[:, 0:S2], ftaps[:, 0:1], None, ALU.mult)
                    else:
                        dve.wait_ge(dchain, NC * q + 1 + j)
                        ins = dve.scalar_tensor_tensor(out=sf[:, :], in0=vpad[:, j:j + S2], scalar=ftaps[:, j:j + 1],
                                                       in1=sf[:, :], op0=ALU.mult, op1=ALU.add)
                    ins.then_inc(dchain if j < SHORT - 1 else sf_ready, 1)

            def sums(q):
                dve.wait_ge(sq_ready, q + 1)
                dve.tensor_reduce(ss[:, 0, :], sq[:, :, :, :].rearrange("p i t (h c) -> p (i t h) c", h=HD),
                                  AX.X, ALU.add).then_inc(dchain, 1)
                dve.wait_ge(dchain, NC * q + SHORT + 1)
                dve.tensor_scalar(ss[:, 1, :], ss[:, 0, :], 1e-6, None, ALU.add).then_inc(ss_ready, 1)

            def normalise(q, late_before):
                if late_before:
                    dve.wait_ge(late_ready, 2 * q)
                dve.wait_ge(rn_ready, q + 1)
                dve.tensor_tensor(qkn[:, :, :, :].rearrange("p i t (h c) -> p (i t h) c", h=HD),
                                  qk_tm[:, :, :, :].rearrange("p i t (h c) -> p (i t h) c", h=HD),
                                  rn[:, :].unsqueeze(2).to_broadcast([P, 4 * HD, DK]), ALU.mult).then_inc(qkn_ready, 1)

            def spread(q):
                dve.wait_ge(qknT_ready, q + 1)
                for i in (1, 0):
                    for h in range(HD):
                        dve.tensor_scalar(qkx[:, i, :, h, :], qknT[:, i, :].rearrange("p (t n) -> p t n", t=2),
                                          hmask[:, h:h + 1], None, ALU.mult).then_inc(qkx_ready, 1)

            def step(q, follows):
                dve.wait_ge(tm_ready, 2 * q + 2)
                bt = beta[:, 1, :, :].unsqueeze(3).to_broadcast([P, 2, HD, DK])
                dve.tensor_tensor(vb[:, :, :].rearrange("p t (h c) -> p t h c", h=HD),
                                  vs_tm[:, 0, :, :].rearrange("p t (h c) -> p t h c", h=HD), bt,
                                  ALU.mult).then_inc(scaled, 1)
                dve.wait_ge(qkn_ready, q + 1)
                dve.tensor_tensor(kb[:, :, :].rearrange("p t (h c) -> p t h c", h=HD),
                                  qkn[:, 1, :, :].rearrange("p t (h c) -> p t h c", h=HD), bt,
                                  ALU.mult).then_inc(scaled, 1)
                for t in range(2):
                    dve.wait_ge(kk_done, 2 * q + t + 1)
                    for h in range(HD):
                        last = dve.scalar_tensor_tensor(out=M[:, t, h, :], in0=B[5 + t][:, h * P:(h + 1) * P],
                                                        scalar=beta[:, 1, t, h:h + 1], in1=strict[:, :],
                                                        op0=ALU.mult, op1=ALU.mult)
                    last.then_inc(m_ready, 1)
                for t in range(2):
                    dve.wait_ge(at_done, 2 * q + t + 1)
                    dve.tensor_tensor(AT[:, t, :, :], B[1 + t][:, :].rearrange("p (h n) -> p h n", h=HD),
                                      causal[:, :].unsqueeze(1).to_broadcast([P, HD, P]), ALU.mult).then_inc(at_ready, 1)
                for t in range(2):
                    dve.wait_ge(ct_ready, 2 * LEVELS * q + t + 1)
                    dve.scalar_tensor_tensor(out=Y[:, t, :, :], in0=CT[:, t, 0, :, :], scalar=-1.0,
                                             in1=ident[:, :].unsqueeze(1).to_broadcast([P, HD, P]),
                                             op0=ALU.mult, op1=ALU.add).then_inc(y_ready, 1)
                for l in range(1, LEVELS):
                    for t in range(2):
                        dve.wait_ge(yy_done, 2 * (LEVELS - 1) * q + 2 * (l - 1) + t + 1)
                        dve.tensor_tensor(Y[:, t, :, :], Y[:, t, :, :],
                                          bY[t][:, :].rearrange("p (h n) -> p h n", h=HD),
                                          ALU.subtract).then_inc(y_ready, 1)
                    if follows and l == 1:
                        convolve(q + 1, (0, 1))
                    if follows and l == 2:
                        convolve(q + 1, (2, 3))
                    if follows and l == 4:
                        short_filter(q + 1)
                if follows:
                    sums(q + 1)
                    normalise(q + 1, True)
                dve.wait_ge(st_done, q + 1)
                dve.tensor_tensor(state[:, :], B[1][:, 0:D], blocks[:, 5, :], ALU.mult).then_inc(state_ready, 1)
                dve.wait_ge(ws_done, q + 1)
                dve.tensor_tensor(ua[:, :], u[:, 1, :], B[2][:, 0:D], ALU.subtract).then_inc(ua_ready, 1)
                if follows:
                    spread(q + 1)

            convolve(0, range(TAPS))
            short_filter(0)
            sums(0)
            normalise(0, False)
            spread(0)
            with dve.Fori(0, nseq - 1) as q:
                step(q, True)
            step(nseq - 1, False)


def long_filter(nc, a, ident, nseq, v_r, long_r):
    CH = 8
    NS2 = 2 * nseq
    W = P + LONG
    FW = 2 * P + LONG
    taps = a["dlt_long"]
    with ExitStack() as ctx:
        s = Space(nc, ctx, "fir")
        tz = s.sb("tz", [P, 2, CH, W])
        vcol = s.sb("vcol", [P, 2, CH, NS2])
        vrev = s.sb("vrev", [P, 2, CH, NS2])
        flip = s.sb("flip", [P, P])
        o4 = s.sb("o4", [P, 2, 2 * P])
        bF = [s.ps("bF0"), s.ps("bF1")]
        bT = [s.ps("bT0"), s.ps("bT1")]
        bV = [s.ps("bV0"), s.ps("bV1")]
        tz_loaded = [s.sem("tz_loaded0"), s.sem("tz_loaded1")]
        flip_ready, vcol_ready, flipped, vrev_ready, fir_done, o4_ready, turn_done, kept = (s.sem(n) for n in (
            "flip_ready", "vcol_ready", "flipped", "vrev_ready", "fir_done", "o4_ready", "turn_done", "kept"))
        block = s.block()
        turns = D // CH

        @block.sync
        def _(sp):
            with sp.Fori(0, turns // 2) as i:
                for half in range(2):
                    sp.wait_ge(fir_done, 2 * i)
                    src = taps[bass.ds((2 * i + half) * CH, CH), 0:W]
                    src = bass.AP(tensor=taps.tensor, offset=src.offset + 1, ap=[[1, P], [FW, CH], [1, W]])
                    sp.dma_start(tz[:, half, :, :], src).then_inc(tz_loaded[half], 16)
            for half in range(2):
                sp.wait_ge(tz_loaded[half], 16 * (turns // 2))

        @block.gpsimd
        def _(pool):
            pool.memset(flip[:, :], 0.0).then_inc(flip_ready, 1)
            pool.wait_ge(flip_ready, 1)
            pool.affine_select(out=flip[:, :], in_=flip[:, :], compare_op=ALU.not_equal, fill=1.0, base=1 - P,
                               pattern=[[1, P]], channel_multiplier=1).then_inc(flip_ready, 1)
            with pool.Fori(0, turns // 2) as i:
                for half in range(2):
                    pool.wait_ge(flipped, 2 * i)
                    pool.tensor_copy(vcol[:, half, :, :].rearrange("p c s -> p s c"),
                                     v_r[:, :, bass.ds((2 * i + half) * CH, CH)]).then_inc(vcol_ready, 1)

        @block.tensor
        def _(pe):
            def turn_over(i, half):
                pe.wait_ge(o4_ready, 2 * i + half + 1)
                for j in range(2):
                    last = pe.transpose(bT[half][:, j * P:(j + 1) * P], o4[:, half, j * P:(j + 1) * P], ident[:, :])
                last.then_inc(turn_done, 1)

            pe.wait_ge(flip_ready, 2)
            with pe.Fori(0, turns // 2) as i:
                for half in range(2):
                    pe.wait_ge(vcol_ready, 2 * i + half + 1)
                    pe.wait_ge(vrev_ready, 2 * i)
                    pe.matmul(bV[half][:, 0:CH * NS2], flip[:, :], vcol[:, half, :, :],
                              start=True, stop=True).then_inc(flipped, 1)
                for half in range(2):
                    pe.wait_ge(tz_loaded[half], 16 * i + 16)
                    pe.wait_ge(vrev_ready, 2 * i + half + 1)
                    pe.wait_ge(o4_ready, 2 * i)
                    for c in range(CH):
                        o = bF[half][32 * (c % 4):32 * (c % 4) + NS2, (c // 4) * P:(c // 4 + 1) * P]
                        pe.matmul(o, vrev[:, half, c, :], tz[:, half, c, 0:P], start=(c < 4), stop=False,
                                  skip_group_check=True)
                        last = pe.matmul(bF[half][32 * (c % 4):32 * (c % 4) + nseq, (c // 4) * P:(c // 4) * P + LONG],
                                         vrev[:, half, c, nseq:NS2], tz[:, half, c, P:W], start=False, stop=True,
                                         skip_group_check=True)
                    last.then_inc(fir_done, 1)
                    if half == 1:
                        turn_over(i, 0)
                turn_over(i, 1)

        @block.scalar
        def _(act):
            with act.Fori(0, turns // 2) as i:
                for half in range(2):
                    act.wait_ge(flipped, 2 * i + half + 1)
                    act.wait_ge(fir_done, 2 * i)
                    act.activation(vrev[:, half, :, :].rearrange("p c s -> p (c s)"), bV[half][:, 0:CH * NS2],
                                   ACT.Copy).then_inc(vrev_ready, 1)
                for half in range(2):
                    act.wait_ge(fir_done, 2 * i + half + 1)
                    act.wait_ge(turn_done, 2 * i)
                    act.activation(o4[:, half, :], bF[half][:, 0:2 * P], ACT.Copy).then_inc(o4_ready, 1)
                for half in range(2):
                    act.wait_ge(turn_done, 2 * i + half + 1)
                    act.activation(long_r[:, :, bass.ds((2 * i + half) * CH, CH)],
                                   bT[half][:, 0:2 * P].rearrange("p (c s) -> p s c", c=CH)[:, 0:NS2, :],
                                   ACT.Copy).then_inc(kept, 1)


def gate_and_project(nc, a, x, ident, ngroups, v_r, short_tm, long_r, delta_tm):
    NSTR = 4
    NC = 24
    HT = TILES * HD
    nseq = 2 * ngroups
    with ExitStack() as ctx:
        s = Space(nc, ctx, "gate")
        w1a = s.sb("w1a", [P, P])
        w1b = s.sb("w1b", [P, HD, P])
        w2 = s.sb("w2", [P, 32])
        ow = s.sb("ow", [P, 2, D])
        col = s.sb("col", [P, 3])
        tmp = s.sb("tmp", [P, 8])
        cr = s.sb("cr", [P, 2, HD])
        mhalf = s.sb("mhalf", [P, 64])
        half = s.sb("half", [P, 64])
        xg = s.sb("xg", [P, G])
        xT = s.sb("xT", [P, G])
        S = s.sb("S", [P, NSTR, TILES, D])
        cen = s.sb("cen", [P, NSTR, TILES, D])
        red = s.sb("red", [P, 6, 64])
        stz = s.sb("stz", [P, TILES, P])
        stT = s.sb("stT", [P, G])
        hg = s.sb("hg", [P, 2, G])
        lT = s.sb("lT", [P, G])
        lt = s.sb("lt", [P, HT, 4])
        pr = s.sb("pr", [P, 4, HT, 4])
        red2 = s.sb("red2", [P, 6, HT])
        mix = s.sb("mix", [P, 4, G])
        o = s.sb("o", [P, G])
        osq = s.sb("osq", [P, G])
        oT = s.sb("oT", [P, G])
        b_x, b_s, b_h0, b_h1, b_l, b_lt, b_o, b_y = (s.ps(n) for n in (
            "b_x", "b_s", "b_h0", "b_h1", "b_l", "b_lt", "b_o", "b_y"))
        b_h = (b_h0, b_h1)
        (loaded, setup_p, setup_v, setup_a, zeroed, xg_ready, s_ready, xt_done, xT_ready, chain, cen_ready, sq_ready,
         l2_in, l2_ready, st_ready, stt_done, stT_ready, h_done, hg_ready, l_done, lT_ready, lt_done, e_in, e_ready,
         prod_in, prod_ready, osq_ready, rms_in, rms_ready, o_ready, ot_done, oT_ready, y_done, x_ready, mixed) = (
            s.sem(n) for n in (
                "loaded setup_p setup_v setup_a zeroed xg_ready s_ready xt_done xT_ready chain cen_ready sq_ready "
                "l2_in l2_ready st_ready stt_done stT_ready h_done hg_ready l_done lT_ready lt_done e_in e_ready "
                "prod_in prod_ready osq_ready rms_in rms_ready o_ready ot_done oT_ready y_done x_ready mixed").split())
        block = s.block()
        NLOAD = 4 + 2 + 2 * HD + 2

        @block.sync
        def _(sp):
            sp.wait_ge(zeroed, 3)
            sp.dma_start(w1a[:, :], a["gate_w1a"]).then_inc(loaded, 16)
            sp.dma_start(w2[:, 0:4], a["gate_w2"]).then_inc(loaded, 16)
            sp.dma_start(ow[:, 0, :], a["gate_ow"]).then_inc(loaded, 16)
            sp.dma_start(col[:, 0:2], a["gate_cols"]).then_inc(loaded, 16)
            sp.dma_start(cr[:, 0, :], a["gate_res"].unsqueeze(0).to_broadcast([P, HD])).then_inc(loaded, 16)
            sp.dma_start(tmp[:, 0:1], a["gate_temp"].unsqueeze(0).to_broadcast([P, 1])).then_inc(loaded, 16)
            for h in range(HD):
                sp.dma_start(w1b[16 * h:16 * h + 16, h, :], a["gate_w1b"]).then_inc(loaded, 16)
                sp.dma_start(col[DK * h:DK * h + 4, 2:3], a["gate_b2"].rearrange("(p o) -> p o", o=1)).then_inc(loaded, 16)
            sp.wait_ge(loaded, 16 * (NLOAD - 2))

        @block.gpsimd
        def _(pool):
            pool.memset(w1b[:, :, :], 0.0).then_inc(zeroed, 1)
            pool.memset(w2[:, :], 0.0).then_inc(zeroed, 1)
            pool.memset(col[:, :], 0.0).then_inc(zeroed, 1)
            pool.memset(stz[:, :, :], 0.0).then_inc(setup_p, 1)
            pool.memset(mhalf[:, :], -0.5).then_inc(setup_p, 1)
            pool.memset(half[:, :], 0.5).then_inc(setup_p, 1)
            pool.wait_ge(setup_p, 3)
            with pool.Fori(0, ngroups) as g:
                pool.wait_ge(mixed, g)
                pool.wait_ge(xt_done, g)
                tiles = bass.ds(g * TILES, TILES)
                pool.tensor_copy(xg[:, :].rearrange("p (t c) -> p t c", t=TILES), x[:, tiles, :]).then_inc(xg_ready, 1)
                pool.tensor_copy(S[:, 0, :, :], short_tm[:, tiles, :]).then_inc(s_ready, 1)
                pool.wait_ge(l2_in, g + 1)
                pool.tensor_tensor(red[:, 5, :], red[:, 4, :], half[:, :], ALU.pow).then_inc(l2_ready, 1)
                pool.wait_ge(prod_in, g + 1)
                for i in (2, 3):
                    pool.tensor_tensor(mix[:, i, :].rearrange("p (t c) -> p t c", c=DK),
                                       S[:, i, :, :].rearrange("p t (h c) -> p (t h) c", c=DK),
                                       pr[:, 3, :, i:i + 1].to_broadcast([P, HT, DK]), ALU.mult).then_inc(prod_ready, 1)
                pool.wait_ge(rms_in, g + 1)
                pool.tensor_tensor(red2[:, 5, :], red2[:, 4, :], mhalf[:, 0:HT], ALU.pow).then_inc(rms_ready, 1)

        @block.tensor
        def _(pe):
            pe.wait_ge(loaded, 16 * (NLOAD - 2))
            pe.wait_ge(setup_v, 6)
            with pe.Fori(0, ngroups) as g:
                pe.wait_ge(xg_ready, g + 1)
                for t in range(TILES):
                    last = pe.transpose(b_x[:, t * P:(t + 1) * P], xg[:, t * P:(t + 1) * P], ident[:, :])
                last.then_inc(xt_done, 1)
                pe.wait_ge(st_ready, 4 * g + 4)
                for t in range(TILES):
                    last = pe.transpose(b_s[:, t * P:(t + 1) * P], stz[:, t, :], ident[:, :])
                last.then_inc(stt_done, 1)
                pe.wait_ge(xT_ready, g + 1)
                for h in range(HD + 1):
                    if h < HD:
                        if h >= 2:
                            pe.wait_ge(hg_ready, HD * g + h - 1)
                        pe.matmul(b_h[h % 2][:, :], w1a[:, :], xT[:, :], start=True, stop=False)
                        if h == 0:
                            pe.wait_ge(stT_ready, g + 1)
                        pe.matmul(b_h[h % 2][:, :], w1b[:, h, :], stT[:, :], start=False, stop=True).then_inc(h_done, 1)
                    if h >= 1:
                        pe.wait_ge(hg_ready, HD * g + h)
                        last = pe.matmul(b_l[32 * (h - 1):32 * h, :], w2[:, :], hg[:, (h - 1) % 2, :],
                                         start=True, stop=True).then_inc(l_done, 1)
                pe.wait_ge(lT_ready, g + 1)
                for t in range(TILES):
                    last = pe.transpose(b_lt[:, t * P:(t + 1) * P], lT[:, t * P:(t + 1) * P], ident[:, :])
                last.then_inc(lt_done, 1)
                pe.wait_ge(o_ready, g + 1)
                for t in range(TILES):
                    last = pe.transpose(b_o[:, t * P:(t + 1) * P], o[:, t * P:(t + 1) * P], ident[:, :])
                last.then_inc(ot_done, 1)
                pe.wait_ge(oT_ready, g + 1)
                for t in range(TILES):
                    last = pe.matmul(b_y[:, t * D:(t + 1) * D], oT[:, t * P:(t + 1) * P], ow[:, 1, :],
                                     start=True, stop=True)
                last.then_inc(y_done, 1)
                pe.wait_ge(x_ready, g + 1)

        @block.scalar
        def _(act):
            act.wait_ge(loaded, 16 * (NLOAD - 2))
            act.wait_ge(setup_v, 2)
            act.activation(tmp[:, 3:4], tmp[:, 2:3], ACT.Exp, scale=-1.0).then_inc(setup_a, 1)
            act.wait_ge(setup_a, 1)
            act.activation(tmp[:, 4:5], tmp[:, 3:4], ACT.Ln, bias=1.0).then_inc(setup_a, 1)
            act.activation(cr[:, 1, :], cr[:, 0, :], ACT.Sigmoid).then_inc(setup_a, 1)
            with act.Fori(0, ngroups) as g:
                tiles = bass.ds(g * TILES, TILES)
                act.wait_ge(mixed, g)
                act.activation(S[:, 2, :, :], delta_tm[:, tiles, :], ACT.Copy).then_inc(s_ready, 1)
                for src, i in ((v_r, 3), (long_r, 1)):
                    for b in range(2):
                        act.activation(S[:, i, 1 - b::2, :], src[:, bass.ds(b * nseq + 2 * g, 2), :],
                                       ACT.Copy).then_inc(s_ready, 1)
                act.wait_ge(xt_done, g + 1)
                act.activation(xT[:, :], b_x[:, :], ACT.Copy).then_inc(xT_ready, 1)
                act.wait_ge(cen_ready, g + 1)
                act.activation(cen[:, :, :, :], cen[:, :, :, :], ACT.Square).then_inc(sq_ready, 1)
                act.wait_ge(stt_done, g + 1)
                act.activation(stT[:, :], b_s[:, :], ACT.Copy).then_inc(stT_ready, 1)
                for h in range(HD):
                    act.wait_ge(h_done, HD * g + h + 1)
                    if h >= 2:
                        act.wait_ge(l_done, HD * g + h - 1)
                    act.activation(hg[:, h % 2, :], b_h[h % 2][:, :], ACT.Gelu_apprx_tanh,
                                   bias=col[:, 0:1]).then_inc(hg_ready, 1)
                act.wait_ge(l_done, HD * (g + 1))
                act.activation(lT[:, :], b_l[:, :], ACT.Identity, bias=col[:, 2:3]).then_inc(lT_ready, 1)
                act.wait_ge(e_in, g + 1)
                act.activation(pr[:, 1, :, :], pr[:, 0, :, :], ACT.Exp, scale=tmp[:, 6:7]).then_inc(e_ready, 1)
                act.wait_ge(ot_done, g + 1)
                act.activation(oT[:, :], b_o[:, :], ACT.Copy).then_inc(oT_ready, 1)
                act.wait_ge(y_done, g + 1)
                act.activation(x[:, tiles, :], b_y[:, :].rearrange("p (t c) -> p t c", t=TILES),
                               ACT.Copy).then_inc(x_ready, 1)

        @block.vector
        def _(dve):
            dve.wait_ge(loaded, 16 * (NLOAD - 2))
            dve.wait_ge(setup_p, 3)
            dve.tensor_scalar(tmp[:, 1:2], tmp[:, 0:1], -1.0, None, ALU.mult).then_inc(setup_v, 1)
            dve.wait_ge(setup_v, 1)
            dve.tensor_tensor(tmp[:, 2:3], tmp[:, 0:1], tmp[:, 1:2], ALU.max).then_inc(setup_v, 1)
            dve.wait_ge(setup_a, 3)
            dve.tensor_scalar(tmp[:, 7:8], tmp[:, 0:1], 0.0, None, ALU.max).then_inc(setup_v, 1)
            dve.wait_ge(setup_v, 3)
            dve.tensor_tensor(tmp[:, 5:6], tmp[:, 7:8], tmp[:, 4:5], ALU.add).then_inc(setup_v, 1)
            dve.wait_ge(setup_v, 4)
            dve.reciprocal(tmp[:, 6:7], tmp[:, 5:6]).then_inc(setup_v, 1)
            dve.tensor_scalar(ow[:, 1, :], ow[:, 0, :], col[:, 1:2], None, ALU.mult).then_inc(setup_v, 1)
            dve.wait_ge(setup_v, 6)
            with dve.Fori(0, ngroups) as g:
                n = NC * g

                def link(ins):
                    nonlocal n
                    n = n + 1
                    ins.then_inc(chain, 1)
                    dve.wait_ge(chain, n)

                rows = S[:, :, :, :].rearrange("p s t (h c) -> p (s t h) c", c=DK)
                crow = cen[:, :, :, :].rearrange("p s t (h c) -> p (s t h) c", c=DK)
                stat = stz[:, :, 0:HD * 16].rearrange("p t (h s k) -> p k s t h", h=HD, s=NSTR)

                def put(k, src):
                    v = src.rearrange("p (s t h) -> p s t h", s=NSTR, t=TILES)
                    for i in range(NSTR):
                        last = dve.tensor_copy(stat[:, k, i, :, :], v[:, i, :, :])
                    last.then_inc(st_ready, 1)

                dve.wait_ge(s_ready, 6 * g + 6)
                dve.wait_ge(stt_done, g)
                link(dve.tensor_reduce(red[:, 0, :], rows, AX.X, ALU.add))
                link(dve.tensor_scalar(red[:, 1, :], red[:, 0, :], 1.0 / DK, None, ALU.mult))
                dve.tensor_tensor(crow, rows, red[:, 1, :].unsqueeze(2).to_broadcast([P, 64, DK]),
                                  ALU.subtract).then_inc(cen_ready, 1)
                link(dve.tensor_reduce(red[:, 0, :], rows, AX.X, ALU.add, apply_absolute_value=True))
                link(dve.tensor_scalar(red[:, 0, :], red[:, 0, :], 1.0 / DK, None, ALU.mult))
                put(0, red[:, 1, :])
                put(2, red[:, 0, :])
                dve.wait_ge(sq_ready, g + 1)
                link(dve.tensor_reduce(red[:, 2, :], crow, AX.X, ALU.add))
                link(dve.tensor_scalar(red[:, 3, :], red[:, 2, :], 1.0 / DK, None, ALU.mult))
                link(dve.tensor_tensor(red[:, 4, :], red[:, 1, :], red[:, 1, :], ALU.mult))
                link(dve.tensor_tensor(red[:, 4, :], red[:, 4, :], red[:, 3, :], ALU.add))
                dve.tensor_scalar(red[:, 4, :], red[:, 4, :], float(DK), None, ALU.mult).then_inc(l2_in, 1)
                put(1, red[:, 3, :])
                dve.wait_ge(l2_ready, g + 1)
                put(3, red[:, 5, :])
                dve.wait_ge(lt_done, g + 1)
                lo = b_lt[:, :].rearrange("p (a e) -> p a e", e=32)[:, :, 0:4]
                link(dve.tensor_copy(lt[:, :, :], lo))
                link(dve.tensor_reduce(red2[:, 0, :], lt[:, :, :], AX.X, ALU.max))
                dve.tensor_tensor(pr[:, 0, :, :], lt[:, :, :], red2[:, 0, :].unsqueeze(2).to_broadcast([P, HT, 4]),
                                  ALU.subtract).then_inc(e_in, 1)
                dve.wait_ge(e_ready, g + 1)
                for i in (1, 2):
                    link(dve.tensor_reduce(red2[:, i, :], pr[:, i, :, :], AX.X, ALU.add))
                    link(dve.reciprocal(red2[:, 3, :], red2[:, i, :]))
                    link(dve.tensor_tensor(pr[:, i + 1, :, :], pr[:, i, :, :],
                                           red2[:, 3, :].unsqueeze(2).to_broadcast([P, HT, 4]), ALU.mult))
                    if i == 1:
                        link(dve.tensor_scalar(pr[:, 2, :, :], pr[:, 2, :, :], 0.02, None, ALU.max))
                dve.tensor_tensor(pr[:, 3, :, 0].rearrange("p (t h) -> p t h", h=HD),
                                  pr[:, 3, :, 0].rearrange("p (t h) -> p t h", h=HD),
                                  cr[:, 1, :].unsqueeze(1).to_broadcast([P, TILES, HD]), ALU.add).then_inc(prod_in, 1)
                dve.wait_ge(prod_in, g + 1)
                for i in (0, 1):
                    ins = dve.tensor_tensor(mix[:, i, :].rearrange("p (t c) -> p t c", c=DK),
                                            S[:, i, :, :].rearrange("p t (h c) -> p (t h) c", c=DK),
                                            pr[:, 3, :, i:i + 1].to_broadcast([P, HT, DK]), ALU.mult)
                    link(ins)
                link(dve.tensor_tensor(o[:, :], mix[:, 0, :], mix[:, 1, :], ALU.add))
                for i in (2, 3):
                    dve.wait_ge(prod_ready, 2 * g + i - 1)
                    link(dve.tensor_tensor(o[:, :], o[:, :], mix[:, i, :], ALU.add))
                dve.tensor_copy(red2[:, 0, 0:1], red2[:, 1, 0:1]).then_inc(mixed, 1)
                link(dve.tensor_tensor(osq[:, :], o[:, :], o[:, :], ALU.mult))
                link(dve.tensor_reduce(red2[:, 3, :], osq[:, :].rearrange("p (a c) -> p a c", c=DK), AX.X, ALU.add))
                dve.tensor_scalar(red2[:, 4, :], red2[:, 3, :], 1.0 / DK, 1e-5, ALU.mult, ALU.add).then_inc(rms_in, 1)
                dve.wait_ge(rms_ready, g + 1)
                dve.tensor_tensor(o[:, :].rearrange("p (a c) -> p a c", c=DK), o[:, :].rearrange("p (a c) -> p a c", c=DK),
                                  red2[:, 5, :].unsqueeze(2).to_broadcast([P, HT, DK]), ALU.mult).then_inc(o_ready, 1)


def lay_out(i):
    import numpy as np

    def A(n):
        return np.asarray(i["L0_attn_" + n])

    nl = A("Wq").shape[0]
    out = {}
    mats = [A(n).transpose(1, 0, 2) for n in ("Wq", "Wk", "Wv", "Wo", "W1")]
    mats.append(A("W2").reshape(nl, FB, P, D).transpose(2, 0, 1, 3).reshape(P, nl, FB * D))
    out["enc_mats"] = np.ascontiguousarray(np.concatenate(mats, axis=2))
    out["enc_rows"] = np.ascontiguousarray(np.concatenate(
        [A(n) for n in ("bv", "bo", "g1", "be1", "bf2", "g2", "be2")], axis=1))
    cols = [A(n).T[:, :, None] for n in ("bq", "bk", "g1", "be1")]
    cols.append(A("bf1").reshape(nl, FB, P).transpose(2, 0, 1))
    out["enc_cols"] = np.ascontiguousarray(np.concatenate(cols, axis=2))
    out["L0_attn_omega"] = A("omega")
    w1, w2, wr = (np.asarray(i["L0_ffn_" + n]) for n in ("W1", "W2", "Wr"))
    out["moe0_up"] = np.ascontiguousarray(w1.reshape(NE, 2, 2, P, D).transpose(4, 0, 1, 2, 3))
    out["moe0_down"] = np.ascontiguousarray(w2.reshape(NE, D, 2, P).transpose(3, 0, 2, 1))
    out["moe0_router"] = np.ascontiguousarray(wr.T)
    w1, w2, cf, cp, gw = (np.asarray(i["L1_ffn_" + n]) for n in ("w1", "w2", "cfc", "cproj", "gate_w"))
    out["moe1_up"] = np.ascontiguousarray(np.concatenate([w1, cf[None]]).transpose(2, 0, 1)[:, :, None, None, :])
    out["moe1_down"] = np.ascontiguousarray(np.concatenate([w2, cp[None]]).transpose(2, 0, 1)[:, :, None, :])
    out["moe1_router"] = np.ascontiguousarray(gw.T)
    w = [np.asarray(i[f"L1_attn_{n}_w"]).T[:, None, :] for n in "qkv"]
    out["dlt_wqkv"] = np.ascontiguousarray(np.concatenate(w, axis=1))
    out["dlt_bw"] = np.ascontiguousarray(np.asarray(i["L1_attn_b_w"]).T)
    out["dlt_taps"] = np.ascontiguousarray(np.stack([np.asarray(i[f"L1_attn_{n}_cw"]) for n in "qkv"], axis=1))
    out["dlt_short"] = np.asarray(i["L1_attn_fir_short_w"]).reshape(D, SHORT)
    f = np.asarray(i["L1_attn_fir_long_w"]).reshape(D, LONG)[:, ::-1]
    out["dlt_long"] = np.ascontiguousarray(np.pad(f, ((0, 0), (P, P))))
    w1 = np.asarray(i["L1_attn_mlp1_w"]).T
    out["gate_w1a"], out["gate_w1b"] = np.ascontiguousarray(w1[:D]), np.ascontiguousarray(w1[D:])
    out["gate_w2"] = np.ascontiguousarray(np.asarray(i["L1_attn_mlp2_w"]).T)
    out["gate_ow"] = np.ascontiguousarray(np.asarray(i["L1_attn_o_w"]).T)
    out["gate_cols"] = np.ascontiguousarray(np.stack(
        [np.asarray(i["L1_attn_mlp1_b"]), np.tile(np.asarray(i["L1_attn_norm_w"]), HD)], axis=1))
    out["gate_res"] = np.asarray(i["L1_attn_conv_res_logit"])
    out["gate_temp"] = np.asarray(i["L1_attn_logit_temp"])
    out["gate_b2"] = np.asarray(i["L1_attn_mlp2_b"])
    out["moe1_bias"] = np.asarray(i["L1_ffn_lb_bias"])
    return out


def store_tokens(nc, resid, update, out, ngroups):
    with ExitStack() as ctx:
        s = Space(nc, ctx, "out")
        row = s.sb("row", [P, ngroups, TILES, D])
        summed, stored = s.sem("summed"), s.sem("stored")
        block = s.block()

        @block.vector
        def _(dve):
            for g in range(ngroups):
                tiles = slice(g * TILES, (g + 1) * TILES)
                dve.tensor_tensor(row[:, g, :, :], resid[:, tiles, :], update[:, tiles, :],
                                  ALU.add).then_inc(summed, 1)

        @block.sync
        def _(sp):
            for g in range(ngroups):
                sp.wait_ge(summed, g + 1)
                sp.dma_start(out[g * G:(g + 1) * G, :].rearrange("(t p) c -> p t c", p=P),
                             row[:, g, :, :]).then_inc(stored, 16)
            sp.wait_ge(stored, 16 * ngroups)


def program(nc, a, out):
    ntok = a["x"].shape[0]
    ngroups, nseq, tiles = ntok // G, ntok // SEQ, ntok // P
    with ExitStack() as ctx:
        s = Space(nc, ctx, "top")
        resid, x = s.sb("resid", [P, tiles, D]), s.sb("x", [P, tiles, D])
        ident = s.sb("ident", [P, P])
        load_tokens(nc, a["x"], resid, ident, ngroups)
        residual_norm(nc, "n0", resid, None, x, ngroups)
        encoder(nc, a, x, ident)
        residual_norm(nc, "n1", resid, x, x, ngroups)
        mixture(nc, "moe0", x, ident, ngroups, NE, 2, a["moe0_up"], a["moe0_down"], a["moe0_router"], None)
        residual_norm(nc, "n2", resid, x, x, ngroups)
        with ExitStack() as inner:
            streams = Space(nc, inner, "str")
            v_r, short_tm, long_r, delta_tm = (streams.sb(n, [P, tiles, D]) for n in ("v", "short", "long", "delta"))
            delta_mixer(nc, a, x, ident, nseq, v_r, short_tm, delta_tm)
            long_filter(nc, a, ident, nseq, v_r, long_r)
            gate_and_project(nc, a, x, ident, ngroups, v_r, short_tm, long_r, delta_tm)
        residual_norm(nc, "n3", resid, x, x, ngroups)
        mixture(nc, "moe1", x, ident, ngroups, NE + 1, 1, a["moe1_up"], a["moe1_down"], a["moe1_router"],
                a["moe1_bias"])
        store_tokens(nc, resid, x, out, ngroups)


def kernel(**inputs):
    import numpy as np
    import concourse.bacc as bacc
    from concourse.bass_utils import run_bass_kernel_spmd

    laid = lay_out(inputs)
    x = np.asarray(inputs["L0_attn_x"])
    laid["x"] = np.ascontiguousarray(x.reshape(-1, D))
    nc = bacc.Bacc("TRN2", target_bir_lowering=False, num_devices=1)
    arrays = {f"in_{n}": v for n, v in laid.items()}
    a = {n: nc.dram_tensor(f"in_{n}", v.shape, mybir.dt.from_np(v.dtype), kind="ExternalInput").ap()
         for n, v in laid.items()}
    out = nc.dram_tensor("out_y", laid["x"].shape, F32, kind="ExternalOutput").ap()
    program(nc, a, out)
    r = run_bass_kernel_spmd(nc, [arrays], core_ids=[0])
    return r.results[0]["out_y"].reshape(x.shape)
```

```python
from contextlib import ExitStack

import concourse.bass as bass
from concourse import mybir

F32 = mybir.dt.float32
U32 = mybir.dt.uint32
ALU = mybir.AluOpType
ACT = mybir.ActivationFunctionType
AX = mybir.AxisListType

P = 128
D = 128
TILES = 4
G = TILES * P
SEQ = 256


class Space:

    def __init__(self, nc, ctx, tag):
        self.nc, self.ctx, self.tag = nc, ctx, tag
        self.sems = []

    def sb(self, name, shape, dt=F32):
        return self.ctx.enter_context(self.nc.sbuf_tensor(f"{self.tag}_{name}", shape, dt))

    def ps(self, name):
        return self.ctx.enter_context(self.nc.psum_tensor(f"{self.tag}_{name}", [P, 512], F32))

    def sem(self, name):
        handle = self.ctx.enter_context(self.nc.semaphore(f"{self.tag}_{name}"))
        self.sems.append(handle.num)
        return handle

    def block(self):
        self.ctx.callback(self.clear)
        return self.ctx.enter_context(self.nc.Block())

    def clear(self):
        nums = sorted(self.sems)
        starts = [n for n in nums if n - 1 not in nums]
        ends = [n + 1 for n in nums if n + 1 not in nums]
        with self.nc.Block() as block:
            @block.gpsimd
            def _(pool):
                for first, end in zip(starts, ends):
                    pool.sem_clear(range(first, end))


def apart(eng, passes):
    eng.sem_inc(passes, 1)


def load_tokens(nc, x_dram, resid, ident, ngroups):
    with ExitStack() as ctx:
        s = Space(nc, ctx, "ld")
        loaded = [s.sem(f"loaded{g}") for g in range(ngroups)]
        zeroed, ident_ready = s.sem("zeroed"), s.sem("ident_ready")
        block = s.block()

        @block.sync
        def _(sp):
            for g in range(ngroups):
                sp.dma_start(resid[:, g * TILES:(g + 1) * TILES, :],
                             x_dram[g * G:(g + 1) * G, :].rearrange("(t p) c -> p t c", p=P)
                             ).then_inc(loaded[g], 16)
            for g in range(ngroups):
                sp.wait_ge(loaded[g], 16)

        @block.gpsimd
        def _(pool):
            pool.memset(ident[:, :], 0.0).then_inc(zeroed, 1)
            pool.wait_ge(zeroed, 1)
            pool.affine_select(out=ident[:, :], in_=ident[:, :], compare_op=ALU.not_equal, fill=1.0,
                               base=0, pattern=[[-1, P]], channel_multiplier=1).then_inc(ident_ready, 1)


def residual_norm(nc, tag, resid, update, normed, ngroups):
    with ExitStack() as ctx:
        s = Space(nc, ctx, tag)
        st6 = s.sb("st6", [P, TILES, 6])
        mv = s.sb("mv", [P, 2, TILES, 2])
        veps = s.sb("veps", [P, 2, TILES])
        mhalf = s.sb("mhalf", [P, TILES])
        rstd = s.sb("rstd", [P, 2, TILES])
        shift = s.sb("shift", [P, 2, TILES])
        const_ready, summed, stats, var_ready, rstd_ready, shift_ready, normed_ready, passes = (s.sem(n) for n in (
            "const_ready", "summed", "stats", "var_ready", "rstd_ready", "shift_ready", "normed_ready", "passes"))
        block = s.block()

        @block.gpsimd
        def _(pool):
            pool.memset(mhalf[:, :], -0.5).then_inc(const_ready, 1)
            pool.wait_ge(const_ready, 1)
            with pool.Fori(0, ngroups // 2) as i:
                for b in range(2):
                    pool.wait_ge(var_ready, 2 * i + b + 1)
                    pool.tensor_tensor(rstd[:, b, :], veps[:, b, :], mhalf[:, :], ALU.pow).then_inc(rstd_ready, 1)

        @block.scalar
        def _(act):
            with act.Fori(0, ngroups // 2) as i:
                for b in range(2):
                    act.wait_ge(shift_ready, 2 * i + b + 1)
                    for t in range(TILES):
                        tile = bass.ds((2 * i + b) * TILES + t, 1)
                        act.activation(normed[:, tile, :], resid[:, tile, :], ACT.Identity, scale=rstd[:, b, t:t + 1],
                                       bias=shift[:, b, t:t + 1]).then_inc(normed_ready, 1)

        @block.vector
        def _(dve):
            def moments(g, b, reused):
                if update is not None:
                    tiles = bass.ds(g * TILES, TILES)
                    dve.tensor_tensor(resid[:, tiles, :], resid[:, tiles, :], update[:, tiles, :],
                                      ALU.add).then_inc(summed, 1)
                    dve.wait_ge(summed, g + 1)
                    apart(dve, passes)
                for t in range(TILES):
                    dve.bn_stats(st6[:, t, :], resid[:, bass.ds(g * TILES + t, 1), :].rearrange("p a c -> p (a c)")
                                 ).then_inc(stats, 1)
                dve.wait_ge(stats, g * 2 * TILES + TILES)
                if reused:
                    dve.wait_ge(normed_ready, TILES * (g - 1))
                apart(dve, passes)
                for t in range(TILES):
                    dve.bn_aggr(mv[:, b, t, :], st6[:, t, :]).then_inc(stats, 1)
                dve.wait_ge(stats, (g + 1) * 2 * TILES)
                dve.tensor_scalar(veps[:, b, :], mv[:, b, :, 1], 1e-5, None, ALU.add).then_inc(var_ready, 1)

            def shifts(g, b):
                dve.wait_ge(rstd_ready, g + 1)
                dve.scalar_tensor_tensor(out=shift[:, b, :], in0=mv[:, b, :, 0], scalar=-1.0, in1=rstd[:, b, :],
                                         op0=ALU.mult, op1=ALU.mult).then_inc(shift_ready, 1)

            moments(0, 0, False)
            moments(1, 1, False)
            shifts(0, 0)
            with dve.Fori(0, ngroups // 2 - 1) as i:
                moments(2 * i + 2, 0, True)
                shifts(2 * i + 1, 1)
                moments(2 * i + 3, 1, True)
                shifts(2 * i + 2, 0)
            shifts(ngroups - 1, 1)


NL = 6
NH = 16
DH = 8
MF = 16
DFF = 512
FB = DFF // P
C_WQ, C_WK, C_WV, C_WO, C_W1, C_W2 = 0, 128, 256, 384, 512, 1024
C_BV, C_BO, C_G1, C_BE1, C_BF2, C_G2, C_BE2 = (1536 + 128 * i for i in range(7))
C_OM = 1536 + 7 * 128
C_BQ = C_OM + DH
C_BK, C_G1C, C_BE1C, C_BF1C = C_BQ + 1, C_BQ + 2, C_BQ + 3, C_BQ + 4
NPAR = C_BF1C + FB
HALVES = ((slice(0, 64), slice(64, 128)), (slice(64, 128), slice(0, 64)))


def encoder(nc, a, x, ident, nlayers=NL, ngroups=8):
    with ExitStack() as ctx:
        s = Space(nc, ctx, "enc")
        params = s.sb("params", [P, nlayers, NPAR])
        w = s.sb("w", [P, NPAR])
        om = s.sb("om", [P, 2, P])
        own = s.sb("own", [P, NH])
        negown = s.sb("negown", [P, NH])
        hm = s.sb("hm", [P, 8])
        ones = s.sb("ones", [P, P])
        cm = s.sb("cm", [P, 4, P])
        bm = s.sb("bm", [P, 1, 4, 2, 2, DH])
        mhalf = s.sb("mhalf", [P, TILES])
        xg = s.sb("xg", [P, G])
        xb = s.sb("xb", [P, G])
        xTr = s.sb("xTr", [P, G])
        xT = s.sb("xT", [P, G])
        q = s.sb("q", [P, 2, G])
        k = s.sb("k", [P, 2, G])
        vx = s.sb("vx", [P, TILES, NH, 32])
        vc = s.sb("vc", [P, 2, NH // 2, 32])
        qf = s.sb("qf", [P, 2, G])
        kf = s.sb("kf", [P, 2, G])
        qx = s.sb("qx", [P, 2, 8, G])
        kt = s.sb("kt", [P, 2, 2, P])
        st = s.sb("st", [P, 2, 2, P])
        sm = s.sb("sm", [P, 4, 4, P])
        osb = s.sb("osb", [P, 2, 2 * P])
        den = s.sb("den", [P, 2, NH])
        at = s.sb("at", [P, TILES, D])
        aT = s.sb("aT", [P, G])
        h = s.sb("h", [P, TILES, D])
        y1 = s.sb("y1", [P, TILES, D])
        h1 = s.sb("h1", [P, TILES, D])
        h1T = s.sb("h1T", [P, G])
        hid = s.sb("hid", [P, FB, G])
        h2 = s.sb("h2", [P, TILES, D])
        beb = s.sb("beb", [P, D])
        st6 = s.sb("st6", [P, TILES, 6])
        mv = s.sb("mv", [P, 2, TILES, 2])
        veps = s.sb("veps", [P, 2, TILES])
        rstd = s.sb("rstd", [P, 2, TILES])

        bk = s.sb("bk", [P, 1])
        scale = float(DH) ** -0.25

        b_t, b_1, b_2, b_tok = (s.ps(n) for n in ("b_t", "b_1", "b_2", "b_tok"))
        b_o = [s.ps("b_o0"), s.ps("b_o1")]
        b_sc = [s.ps("b_sc0"), s.ps("b_sc1")]

        loaded = s.sem("loaded")
        const, masks_ready, w_ready, om_ready = (s.sem(n) for n in ("const", "masks_ready", "w_ready", "om_ready"))
        xg_ready, xb_ready, sq_ready, vc_ready, h1_ready, rstd_ready = (
            s.sem(n) for n in ("xg_ready", "xb_ready", "sq_ready", "vc_ready", "h1_ready", "rstd_ready"))
        xt_done, qk_done, v_done, phi_done, kt_done, st_done, sc_done, av_done, ot_done, at_done, wo_done, \
            ht_done, hid_done, ffn_done = (s.sem(n) for n in (
                "xt_done", "qk_done", "v_done", "phi_done", "kt_done", "st_done", "sc_done", "av_done",
                "ot_done", "at_done", "wo_done", "ht_done", "hid_done", "ffn_done"))
        q_ready, k_ready, bk_ready, v_ready, qx_ready, st_ready, sm_ready, den_step, a_ready, h_ready, ln_step, var_ready, \
            y1_ready, h2_ready, x_ready = (s.sem(n) for n in (
                "q_ready", "k_ready", "bk_ready", "v_ready", "qx_ready", "st_ready", "sm_ready", "den_step", "a_ready", "h_ready",
                "ln_step", "var_ready", "y1_ready", "h2_ready", "x_ready"))
        xT_ready, f_ready, kt_ready, o_ready, aT_ready, h1T_ready, hid_ready = (
            s.sem(n) for n in ("xT_ready", "f_ready", "kt_ready", "o_ready", "aT_ready", "h1T_ready", "hid_ready"))
        qx1_ready, y2_step, bias_ready = s.sem("qx1_ready"), s.sem("y2_step"), s.sem("bias_ready")
        passes = s.sem("passes")
        dve_const = s.sem("dve_const")
        block = s.block()

        @block.sync
        def _(sp):
            sp.dma_start(params[:, :, 0:C_BV], a["enc_mats"][:, 0:nlayers, :]).then_inc(loaded, 16)
            sp.dma_start(params[:, :, C_BV:C_OM],
                         a["enc_rows"][0:nlayers].unsqueeze(0).to_broadcast([P, nlayers, C_OM - C_BV])
                         ).then_inc(loaded, 16)
            sp.dma_start(params[:, :, C_BQ:NPAR], a["enc_cols"][:, 0:nlayers, :]).then_inc(loaded, 16)
            for hd in range(NH):
                sp.dma_start(params[hd * DH:(hd + 1) * DH, :, C_OM:C_OM + DH],
                             a["L0_attn_omega"][0:nlayers].rearrange("l d m -> d l m")).then_inc(loaded, 16)
            sp.wait_ge(loaded, 16 * (3 + NH))

        @block.gpsimd
        def _(pool):
            n = 0

            def step(ins):
                nonlocal n
                n += 1
                ins.then_inc(const, 1)
                pool.wait_ge(const, n)

            step(pool.memset(ones[:, :], 1.0))
            step(pool.memset(mhalf[:, :], -0.5))
            step(pool.memset(cm[:, :, :], 1.0 / MF))
            step(pool.affine_select(out=cm[:, 0::2, :], in_=cm[:, 0::2, :], compare_op=ALU.is_ge, fill=0.0, base=0,
                                    pattern=[[0, 2], [1, P]], channel_multiplier=-1))
            for b in range(4):
                rows = cm[32 * b:32 * b + 32, 1::2, :]
                step(pool.affine_select(out=rows, in_=rows, compare_op=ALU.is_ge, fill=0.0, base=-32 * (3 - b),
                                        pattern=[[0, 2], [1, P]], channel_multiplier=-1))
            step(pool.affine_select(out=own[:, :], in_=ones[:, 0:NH], compare_op=ALU.is_ge, fill=0.0, base=0,
                                    pattern=[[-DH, NH]], channel_multiplier=1))
            step(pool.affine_select(out=own[:, :], in_=own[:, :], compare_op=ALU.is_ge, fill=0.0, base=DH - 1,
                                    pattern=[[DH, NH]], channel_multiplier=-1))
            step(pool.affine_select(out=hm[:, :], in_=ones[:, 0:8], compare_op=ALU.is_ge, fill=0.0, base=0,
                                    pattern=[[-MF, 8]], channel_multiplier=1))
            step(pool.affine_select(out=hm[:, :], in_=hm[:, :], compare_op=ALU.is_ge, fill=0.0, base=MF - 1,
                                    pattern=[[MF, 8]], channel_multiplier=-1))
            step(pool.memset(vx[:, :, :, :], 0.0))
            for par in (0, 1):
                step(pool.memset(vx[:, :, par::2, 16 + DH * par:24 + DH * par], 1.0))
            pool.memset(vc[:, :, :, 16:32], 1.0).then_inc(masks_ready, 1)

            def residual(it):
                pool.wait_ge(xg_ready, it + 1)
                pool.tensor_tensor(
                    xb[:, :].rearrange("p (t c) -> p t c", t=TILES),
                    xg[:, :].rearrange("p (t c) -> p t c", t=TILES),
                    w[:, C_BO:C_BO + D].unsqueeze(1).to_broadcast([P, TILES, D]), ALU.add).then_inc(xb_ready, 1)

            def first_norm(it):
                pool.wait_ge(var_ready, 2 * it + 1)
                pool.tensor_tensor(rstd[:, 0, :], veps[:, 0, :], mhalf[:, :], ALU.pow).then_inc(rstd_ready, 1)

            def values(it):
                pool.wait_ge(v_ready, it + 1)
                apart(pool, passes)
                for i in range(2):
                    pool.tensor_copy(vc[:, i, :, 0:DH], vx[:, 2 * i, 0::2, 0:DH]).then_inc(vc_ready, 1)

            def ffn_side(it, g):
                pool.wait_ge(y1_ready, TILES * (it + 1))
                pool.tensor_tensor(h1[:, :, :], y1[:, :, :], w[:, C_G1:C_G1 + D].unsqueeze(1).to_broadcast([P, TILES, D]),
                                   ALU.mult).then_inc(h1_ready, 1)
                pool.wait_ge(h1_ready, 2 * it + 1)
                pool.tensor_tensor(h1[:, :, :], h1[:, :, :], beb[:, :].unsqueeze(1).to_broadcast([P, TILES, D]),
                                   ALU.add).then_inc(h1_ready, 1)
                pool.wait_ge(var_ready, 2 * it + 2)
                pool.tensor_tensor(rstd[:, 1, :], veps[:, 1, :], mhalf[:, :], ALU.pow).then_inc(rstd_ready, 1)
                pool.wait_ge(rstd_ready, 2 * it + 2)
                apart(pool, passes)
                for t in range(TILES):
                    pool.tensor_scalar(h2[:, t, :], h2[:, t, :], mv[:, 1, t, 0:1], rstd[:, 1, t:t + 1],
                                       ALU.subtract, ALU.mult).then_inc(y2_step, 1)
                pool.wait_ge(y2_step, 5 * it + TILES)
                pool.tensor_tensor(h2[:, :, :], h2[:, :, :], w[:, C_G2:C_G2 + D].unsqueeze(1).to_broadcast([P, TILES, D]),
                                   ALU.mult).then_inc(y2_step, 1)
                pool.wait_ge(y2_step, 5 * it + TILES + 1)
                pool.tensor_tensor(x[:, bass.ds(g * TILES, TILES), :], h2[:, :, :],
                                   w[:, C_BE2:C_BE2 + D].unsqueeze(1).to_broadcast([P, TILES, D]),
                                   ALU.add).then_inc(x_ready, 1)

            pool.sem_inc(x_ready, 1)
            with pool.Fori(0, nlayers) as l:
                pool.wait_ge(w_ready, 3 * l + 3)
                pool.tensor_tensor(beb[:, :], w[:, C_BE1:C_BE1 + D], w[:, C_BF2:C_BF2 + D],
                                   ALU.add).then_inc(bias_ready, 1)
                pool.wait_ge(bias_ready, l + 1)
                first = l * ngroups
                residual(first)
                values(first)
                with pool.Fori(0, ngroups - 1) as g:
                    it = first + g
                    first_norm(it)
                    residual(it + 1)
                    values(it + 1)
                    ffn_side(it, g)
                last_it = first + (ngroups - 1)
                first_norm(last_it)
                ffn_side(last_it, ngroups - 1)

        @block.tensor
        def _(pe):
            def turn_input(it):
                pe.wait_ge(xg_ready, it + 1)
                for t in range(TILES):
                    last = pe.transpose(b_1[:, t * P:(t + 1) * P], xg[:, t * P:(t + 1) * P], ident[:, :])
                last.then_inc(xt_done, 1)

            def project(it):
                pe.wait_ge(xT_ready, 2 * it + 2)
                for c, b in ((C_WQ, b_1), (C_WK, b_tok)):
                    pe.matmul(b[:, :], w[:, c:c + D], xT[:, :], start=True, stop=True).then_inc(qk_done, 1)

            def values(it):
                for b, src in ((b_t, xT), (b_2, xTr)):
                    if src is xTr:
                        pe.wait_ge(f_ready, 4 * it + 3)
                    for t in range(TILES):
                        last = pe.matmul(b[:, t * D:(t + 1) * D], src[:, t * P:(t + 1) * P], w[:, C_WV:C_WV + D],
                                         start=True, stop=True)
                last.then_inc(v_done, 1)

            def exponents(it, i):
                f, b, src = ((0, b_1, q), (0, b_o[0], k), (1, b_2, q), (1, b_1, k))[i]
                if i < 2:
                    pe.wait_ge(sq_ready, 4 * it + 2 * i + 2)
                if i == 3:
                    pe.wait_ge(f_ready, 4 * it + 1)
                pe.matmul(b[:, :], om[:, f, :], src[:, f, :], start=True, stop=True).then_inc(phi_done, 1)

            def turn_keys(it):
                pe.wait_ge(f_ready, 4 * it + 4)
                for i in range(2):
                    for f in range(2):
                        last = pe.transpose(b_1[:, (2 * i + f) * P:(2 * i + f + 1) * P],
                                            kf[:, f, 2 * i * P:(2 * i + 1) * P], ident[:, :])
                last.then_inc(kt_done, 1)

            def scores(it, c):
                t, f, n = c // 4, c // 2 % 2, c % 4
                if c < 4:
                    pe.wait_ge(qx_ready if n < 2 else qx1_ready, 8 * it + 4 * (n % 2 + 1))
                if c >= 2:
                    pe.wait_ge(sm_ready, 16 * it + c - 1)
                for odd in (0, 1):
                    for b in range(4):
                        kb = 3 - b if odd else b
                        last = pe.matmul(
                            b_sc[c % 2][32 * b:32 * b + 32, :].rearrange("p (h i) -> p h i", h=4)[:, odd::2, 32 * kb:P],
                            kf[:, f, t * P + 32 * kb:t * P + 32 * kb + 32],
                            qx[:, f, 4 * (n % 2) + odd:4 * (n % 2) + 4:2, t * P + 32 * kb:(t + 1) * P],
                            start=True, stop=True)
                last.then_inc(sc_done, 1)

            def combine(it, c):
                t, f, n = c // 4, c // 2 % 2, c % 4
                if n == 0 and t >= 2:
                    pe.wait_ge(o_ready, TILES * it + t - 1)
                if n == 0 and t == 1:
                    pe.wait_ge(st_ready, it + 1)
                pe.wait_ge(sm_ready, 16 * it + c + 2)
                where = [b_o[t % 2][32 * r:32 * r + 32, n // 2 * P:(n // 2 + 1) * P] for r in range(4)]
                for j in (0, 1):
                    for r in range(4):
                        last = pe.matmul(where[r], vx[:, t, 4 * n + 2 * r + j, :],
                                         sm[:, (c + r // 2) % 4, 2 * (r % 2) + j, :], start=(n == 0 and j == 0),
                                         stop=(j == 1 and t % 2 == 0), skip_group_check=True)
                if t % 2:
                    for r in range(4):
                        last = pe.matmul(where[r], st[:, t // 2, f, 32 * r:32 * r + 32], qf[:, f, t * P:(t + 1) * P],
                                         start=False, stop=True, skip_group_check=True)
                last.then_inc(av_done, 1)

            def turn(it, t):
                pe.wait_ge(o_ready, TILES * it + t + 1)
                if t == 0:
                    pass
                else:
                    pe.wait_ge(a_ready, TILES * it + t)
                for i in range(2):
                    last = pe.transpose(b_2[:, i * P:(i + 1) * P], osb[:, t % 2, i * P:(i + 1) * P], ident[:, :])
                last.then_inc(ot_done, 1)

            def turn_back(it, t):
                pe.wait_ge(a_ready, TILES * it + t + 1)
                pe.transpose(b_t[:, t * P:(t + 1) * P], at[:, t, :], ident[:, :]).then_inc(at_done, 1)

            def states(it):
                pe.wait_ge(kt_ready, it + 1)
                pe.wait_ge(vc_ready, 2 * it + 2)
                for i in range(2):
                    for f in range(2):
                        last = pe.matmul(b_t[:, (2 * i + f) * P:(2 * i + f + 1) * P], kt[:, i, f, :],
                                         vc[:, i, 4 * f:4 * f + 4, :], start=True, stop=True)
                last.then_inc(st_done, 1)

            def out_projection(it):
                pe.wait_ge(aT_ready, it + 1)
                for t in range(TILES):
                    last = pe.matmul(b_tok[:, t * D:(t + 1) * D], aT[:, t * P:(t + 1) * P], w[:, C_WO:C_WO + D],
                                     start=True, stop=True)
                last.then_inc(wo_done, 1)

            def ffn(it, follows):
                pe.wait_ge(y1_ready, TILES * (it + 1))
                for t in range(TILES):
                    last = pe.transpose(b_o[0][:, t * P:(t + 1) * P], y1[:, t, :], ident[:, :])
                last.then_inc(ht_done, 1)
                if follows:
                    scores(it + 1, 1)
                pe.wait_ge(h1T_ready, it + 1)
                for f in range(FB):
                    if f >= 2:
                        pe.wait_ge(hid_ready, FB * it + f - 1)
                    pe.matmul(b_o[1 - f % 2][:, :], w[:, C_W1 + f * P:C_W1 + (f + 1) * P], h1T[:, :],
                              start=True, stop=True).then_inc(hid_done, 1)
                for f in range(FB):
                    pe.wait_ge(hid_ready, FB * it + f + 1)
                    for t in range(TILES):
                        last = pe.matmul(b_tok[:, t * D:(t + 1) * D], hid[:, f, t * P:(t + 1) * P],
                                         w[:, C_W2 + f * D:C_W2 + (f + 1) * D], start=(f == 0 and t == 0),
                                         stop=(f == FB - 1), skip_group_check=True)
                last.then_inc(ffn_done, 1)

            def group(it, follows):
                for c in range(3, 4 * TILES + 2):
                    if 4 <= c < 4 * TILES:
                        scores(it, c)
                    if c == 3:
                        states(it)
                    if c % 2:
                        combine(it, c - 3)
                    if c in (7, 11, 15):
                        turn(it, c // 4 - 1)
                    if c in (9, 13, 17):
                        turn_back(it, c // 4 - 2)
                    if follows and c == 6:
                        turn_input(it + 1)
                    if follows and c == 8:
                        project(it + 1)
                if follows:
                    exponents(it + 1, 0)
                turn(it, TILES - 1)
                if follows:
                    exponents(it + 1, 1)
                turn_back(it, TILES - 1)
                if follows:
                    exponents(it + 1, 2)
                out_projection(it)
                if follows:
                    exponents(it + 1, 3)
                    values(it + 1)
                    turn_keys(it + 1)
                    scores(it + 1, 0)
                ffn(it, follows)
                if follows:
                    scores(it + 1, 2)
                    scores(it + 1, 3)

            pe.wait_ge(masks_ready, 1)
            with pe.Fori(0, nlayers) as l:
                first = l * ngroups
                turn_input(first)
                pe.wait_ge(w_ready, 3 * l + 2)
                project(first)
                pe.wait_ge(om_ready, 4 * l + 4)
                for i in range(4):
                    exponents(first, i)
                values(first)
                turn_keys(first)
                for c in range(4):
                    scores(first, c)
                with pe.Fori(0, ngroups - 1) as g:
                    group(first + g, True)
                group(first + (ngroups - 1), False)

        @block.scalar
        def _(act):
            def fetch(it, g):
                act.activation(xg[:, :].rearrange("p (t c) -> p t c", t=TILES), x[:, bass.ds(g * TILES, TILES), :],
                               ACT.Copy).then_inc(xg_ready, 1)

            def turned(it):
                act.wait_ge(xt_done, it + 1)
                act.activation(xT[:, :], b_1[:, :], ACT.Copy).then_inc(xT_ready, 1)
                act.activation(xTr[:, :].rearrange("p (t b r) -> p t b r", t=TILES, b=4),
                               b_1[:, :].rearrange("p (t b r) -> p t b r", t=TILES, b=4)[:, :, ::-1, :],
                               ACT.Copy).then_inc(xT_ready, 1)

            def squares(it):
                act.wait_ge(qk_done, 2 * it + 2)
                for f, (own_rows, _) in enumerate(HALVES):
                    act.activation(k[own_rows, f, :], b_tok[own_rows, :], ACT.Identity, scale=scale,
                                   bias=bk[own_rows, :]).then_inc(k_ready, 1)
                for i, (v, ready) in enumerate(((q, q_ready), (k, k_ready))):
                    act.wait_ge(ready, 2 * it + 2)
                    for f, (own_rows, other) in enumerate(HALVES):
                        act.activation(v[other, f, :], v[own_rows, f, :], ACT.Square).then_inc(sq_ready, 1)

            def features(it, i):
                f, b, dst = ((0, b_1, qf), (0, b_o[0], kf), (1, b_2, qf), (1, b_1, kf))[i]
                act.wait_ge(phi_done, 4 * it + i + 1)
                act.activation(dst[:, f, :], b[:, :], ACT.Exp).then_inc(f_ready, 1)

            def expand(it, half):
                for hd in range(4 * half, 4 * half + 4):
                    act.activation(qx[:, 1, hd, :], qf[:, 1, :], ACT.Identity,
                                   scale=hm[:, hd:hd + 1]).then_inc(qx1_ready, 1)

            def keys(it):
                act.wait_ge(kt_done, it + 1)
                act.activation(kt[:, :, :, :].rearrange("p a b c -> p (a b c)"), b_1[:, :],
                               ACT.Copy).then_inc(kt_ready, 1)

            def outputs(it, t):
                act.wait_ge(av_done, 8 * it + 2 * (t + 1))
                act.activation(osb[:, t % 2, :], b_o[t % 2][:, 0:2 * P], ACT.Copy).then_inc(o_ready, 1)

            def group(it, g, follows):
                outputs(it, 0)
                if follows:
                    act.wait_ge(xb_ready, it + 1)
                    fetch(it + 1, g + 1)
                    turned(it + 1)
                outputs(it, 1)
                if follows:
                    squares(it + 1)
                outputs(it, 2)
                outputs(it, 3)
                if follows:
                    features(it + 1, 0)
                    features(it + 1, 1)
                act.wait_ge(at_done, TILES * (it + 1))
                act.activation(aT[:, :], b_t[:, :], ACT.Copy).then_inc(aT_ready, 1)
                if follows:
                    features(it + 1, 2)
                    features(it + 1, 3)
                    act.wait_ge(f_ready, 4 * it + 7)
                    expand(it + 1, 0)
                    keys(it + 1)
                act.wait_ge(ht_done, it + 1)
                act.activation(h1T[:, :], b_o[0][:, :], ACT.Identity, scale=w[:, C_G1C:C_G1C + 1],
                               bias=w[:, C_BE1C:C_BE1C + 1]).then_inc(h1T_ready, 1)
                for f in range(FB):
                    act.wait_ge(hid_done, FB * it + f + 1)
                    act.activation(hid[:, f, :], b_o[1 - f % 2][:, :], ACT.Relu,
                                   bias=w[:, C_BF1C + f:C_BF1C + f + 1]).then_inc(hid_ready, 1)
                if follows:
                    expand(it + 1, 1)

            act.wait_ge(loaded, 16 * (3 + NH))
            act.wait_ge(masks_ready, 1)
            with act.Fori(0, nlayers) as l:
                first = l * ngroups
                act.wait_ge(h2_ready, first + 1)
                for start, end in ((C_OM, NPAR), (0, C_BV)):
                    act.activation(w[:, start:end], params[:, bass.ds(l, 1), start:end].rearrange("p a b -> p (a b)"),
                                   ACT.Copy).then_inc(w_ready, 1)
                act.wait_ge(w_ready, 3 * l + 1)
                act.activation(bk[:, :], w[:, C_BK:C_BK + 1], ACT.Copy, scale=scale).then_inc(bk_ready, 1)
                fetch(first, 0)
                turned(first)
                act.wait_ge(bk_ready, l + 1)
                squares(first)
                act.wait_ge(x_ready, first + 1)
                act.activation(w[:, C_BV:C_OM], params[:, bass.ds(l, 1), C_BV:C_OM].rearrange("p a b -> p (a b)"),
                               ACT.Copy).then_inc(w_ready, 1)
                for i in range(4):
                    features(first, i)
                act.wait_ge(f_ready, 4 * first + 3)
                expand(first, 0)
                keys(first)
                expand(first, 1)
                with act.Fori(0, ngroups - 1) as g:
                    group(first + g, g, True)
                group(first + (ngroups - 1), ngroups - 1, False)

        @block.vector
        def _(dve):
            def queries(it):
                dve.wait_ge(qk_done, 2 * it + 1)
                for f, (rows, _) in enumerate(HALVES):
                    dve.tensor_scalar(q[rows, f, :], b_1[rows, :], w[rows, C_BQ:C_BQ + 1], scale, ALU.add,
                                      ALU.mult).then_inc(q_ready, 1)

            def values(it):
                dve.wait_ge(v_done, it + 1)
                dve.tensor_tensor(
                    vc[:, :, :, DH:2 * DH],
                    b_t[:, :].rearrange("p (t a b d) -> p t a b d", t=TILES, a=8, b=2)[:, 0::2, :, 1, :],
                    w[:, C_BV:C_BV + D].rearrange("p (a b d) -> p a b d", a=8, b=2)[:, :, 1, :]
                    .unsqueeze(1).to_broadcast([P, 2, 8, DH]), ALU.add)
                for par in (0, 1):
                    last = dve.tensor_tensor(
                        vx[:, :, par::2, DH * par:DH * par + DH],
                        (b_t, b_2)[par][:, :].rearrange("p (t a b d) -> p t a b d", t=TILES, a=8, b=2)[:, :, :, par, :],
                        w[:, C_BV:C_BV + D].rearrange("p (a b d) -> p a b d", a=8, b=2)[:, :, par, :]
                        .unsqueeze(1).to_broadcast([P, TILES, 8, DH]), ALU.add)
                last.then_inc(v_ready, 1)

            def expand(it, start, end):
                if start == 0:
                    dve.wait_ge(f_ready, 4 * it + 1)
                for hd in range(start, end):
                    dve.tensor_scalar(qx[:, 0, hd, :], qf[:, 0, :], hm[:, hd:hd + 1], None,
                                      ALU.mult).then_inc(qx_ready, 1)

            def mask(it, c):
                dve.wait_ge(sc_done, 16 * it + c + 1)
                if c >= 4:
                    dve.wait_ge(av_done, 8 * it + (c - 4) // 2 + 1)
                dve.tensor_tensor(sm[:, c % 4, :, :], b_sc[c % 2][:, :].rearrange("p (h i) -> p h i", h=4),
                                  cm[:, :, :], ALU.mult).then_inc(sm_ready, 1)

            def normalise(it, t):
                dve.wait_ge(ot_done, TILES * it + t + 1)
                o = b_2[:, 0:256].rearrange("p (a k j d) -> p a k j d", k=2, j=2, d=DH)
                dve.tensor_scalar(den[:, 0, :].rearrange("p (a j) -> p a j", j=2), o[:, :, 1, :, 0],
                                  1e-6, None, ALU.add).then_inc(den_step, 1)
                dve.wait_ge(den_step, 2 * (TILES * it + t) + 1)
                dve.reciprocal(den[:, 1, :], den[:, 0, :]).then_inc(den_step, 1)
                dve.wait_ge(den_step, 2 * (TILES * it + t) + 2)
                dve.tensor_tensor(at[:, t, :].rearrange("p (a j d) -> p a j d", j=2, d=DH), o[:, :, 0, :, :],
                                  den[:, 1, :].rearrange("p (a j) -> p a j", j=2).unsqueeze(3)
                                  .to_broadcast([P, 8, 2, DH]), ALU.mult).then_inc(a_ready, 1)

            def moments(it, which, src):
                base = (2 * it + which) * 2 * TILES
                for t in range(TILES):
                    dve.bn_stats(st6[:, t, :], src[:, t, :]).then_inc(ln_step, 1)
                dve.wait_ge(ln_step, base + TILES)
                apart(dve, passes)
                for t in range(TILES):
                    dve.bn_aggr(mv[:, which, t, :], st6[:, t, :]).then_inc(ln_step, 1)
                dve.wait_ge(ln_step, base + 2 * TILES)
                dve.tensor_scalar(veps[:, which, :], mv[:, which, :, 1], 1e-5, None, ALU.add).then_inc(var_ready, 1)

            def group(it, follows):
                for c in range(3, 4 * TILES):
                    if c >= 4:
                        mask(it, c)
                    if c == 3:
                        dve.wait_ge(st_done, it + 1)
                        dve.tensor_tensor(
                            st[:, :, :, :].rearrange("p i f c -> p (i f) c"),
                            b_t[:, :].rearrange("p (i c) -> p i c", i=4),
                            bm[:, 0, :, :, :, :].rearrange("p a k j d -> p (a k j d)").unsqueeze(1)
                            .to_broadcast([P, 4, P]), ALU.mult).then_inc(st_ready, 1)
                    if c >= 5 and c % 4 == 3:
                        normalise(it, c // 4 - 1)
                    if follows and c == 9:
                        queries(it + 1)
                normalise(it, TILES - 1)
                if follows:
                    expand(it + 1, 0, 6)
                dve.wait_ge(wo_done, it + 1)
                dve.wait_ge(xb_ready, it + 1)
                dve.tensor_tensor(h[:, :, :].rearrange("p t c -> p (t c)"), b_tok[:, :], xb[:, :],
                                  ALU.add).then_inc(h_ready, 1)
                dve.wait_ge(h_ready, it + 1)
                moments(it, 0, h)
                if follows:
                    expand(it + 1, 6, 8)
                dve.wait_ge(rstd_ready, 2 * it + 1)
                for t in range(TILES):
                    dve.tensor_scalar(y1[:, t, :], h[:, t, :], mv[:, 0, t, 0:1], rstd[:, 0, t:t + 1],
                                      ALU.subtract, ALU.mult).then_inc(y1_ready, 1)
                if follows:
                    values(it + 1)
                    mask(it + 1, 0)
                    mask(it + 1, 1)
                dve.wait_ge(ffn_done, it + 1)
                dve.wait_ge(h1_ready, 2 * it + 2)
                dve.wait_ge(x_ready, it + 1)
                dve.tensor_tensor(h2[:, :, :].rearrange("p t c -> p (t c)"), b_tok[:, :],
                                  h1[:, :, :].rearrange("p t c -> p (t c)"), ALU.add).then_inc(h2_ready, 1)
                if follows:
                    mask(it + 1, 2)
                    mask(it + 1, 3)
                dve.wait_ge(h2_ready, it + 2)
                moments(it, 1, h2)

            dve.sem_inc(h2_ready, 1)
            dve.wait_ge(masks_ready, 1)
            for i in range(2):
                dve.memset(b_sc[i][:, :], 0.0).then_inc(dve_const, 1)
            dve.tensor_scalar(negown[:, :], own[:, :], -1.0, None, ALU.mult).then_inc(dve_const, 1)
            for f, (_, other) in enumerate(HALVES):
                dve.tensor_scalar(om[other, f, :].rearrange("p (h m) -> p h m", m=MF),
                                  own[other, 8 * (1 - f):8 * (2 - f)].unsqueeze(2).to_broadcast([64, 8, MF]), -0.5, None,
                                  ALU.mult).then_inc(dve_const, 1)
            for kind in range(2):
                dve.tensor_scalar(bm[:, 0, :, kind, :, :],
                                  hm[:, :].rearrange("p (a b) -> p a b", a=4).unsqueeze(3).to_broadcast([P, 4, 2, DH]),
                                  1.0 / MF, None, ALU.mult).then_inc(dve_const, 1)
            dve.wait_ge(dve_const, 7)
            with dve.Fori(0, nlayers) as l:
                dve.wait_ge(w_ready, 3 * l + 1)
                for sign, o in ((0, own), (1, negown)):
                    for f, (rows, _) in enumerate(HALVES):
                        dve.tensor_tensor(
                            om[rows, f, :].rearrange("p (h m) -> p h m", m=MF)[:, :, DH * sign:DH * sign + DH],
                            w[rows, C_OM:C_OM + DH].unsqueeze(1).to_broadcast([64, 8, DH]),
                            o[rows, 8 * f:8 * f + 8].unsqueeze(2).to_broadcast([64, 8, DH]),
                            ALU.mult).then_inc(om_ready, 1)
                first = l * ngroups
                queries(first)
                expand(first, 0, 8)
                dve.wait_ge(w_ready, 3 * l + 3)
                values(first)
                for c in range(4):
                    mask(first, c)
                with dve.Fori(0, ngroups - 1) as g:
                    group(first + g, True)
                group(first + (ngroups - 1), False)


NE = 8


def mixture(nc, tag, x, ident, ngroups, experts, blocks, up_dram, down_dram, router_dram, bias_dram):
    gated = bias_dram is None
    ways = 2 if gated else 1
    units = [(e, f) for e in range(experts) for f in range(blocks)]
    U = len(units)
    TURN, ROUTE, CHOOSE, MARK, WEIGH = (3, 5, U - 3, U - 2, U) if gated else (2, 3, 4, 7, U)
    with ExitStack() as ctx:
        s = Space(nc, ctx, tag)
        up = s.sb("up", [P, experts, ways, blocks, P])
        down = s.sb("down", [P, experts, blocks, D])
        wr = s.sb("wr", [P, NE])
        bias = s.sb("bias", [P, NE])
        xg = s.sb("xg", [P, G])
        xT = s.sb("xT", [P, 2, G])
        act = s.sb("act", [P, 2, G])
        hid = s.sb("hid", [P, 3, G])
        acc = s.sb("acc", [P, TILES, D])
        index = s.sb("index", [P, NE])
        lg = s.sb("lg", [P, TILES, NE])
        lb = s.sb("lb", [P, TILES, NE])
        top = s.sb("top", [P, TILES, 8])
        tidx = s.sb("tidx", [P, TILES, 8], U32)
        tif = s.sb("tif", [P, TILES, 8])
        eq1 = s.sb("eq1", [P, TILES, NE])
        eq2 = s.sb("eq2", [P, TILES, NE])
        score = s.sb("score", [P, TILES, NE])
        done = s.sb("done", [P, 1])
        total = s.sb("total", [P, 2, TILES])
        rw = s.sb("rw", [P, 2, TILES, experts])
        b_t, b_r = s.ps("b_t"), s.ps("b_r")
        b_v = [s.ps("b_v0"), s.ps("b_v1")]
        b_g = [s.ps("b_g0"), s.ps("b_g1")] if gated else b_v
        b_y = [s.ps("b_y0"), s.ps("b_y1")]
        loaded, const_ready = s.sem("loaded"), s.sem("const_ready")
        xg_ready, xt_done, xT_ready, lg_done, route, route_act, score_ready, rw_ready = (s.sem(n) for n in (
            "xg_ready", "xt_done", "xT_ready", "lg_done", "route", "route_act", "score_ready", "rw_ready"))
        up_done, act_ready, hid_ready, down_done, acc_ready, stored = (s.sem(n) for n in (
            "up_done", "act_ready", "hid_ready", "down_done", "acc_ready", "stored"))
        acc_step, chain, passes = s.sem("acc_step"), s.sem("chain"), s.sem("passes")
        block = s.block()
        NLOAD = 3 if gated else 4

        @block.sync
        def _(sp):
            sp.dma_start(wr[:, :], router_dram).then_inc(loaded, 16)
            sp.dma_start(up[:, :, :, :, :], up_dram).then_inc(loaded, 16)
            sp.dma_start(down[:, :, :, :], down_dram).then_inc(loaded, 16)
            if not gated:
                sp.dma_start(bias[:, :], bias_dram.unsqueeze(0).to_broadcast([P, NE])).then_inc(loaded, 16)
            sp.wait_ge(loaded, 16 * NLOAD)

        @block.gpsimd
        def _(pool):
            for e in range(NE):
                pool.memset(index[:, e:e + 1], float(e)).then_inc(const_ready, 1)
            pool.memset(rw[:, :, :, :], 1.0).then_inc(const_ready, 1)

            def fetch(g):
                pool.tensor_copy(xg[:, :].rearrange("p (t c) -> p t c", t=TILES),
                                 x[:, bass.ds(g * TILES, TILES), :]).then_inc(xg_ready, 1)

            def store(g):
                pool.wait_ge(acc_ready, g + 1)
                pool.tensor_copy(x[:, bass.ds(g * TILES, TILES), :], acc[:, :, :]).then_inc(stored, 1)

            pool.sem_inc(stored, 1)
            fetch(0)
            pool.wait_ge(xt_done, 1)
            fetch(1)
            with pool.Fori(0, ngroups - 2) as g:
                pool.wait_ge(xt_done, g + 2)
                fetch(g + 2)
                store(g)
            store(ngroups - 2)
            store(ngroups - 1)

        @block.tensor
        def _(pe):
            def turn(g):
                pe.wait_ge(xg_ready, g + 1)
                for t in range(TILES):
                    last = pe.transpose(b_t[:, t * P:(t + 1) * P], xg[:, t * P:(t + 1) * P], ident[:, :])
                last.then_inc(xt_done, 1)

            def logits(g, b):
                pe.wait_ge(xT_ready, g + 1)
                for t in range(TILES):
                    last = pe.matmul(b_r[:, t * NE:(t + 1) * NE], xT[:, b, t * P:(t + 1) * P], wr[:, :],
                                     start=True, stop=True)
                last.then_inc(lg_done, 1)

            def expand(g, b, u):
                e, f = units[u]
                if u >= 2:
                    pe.wait_ge(hid_ready, g * U + u - 1)
                for i in reversed(range(ways)):
                    last = pe.matmul((b_v, b_g)[i][u % 2][:, :], up[:, e, i, f, :], xT[:, b, :], start=True, stop=True)
                last.then_inc(up_done, 1)

            def contract(g, u):
                e, f = units[u]
                pe.wait_ge(hid_ready, g * U + u + 1)
                if f == 0:
                    pe.wait_ge(acc_step, (g * experts + max(e - 1, 0)) * TILES + 1)
                for t in range(TILES):
                    last = pe.matmul(b_y[e % 2][:, t * D:(t + 1) * D], hid[:, u % 3, t * P:(t + 1) * P],
                                     down[:, e, f, :], start=(f == 0 and t == 0), stop=(f == blocks - 1),
                                     skip_group_check=True)
                last.then_inc(down_done, 1)

            def group(g, b, last=False):
                for u in range(U + 2):
                    if u < U:
                        expand(g, b, u)
                    if u == TURN and not last:
                        turn(g + 1)
                    if u == ROUTE and not last:
                        logits(g + 1, 1 - b)
                    if u >= 2:
                        contract(g, u - 2)

            pe.wait_ge(loaded, 16 * NLOAD)
            turn(0)
            logits(0, 0)
            group(0, 0)
            with pe.Fori(0, ngroups // 2 - 1) as i:
                group(2 * i + 1, 1)
                group(2 * i + 2, 0)
            group(ngroups - 1, 1, last=True)

        @block.scalar
        def _(act_e):
            def copy_x(g, b):
                act_e.wait_ge(xt_done, g + 1)
                act_e.activation(xT[:, b, :], b_t[:, :], ACT.Copy).then_inc(xT_ready, 1)

            def scores(g):
                act_e.wait_ge(route, g + 1)
                act_e.activation(score[:, :, :], score[:, :, :],
                                 ACT.Exp if gated else ACT.Sigmoid).then_inc(route_act, 1)

            def group(g, b, last=False):
                for u in range(U):
                    act_e.wait_ge(up_done, g * U + u + 1)
                    if u >= 2:
                        act_e.wait_ge(hid_ready, g * U + u - 1)
                    act_e.activation(act[:, u % 2, :], b_g[u % 2][:, :],
                                     ACT.Silu if gated else ACT.Relu).then_inc(act_ready, 1)
                    if not gated:
                        act_e.wait_ge(act_ready, g * U + u + 1)
                        act_e.activation(hid[:, u % 3, :], act[:, u % 2, :], ACT.Square).then_inc(hid_ready, 1)
                    if u == TURN and not last:
                        copy_x(g + 1, 1 - b)
                if not last:
                    scores(g + 1)

            copy_x(0, 0)
            scores(0)
            group(0, 0)
            with act_e.Fori(0, ngroups // 2 - 1) as i:
                group(2 * i + 1, 1)
                group(2 * i + 2, 0)
            group(ngroups - 1, 1, last=True)

        @block.vector
        def _(dve):
            def links(n):
                def link(ins):
                    nonlocal n
                    n = n + 1
                    ins.then_inc(chain, 1)
                    dve.wait_ge(chain, n)
                    apart(dve, passes)
                return link

            def choose(g):
                link = links(NR * g)
                dve.wait_ge(lg_done, g + 1)
                link(dve.tensor_copy(lg[:, :, :].rearrange("p t e -> p (t e)"), b_r[:, 0:TILES * NE]))
                if gated:
                    pick = lg
                else:
                    pick = lb
                    link(dve.tensor_tensor(lb[:, :, :], lg[:, :, :], bias[:, :].unsqueeze(1).to_broadcast([P, TILES, NE]),
                                           ALU.add))
                for t in range(TILES):
                    link(dve.max(top[:, t, :], pick[:, t, :]))
                for t in range(TILES):
                    link(dve.max_index(tidx[:, t, :], top[:, t, :], pick[:, t, :]))
                if gated:
                    dve.tensor_tensor(score[:, :, :], lg[:, :, :], top[:, :, 0:1].to_broadcast([P, TILES, NE]),
                                      ALU.subtract).then_inc(route, 1)
                else:
                    dve.tensor_copy(score[:, :, :], lg[:, :, :]).then_inc(route, 1)

            def mark(g):
                link = links(NR * g + (9 if gated else 10))
                link(dve.tensor_copy(tif[:, :, :], tidx[:, :, :]))
                for i, eq in enumerate((eq1, eq2)):
                    link(dve.tensor_tensor(eq[:, :, :], index[:, :].unsqueeze(1).to_broadcast([P, TILES, NE]),
                                           tif[:, :, i:i + 1].to_broadcast([P, TILES, NE]), ALU.is_equal))
                link(dve.tensor_tensor(eq1[:, :, :], eq1[:, :, :], eq2[:, :, :], ALU.add))

            def weigh(g, b):
                link = links(NR * g + (13 if gated else 14))
                dve.wait_ge(route_act, g + 1)
                link(dve.tensor_tensor(eq1[:, :, :], eq1[:, :, :], score[:, :, :], ALU.mult))
                link(dve.tensor_reduce(total[:, 0, :], eq1[:, :, :], AX.X, ALU.add))
                if not gated:
                    link(dve.tensor_scalar(total[:, 0, :], total[:, 0, :], 1e-6, None, ALU.add))
                link(dve.reciprocal(total[:, 1, :], total[:, 0, :]))
                link(dve.tensor_tensor(rw[:, b, :, 0:NE], eq1[:, :, :], total[:, 1, :].unsqueeze(2)
                                       .to_broadcast([P, TILES, NE]), ALU.mult))

            NR = 17 if gated else 19

            def product(g, u):
                dve.wait_ge(act_ready, g * U + u + 1)
                if u >= 3:
                    dve.wait_ge(down_done, g * U + u - 2)
                dve.tensor_tensor(hid[:, u % 3, :], b_v[u % 2][:, :], act[:, u % 2, :], ALU.mult).then_inc(hid_ready, 1)

            def gather(g, b, e):
                dve.wait_ge(down_done, g * U + (e + 1) * blocks)
                if e == 0:
                    dve.wait_ge(stored, g + 1)
                else:
                    dve.wait_ge(acc_step, (g * experts + e) * TILES + 1)
                for t in range(TILES):
                    y, wt = b_y[e % 2][:, t * D:(t + 1) * D], rw[:, b, t, e:e + 1]
                    if e == 0:
                        dve.tensor_scalar(acc[:, t, :], y, wt, None, ALU.mult).then_inc(acc_step, 1)
                    else:
                        dve.scalar_tensor_tensor(out=acc[:, t, :], in0=y, scalar=wt, in1=acc[:, t, :],
                                                 op0=ALU.mult, op1=ALU.add).then_inc(acc_step, 1)

            def group(g, b, last=False):
                for u in range(U + 3):
                    if u < U and gated:
                        product(g, u)
                    if u == CHOOSE and not last:
                        choose(g + 1)
                    if u == MARK and not last:
                        mark(g + 1)
                    if u >= 3 and units[u - 3][1] == blocks - 1:
                        gather(g, b, units[u - 3][0])
                    if u == WEIGH and not last:
                        weigh(g + 1, 1 - b)
                dve.wait_ge(acc_step, (g + 1) * experts * TILES + 1)
                dve.memset(done[:, :], 0.0).then_inc(acc_ready, 1)

            dve.sem_inc(acc_step, 1)
            dve.wait_ge(const_ready, NE + 1)
            dve.wait_ge(loaded, 16 * NLOAD)
            choose(0)
            mark(0)
            weigh(0, 0)
            group(0, 0)
            with dve.Fori(0, ngroups // 2 - 1) as i:
                group(2 * i + 1, 1)
                group(2 * i + 2, 0)
            group(ngroups - 1, 1, last=True)


HD = 4
DK = 32
LEVELS = 7
TAPS, SHORT, LONG = 4, 5, 64


def delta_mixer(nc, a, x, ident, nseq, v_r, short_tm, delta_tm):
    S2 = 2 * P
    NC = SHORT + 1
    with ExitStack() as ctx:
        s = Space(nc, ctx, "dlt")
        wqkv = s.sb("wqkv", [P, 3, D])
        bw = s.sb("bw", [P, HD])
        taps = s.sb("taps", [P, 3, TAPS])
        ftaps = s.sb("ftaps", [P, SHORT])
        ones = s.sb("ones", [P, P])
        hmask = s.sb("hmask", [P, HD])
        strict = s.sb("strict", [P, P])
        causal = s.sb("causal", [P, P])
        blocks = s.sb("blocks", [P, LEVELS + 1, P])
        couple = s.sb("couple", [P, LEVELS, P])
        mhalf = s.sb("mhalf", [P, 4 * HD])
        xg = s.sb("xg", [P, S2])
        xT = s.sb("xT", [P, S2])
        pad = s.sb("pad", [P, 3, TAPS - 1 + S2])
        conv = s.sb("conv", [P, 3, S2])
        sg = s.sb("sg", [P, 3, S2])
        qk = s.sb("qk", [P, 2, S2])
        vpad = s.sb("vpad", [P, SHORT - 1 + S2])
        sf = s.sb("sf", [P, S2])
        beta = s.sb("beta", [P, 2, 2, HD])
        qk_tm = s.sb("qk_tm", [P, 2, 2, D])
        vs_tm = s.sb("vs_tm", [P, 2, 2, D])
        sq = s.sb("sq", [P, 2, 2, D])
        ss = s.sb("ss", [P, 2, 4 * HD])
        rn = s.sb("rn", [P, 4 * HD])
        qkn = s.sb("qkn", [P, 2, 2, D])
        kb = s.sb("kb", [P, 2, D])
        vb = s.sb("vb", [P, 2, D])
        k0 = s.sb("k0", [P, D])
        qT1 = s.sb("qT1", [P, P])
        qknT = s.sb("qknT", [P, 2, S2])
        qkx = s.sb("qkx", [P, 2, 2, HD, P])
        M = s.sb("M", [P, 2, HD, P])
        MT = s.sb("MT", [P, 2, HD, P])
        AT = s.sb("AT", [P, 2, HD, P])
        CT = s.sb("CT", [P, 2, 2, HD, P])
        X = s.sb("X", [P, 2, HD, P])
        Y = s.sb("Y", [P, 2, HD, P])
        PX = s.sb("PX", [P, 2, HD, P])
        uwT = s.sb("uwT", [P, 3, P])
        u = s.sb("u", [P, 2, D])
        state = s.sb("state", [P, D])
        ua = s.sb("ua", [P, D])
        oT = s.sb("oT", [P, S2])
        B = [s.ps(f"b{i}") for i in range(8)]
        bP, bY, bX = (B[5], B[6]), (B[1], B[2]), (B[7], B[0])
        (loaded, const, const_ready, xg_ready, xt_done, xT_ready, proj_done, pad_ready, beta_sig, dchain, conv_ready,
         silu_ready, sf_ready, tm_done, tm_ready, sq_ready, rn_ready, ss_ready, qkn_ready, qknt_done, qknT_ready,
         qkx_ready, kk_done, at_done, m_ready, at_ready, mt_done, mt_ready, ct_ready, xt2_done, x_ready, p_done,
         p_ready, yy_done, y_ready, uw_done, uw_ready, ut_done, u_ready, st_done, state_ready, ws_done, ua_ready,
         ot_done, oT_ready, o_done, o_ready, kept, scaled, late_ready, sg_ready,
         passes) = (s.sem(n) for n in (
             "loaded const const_ready xg_ready xt_done xT_ready proj_done pad_ready beta_sig dchain conv_ready "
             "silu_ready sf_ready tm_done tm_ready sq_ready rn_ready ss_ready qkn_ready qknt_done qknT_ready "
             "qkx_ready kk_done at_done m_ready at_ready mt_done mt_ready ct_ready xt2_done x_ready p_done "
             "p_ready yy_done y_ready uw_done uw_ready ut_done u_ready st_done state_ready ws_done ua_ready "
             "ot_done oT_ready o_done o_ready kept scaled late_ready "
             "sg_ready passes").split())
        block = s.block()

        @block.sync
        def _(sp):
            for dst, src in ((wqkv[:, :, :], a["dlt_wqkv"]), (bw[:, :], a["dlt_bw"]), (taps[:, :, :], a["dlt_taps"]),
                             (ftaps[:, :], a["dlt_short"])):
                sp.dma_start(dst, src).then_inc(loaded, 16)
            sp.wait_ge(loaded, 64)

        @block.gpsimd
        def _(pool):
            n = 0

            def step(ins):
                nonlocal n
                n += 1
                ins.then_inc(const, 1)
                pool.wait_ge(const, n)

            def in_blocks(dst, size, count, src):
                w = dst.shape[-1] // count
                d3 = dst.rearrange("p (a r) -> p a r", a=count)
                s3 = src.rearrange("p (a r) -> p a r", a=count)
                step(pool.affine_select(out=d3, in_=s3, compare_op=ALU.is_ge, fill=0.0, base=0,
                                        pattern=[[-size, count], [0, w]], channel_multiplier=1))
                step(pool.affine_select(out=d3, in_=d3, compare_op=ALU.is_ge, fill=0.0, base=size - 1,
                                        pattern=[[size, count], [0, w]], channel_multiplier=-1))

            step(pool.memset(ones[:, :], 1.0))
            step(pool.memset(mhalf[:, :], -0.5))
            step(pool.memset(pad[:, :, 0:TAPS - 1], 0.0))
            step(pool.memset(vpad[:, 0:SHORT - 1], 0.0))
            step(pool.affine_select(out=strict[:, :], in_=ones[:, :], compare_op=ALU.is_gt, fill=0.0, base=0,
                                    pattern=[[-1, P]], channel_multiplier=1))
            step(pool.affine_select(out=causal[:, :], in_=ones[:, :], compare_op=ALU.is_ge, fill=0.0, base=0,
                                    pattern=[[1, P]], channel_multiplier=-1))
            in_blocks(hmask[:, :], DK, HD, ones[:, 0:HD])
            for l in range(LEVELS + 1):
                in_blocks(blocks[:, l, :], 2 ** l, P >> l, ones[:, :])
            for l in range(LEVELS):
                step(pool.tensor_tensor(couple[:, l, :], blocks[:, l + 1, :], blocks[:, l, :], ALU.subtract))
            pool.memset(ua[:, :], 0.0).then_inc(const_ready, 1)
            def fetch(q):
                pool.tensor_copy(xg[:, :].rearrange("p (t c) -> p t c", t=2),
                                 x[:, bass.ds(q * 2, 2), :]).then_inc(xg_ready, 1)

            def squares(q):
                pool.wait_ge(tm_ready, 2 * q + 1)
                pool.tensor_tensor(sq[:, :, :, :], qk_tm[:, :, :, :], qk_tm[:, :, :, :], ALU.mult).then_inc(sq_ready, 1)

            def norms(q):
                pool.wait_ge(ss_ready, q + 1)
                pool.tensor_tensor(rn[:, :], ss[:, 1, :], mhalf[:, :], ALU.pow).then_inc(rn_ready, 1)

            def keep(q):
                pool.wait_ge(tm_ready, 2 * q + 2)
                apart(pool, passes)
                for t in range(2):
                    pool.tensor_copy(v_r[:, bass.ds(q + (1 - t) * nseq, 1), :], vs_tm[:, 0, t:t + 1, :]).then_inc(kept, 1)
                pool.tensor_copy(short_tm[:, bass.ds(q * 2, 2), :], vs_tm[:, 1, :, :]).then_inc(kept, 1)

            def couplings(q, levels):
                for l in levels:
                    for t in range(2):
                        if l == 0:
                            pool.wait_ge(mt_ready, 2 * q + t + 1)
                        if l >= 2:
                            pool.wait_ge(y_ready if l == 2 else p_ready,
                                         (2 * LEVELS * q + t + 1) if l == 2 else (2 * (LEVELS - 1) * q + 2 * (l - 3) + t + 1))
                        pool.tensor_tensor(CT[:, t, l % 2, :, :], MT[:, t, :, :],
                                           couple[:, l, :].unsqueeze(1).to_broadcast([P, HD, P]),
                                           ALU.mult).then_inc(ct_ready, 1)

            fetch(0)
            squares(0)
            norms(0)
            with pool.Fori(0, nseq - 1) as q:
                pool.wait_ge(xt_done, q + 1)
                apart(pool, passes)
                fetch(q + 1)
                couplings(q, (0, 1))
                keep(q)
                couplings(q, range(2, LEVELS - 1))
                squares(q + 1)
                couplings(q, (LEVELS - 1,))
                norms(q + 1)
            couplings(nseq - 1, range(LEVELS))
            keep(nseq - 1)

        @block.tensor
        def _(pe):
            pe.wait_ge(const_ready, 1)
            pe.wait_ge(loaded, 64)
            def turn_input(q):
                pe.wait_ge(xg_ready, q + 1)
                for t in range(2):
                    last = pe.transpose(B[3][:, t * P:(t + 1) * P], xg[:, t * P:(t + 1) * P], ident[:, :])
                last.then_inc(xt_done, 1)

            def project(q):
                pe.wait_ge(xT_ready, q + 1)
                for i in range(3):
                    last = pe.matmul(B[4 - i // 2][:, (i % 2) * S2:(i % 2 + 1) * S2], wqkv[:, i, :], xT[:, :],
                                     start=True, stop=True)
                    if i == 1:
                        last.then_inc(proj_done, 1)
                for t in range(2):
                    last = pe.matmul(B[3][:, S2 + t * HD:S2 + (t + 1) * HD], xT[:, t * P:(t + 1) * P], bw[:, :],
                                     start=True, stop=True)
                last.then_inc(proj_done, 1)

            def turn_qk(q):
                pe.wait_ge(silu_ready, 3 * q + 2)
                for i in range(4):
                    last = pe.transpose(B[4][:, i * P:(i + 1) * P], qk[:, i // 2, (i % 2) * P:(i % 2 + 1) * P], ident[:, :])
                last.then_inc(tm_done, 1)

            def turn_v(q):
                pe.wait_ge(silu_ready, 3 * q + 3)
                for t in range(2):
                    pe.transpose(B[3][:, t * P:(t + 1) * P],
                                 vpad[:, SHORT - 1 + t * P:SHORT - 1 + (t + 1) * P], ident[:, :])
                pe.wait_ge(sf_ready, q + 1)
                for t in range(2):
                    last = pe.transpose(B[3][:, (2 + t) * P:(3 + t) * P], sf[:, t * P:(t + 1) * P], ident[:, :])
                last.then_inc(tm_done, 1)

            def turn_normalised(q):
                pe.wait_ge(qkn_ready, q + 1)
                for i in range(4):
                    last = pe.transpose(B[4][:, i * P:(i + 1) * P], qkn[:, i // 2, i % 2, :], ident[:, :])
                last.then_inc(qknt_done, 1)

            def key_products(q):
                pe.wait_ge(qkx_ready, q * 2 * HD + HD)
                for t in range(2):
                    pe.matmul(B[3 + t][:, :], qknT[:, 1, t * P:(t + 1) * P], qkx[:, 1, t, :, :],
                              start=True, stop=True).then_inc(kk_done, 1)

            def step(q, follows):
                for t in range(2):
                    pe.wait_ge(m_ready, 2 * q + t + 1)
                    for h in range(HD):
                        last = pe.transpose(B[5 + t][:, h * P:(h + 1) * P], M[:, t, h, :], ident[:, :])
                    last.then_inc(mt_done, 1)
                pe.wait_ge(qkx_ready, q * 2 * HD + 2 * HD)
                for t in range(2):
                    pe.matmul(B[1 + t][:, :], qknT[:, 1, t * P:(t + 1) * P], qkx[:, 0, t, :, :],
                              start=True, stop=True).then_inc(at_done, 1)
                for l in range(LEVELS):
                    if l:
                        for t in range(2):
                            pe.wait_ge(x_ready, 2 * (LEVELS - 1) * q + 2 * (l - 1) + t + 1)
                            pe.wait_ge(ct_ready, 2 * LEVELS * q + 2 * l + t + 1)
                            for h in range(HD):
                                last = pe.matmul(bP[t][:, h * P:(h + 1) * P], CT[:, t, l % 2, h, :], X[:, t, h, :],
                                                 start=True, stop=True)
                            last.then_inc(p_done, 1)
                        for t in range(2):
                            pe.wait_ge(p_ready, 2 * (LEVELS - 1) * q + 2 * (l - 1) + t + 1)
                            if l == 1:
                                pe.wait_ge(at_ready, 2 * q + t + 1)
                            for h in range(HD):
                                last = pe.matmul(bY[t][:, h * P:(h + 1) * P], PX[:, t, h, :], Y[:, t, h, :],
                                                 start=True, stop=True)
                            last.then_inc(yy_done, 1)
                    if l < LEVELS - 1:
                        for t in range(2):
                            pe.wait_ge(y_ready, 2 * LEVELS * q + 2 * l + t + 1)
                            for h in range(HD):
                                last = pe.transpose(bX[t][:, h * P:(h + 1) * P], Y[:, t, h, :], ident[:, :])
                            last.then_inc(xt2_done, 1)
                    if follows and l == 0:
                        turn_input(q + 1)
                    if follows and l == 1:
                        project(q + 1)
                    if follows and l == 3:
                        turn_qk(q + 1)
                    if follows and l == 4:
                        turn_v(q + 1)
                for i, (src, t) in enumerate(((vb, 0), (vb, 1), (kb, 1))):
                    pe.wait_ge(y_ready, 2 * LEVELS * q + 2 * (LEVELS - 1) + t + 1)
                    for h in range(HD):
                        last = pe.matmul(B[5][DK * h:DK * (h + 1), i * P:(i + 1) * P], src[:, t, DK * h:DK * (h + 1)],
                                         Y[:, t, h, :], start=True, stop=True)
                last.then_inc(uw_done, 1)
                if follows:
                    turn_normalised(q + 1)
                pe.wait_ge(uw_ready, q + 1)
                for t in range(2):
                    last = pe.transpose(B[6][:, t * P:(t + 1) * P], uwT[:, t, :], ident[:, :])
                last.then_inc(ut_done, 1)
                pe.wait_ge(u_ready, q + 1)
                pe.wait_ge(late_ready, 2 * q + 2)
                pe.matmul(B[1][:, 0:D], k0[:, :], u[:, 0, :], start=True, stop=True).then_inc(st_done, 1)
                for h in range(HD):
                    pe.matmul(B[7][DK * h:DK * (h + 1), 0:P], u[:, 0, DK * h:DK * (h + 1)], AT[:, 0, h, :],
                              start=True, stop=True)
                if follows:
                    key_products(q + 1)
                pe.wait_ge(state_ready, q + 1)
                pe.matmul(B[2][:, 0:D], uwT[:, 2, :], state[:, :], start=True, stop=True).then_inc(ws_done, 1)
                pe.matmul(B[7][:, P:S2], state[:, :], qT1[:, :], start=True, stop=False, skip_group_check=True)
                pe.wait_ge(ua_ready, q + 1)
                for h in range(HD):
                    last = pe.matmul(B[7][DK * h:DK * (h + 1), P:S2], ua[:, DK * h:DK * (h + 1)], AT[:, 1, h, :],
                                     start=False, stop=True, skip_group_check=True)
                last.then_inc(ot_done, 1)
                pe.wait_ge(oT_ready, q + 1)
                for t in range(2):
                    last = pe.transpose(B[0][:, t * P:(t + 1) * P], oT[:, t * P:(t + 1) * P], ident[:, :])
                last.then_inc(o_done, 1)
                pe.wait_ge(o_ready, q + 1)

            turn_input(0)
            project(0)
            turn_qk(0)
            turn_v(0)
            turn_normalised(0)
            key_products(0)
            with pe.Fori(0, nseq - 1) as q:
                step(q, True)
            step(nseq - 1, False)

        @block.scalar
        def _(act):
            act.wait_ge(const_ready, 1)
            def turned(q):
                act.wait_ge(xt_done, q + 1)
                act.activation(xT[:, :], B[3][:, 0:S2], ACT.Copy).then_inc(xT_ready, 1)

            def projected(q):
                act.wait_ge(proj_done, 2 * q + 1)
                act.activation(pad[:, 0:2, TAPS - 1:], B[4][:, :].rearrange("p (i n) -> p i n", i=2),
                               ACT.Copy).then_inc(pad_ready, 1)
                act.wait_ge(proj_done, 2 * q + 2)
                act.activation(pad[:, 2, TAPS - 1:], B[3][:, 0:S2], ACT.Copy).then_inc(pad_ready, 1)
                act.activation(beta[:, 0, :, :].rearrange("p t h -> p (t h)"), B[3][:, S2:S2 + 2 * HD],
                               ACT.Sigmoid).then_inc(beta_sig, 1)

            def sigmoids(q):
                for i in range(3):
                    act.wait_ge(conv_ready, 3 * TAPS * q + 3 * (TAPS - 1) + i + 1)
                    act.activation(sg[:, i, :], conv[:, i, :], ACT.Sigmoid).then_inc(sg_ready, 1)

            def turned_qk(q):
                act.wait_ge(tm_done, 2 * q + 1)
                act.activation(qk_tm[:, :, :, :].rearrange("p i t c -> p (i t c)"), B[4][:, :], ACT.Copy).then_inc(tm_ready, 1)

            def turned_v(q, kept_before):
                act.wait_ge(tm_done, 2 * q + 2)
                if kept_before:
                    act.wait_ge(kept, 3 * q)
                    act.wait_ge(scaled, 2 * q)
                act.activation(vs_tm[:, :, :, :].rearrange("p i t c -> p (i t c)"), B[3][:, :], ACT.Copy).then_inc(tm_ready, 1)

            def turned_normalised(q):
                act.wait_ge(qknt_done, q + 1)
                act.activation(qknT[:, :, :].rearrange("p i n -> p (i n)"), B[4][:, :], ACT.Copy).then_inc(qknT_ready, 1)

            def step(q, follows):
                act.activation(k0[:, :], qkn[:, 1, 0, :], ACT.Copy).then_inc(late_ready, 1)
                act.wait_ge(qknT_ready, q + 1)
                act.activation(qT1[:, :], qknT[:, 0, P:S2], ACT.Copy).then_inc(late_ready, 1)
                for t in range(2):
                    act.wait_ge(mt_done, 2 * q + t + 1)
                    act.activation(MT[:, t, :, :].rearrange("p h n -> p (h n)"), B[5 + t][:, :], ACT.Copy).then_inc(mt_ready, 1)
                for l in range(LEVELS):
                    if l:
                        for t in range(2):
                            act.wait_ge(p_done, 2 * (LEVELS - 1) * q + 2 * (l - 1) + t + 1)
                            act.activation(PX[:, t, :, :].rearrange("p h n -> p (h n)"), bP[t][:, :],
                                           ACT.Copy).then_inc(p_ready, 1)
                    if l < LEVELS - 1:
                        for t in range(2):
                            act.wait_ge(xt2_done, 2 * (LEVELS - 1) * q + 2 * l + t + 1)
                            act.activation(X[:, t, :, :].rearrange("p h n -> p (h n)"), bX[t][:, :],
                                           ACT.Copy).then_inc(x_ready, 1)
                    if follows and l == 0:
                        turned(q + 1)
                    if follows and l == 1:
                        projected(q + 1)
                    if follows and l == 2:
                        sigmoids(q + 1)
                    if follows and l == 4:
                        turned_qk(q + 1)
                    if follows and l == 5:
                        turned_v(q + 1, True)
                act.wait_ge(uw_done, q + 1)
                act.activation(uwT[:, :, :].rearrange("p i n -> p (i n)"), B[5][:, 0:3 * P], ACT.Copy).then_inc(uw_ready, 1)
                if follows:
                    turned_normalised(q + 1)
                act.wait_ge(ut_done, q + 1)
                act.activation(u[:, :, :].rearrange("p t n -> p (t n)"), B[6][:, 0:S2], ACT.Copy).then_inc(u_ready, 1)
                act.wait_ge(ot_done, q + 1)
                act.activation(oT[:, :], B[7][:, 0:S2], ACT.Copy).then_inc(oT_ready, 1)
                act.wait_ge(o_done, q + 1)
                act.activation(delta_tm[:, bass.ds(q * 2, 2), :], B[0][:, 0:S2].rearrange("p (t c) -> p t c", t=2),
                               ACT.Copy).then_inc(o_ready, 1)

            turned(0)
            projected(0)
            sigmoids(0)
            turned_qk(0)
            turned_v(0, False)
            turned_normalised(0)
            with act.Fori(0, nseq - 1) as q:
                step(q, True)
            step(nseq - 1, False)

        @block.vector
        def _(dve):
            dve.wait_ge(const_ready, 1)
            dve.wait_ge(loaded, 64)
            def convolve(q, steps):
                for j in steps:
                    for i in range(3):
                        if j == 0:
                            dve.wait_ge(pad_ready, 2 * q + 1 + i // 2)
                            dve.tensor_scalar(conv[:, i, :], pad[:, i, 0:S2], taps[:, i, 0:1], None,
                                              ALU.mult).then_inc(conv_ready, 1)
                        else:
                            dve.wait_ge(conv_ready, 3 * TAPS * q + 3 * (j - 1) + i + 1)
                            dve.scalar_tensor_tensor(out=conv[:, i, :], in0=pad[:, i, j:j + S2],
                                                     scalar=taps[:, i, j:j + 1], in1=conv[:, i, :],
                                                     op0=ALU.mult, op1=ALU.add).then_inc(conv_ready, 1)

            def silus(q):
                for i in range(3):
                    dve.wait_ge(sg_ready, 3 * q + i + 1)
                    dve.tensor_tensor(qk[:, i, :] if i < 2 else vpad[:, SHORT - 1:], conv[:, i, :], sg[:, i, :],
                                      ALU.mult).then_inc(silu_ready, 1)

            def short_filter(q):
                dve.wait_ge(beta_sig, q + 1)
                dve.tensor_scalar(beta[:, 1, :, :], beta[:, 0, :, :], 1e-6, None, ALU.max).then_inc(dchain, 1)
                dve.wait_ge(silu_ready, 3 * q + 3)
                for j in range(SHORT):
                    if j == 0:
                        ins = dve.tensor_scalar(sf[:, :], vpad[:, 0:S2], ftaps[:, 0:1], None, ALU.mult)
                    else:
                        dve.wait_ge(dchain, NC * q + 1 + j)
                        ins = dve.scalar_tensor_tensor(out=sf[:, :], in0=vpad[:, j:j + S2], scalar=ftaps[:, j:j + 1],
                                                       in1=sf[:, :], op0=ALU.mult, op1=ALU.add)
                    ins.then_inc(dchain if j < SHORT - 1 else sf_ready, 1)

            def sums(q):
                dve.wait_ge(sq_ready, q + 1)
                dve.tensor_reduce(ss[:, 0, :], sq[:, :, :, :].rearrange("p i t (h c) -> p (i t h) c", h=HD),
                                  AX.X, ALU.add).then_inc(dchain, 1)
                dve.wait_ge(dchain, NC * q + SHORT + 1)
                dve.tensor_scalar(ss[:, 1, :], ss[:, 0, :], 1e-6, None, ALU.add).then_inc(ss_ready, 1)

            def normalise(q, late_before):
                if late_before:
                    dve.wait_ge(late_ready, 2 * q)
                dve.wait_ge(rn_ready, q + 1)
                dve.tensor_tensor(qkn[:, :, :, :].rearrange("p i t (h c) -> p (i t h) c", h=HD),
                                  qk_tm[:, :, :, :].rearrange("p i t (h c) -> p (i t h) c", h=HD),
                                  rn[:, :].unsqueeze(2).to_broadcast([P, 4 * HD, DK]), ALU.mult).then_inc(qkn_ready, 1)

            def spread(q):
                dve.wait_ge(qknT_ready, q + 1)
                for i in (1, 0):
                    for h in range(HD):
                        dve.tensor_scalar(qkx[:, i, :, h, :], qknT[:, i, :].rearrange("p (t n) -> p t n", t=2),
                                          hmask[:, h:h + 1], None, ALU.mult).then_inc(qkx_ready, 1)

            def key_matrix(q):
                for t in range(2):
                    dve.wait_ge(kk_done, 2 * q + t + 1)
                    for h in range(HD):
                        last = dve.scalar_tensor_tensor(out=M[:, t, h, :], in0=B[3 + t][:, h * P:(h + 1) * P],
                                                        scalar=beta[:, 1, t, h:h + 1], in1=strict[:, :],
                                                        op0=ALU.mult, op1=ALU.mult)
                    last.then_inc(m_ready, 1)

            def step(q, follows):
                dve.wait_ge(tm_ready, 2 * q + 2)
                bt = beta[:, 1, :, :].unsqueeze(3).to_broadcast([P, 2, HD, DK])
                dve.tensor_tensor(vb[:, :, :].rearrange("p t (h c) -> p t h c", h=HD),
                                  vs_tm[:, 0, :, :].rearrange("p t (h c) -> p t h c", h=HD), bt,
                                  ALU.mult).then_inc(scaled, 1)
                dve.wait_ge(qkn_ready, q + 1)
                dve.tensor_tensor(kb[:, :, :].rearrange("p t (h c) -> p t h c", h=HD),
                                  qkn[:, 1, :, :].rearrange("p t (h c) -> p t h c", h=HD), bt,
                                  ALU.mult).then_inc(scaled, 1)
                for t in range(2):
                    dve.wait_ge(ct_ready, 2 * LEVELS * q + t + 1)
                    dve.scalar_tensor_tensor(out=Y[:, t, :, :], in0=CT[:, t, 0, :, :], scalar=-1.0,
                                             in1=ident[:, :].unsqueeze(1).to_broadcast([P, HD, P]),
                                             op0=ALU.mult, op1=ALU.add).then_inc(y_ready, 1)
                for t in range(2):
                    dve.wait_ge(at_done, 2 * q + t + 1)
                    dve.tensor_tensor(AT[:, t, :, :], B[1 + t][:, :].rearrange("p (h n) -> p h n", h=HD),
                                      causal[:, :].unsqueeze(1).to_broadcast([P, HD, P]), ALU.mult).then_inc(at_ready, 1)
                for l in range(1, LEVELS):
                    for t in range(2):
                        dve.wait_ge(yy_done, 2 * (LEVELS - 1) * q + 2 * (l - 1) + t + 1)
                        dve.tensor_tensor(Y[:, t, :, :], Y[:, t, :, :],
                                          bY[t][:, :].rearrange("p (h n) -> p h n", h=HD),
                                          ALU.subtract).then_inc(y_ready, 1)
                    if follows and l == 1:
                        convolve(q + 1, (0, 1, 2))
                    if follows and l == 2:
                        convolve(q + 1, (3,))
                        silus(q + 1)
                    if follows and l == 3:
                        short_filter(q + 1)
                    if follows and l == 5:
                        sums(q + 1)
                if follows:
                    normalise(q + 1, True)
                    spread(q + 1)
                dve.wait_ge(st_done, q + 1)
                dve.tensor_tensor(state[:, :], B[1][:, 0:D], blocks[:, 5, :], ALU.mult).then_inc(state_ready, 1)
                dve.wait_ge(ws_done, q + 1)
                dve.tensor_tensor(ua[:, :], u[:, 1, :], B[2][:, 0:D], ALU.subtract).then_inc(ua_ready, 1)
                if follows:
                    key_matrix(q + 1)

            convolve(0, range(TAPS))
            silus(0)
            short_filter(0)
            sums(0)
            normalise(0, False)
            spread(0)
            key_matrix(0)
            with dve.Fori(0, nseq - 1) as q:
                step(q, True)
            step(nseq - 1, False)


def long_filter(nc, a, ident, nseq, v_r, long_r):
    CH = 8
    NS2 = 2 * nseq
    W = P + LONG
    FW = 2 * P + LONG
    taps = a["dlt_long"]
    with ExitStack() as ctx:
        s = Space(nc, ctx, "fir")
        tz = s.sb("tz", [P, 2, CH, W])
        vcol = s.sb("vcol", [P, 2, CH, NS2])
        vrev = s.sb("vrev", [P, 2, CH, NS2])
        flip = s.sb("flip", [P, P])
        o4 = s.sb("o4", [P, 2, 2 * P])
        bF = [s.ps("bF0"), s.ps("bF1")]
        bT = [s.ps("bT0"), s.ps("bT1")]
        bV = [s.ps("bV0"), s.ps("bV1")]
        tz_loaded = [s.sem("tz_loaded0"), s.sem("tz_loaded1")]
        flip_ready, vcol_ready, flipped, vrev_ready, fir_done, o4_ready, turn_done, kept = (s.sem(n) for n in (
            "flip_ready", "vcol_ready", "flipped", "vrev_ready", "fir_done", "o4_ready", "turn_done", "kept"))
        block = s.block()
        turns = D // CH

        @block.sync
        def _(sp):
            with sp.Fori(0, turns // 2) as i:
                for half in range(2):
                    sp.wait_ge(fir_done, 2 * i + 1)
                    src = taps[bass.ds((2 * i + half) * CH, CH), 0:W]
                    src = bass.AP(tensor=taps.tensor, offset=src.offset + 1, ap=[[1, P], [FW, CH], [1, W]])
                    sp.dma_start(tz[:, half, :, :], src).then_inc(tz_loaded[half], 16)
            for half in range(2):
                sp.wait_ge(tz_loaded[half], 16 * (turns // 2))

        @block.gpsimd
        def _(pool):
            pool.memset(flip[:, :], 0.0).then_inc(flip_ready, 1)
            pool.wait_ge(flip_ready, 1)
            pool.affine_select(out=flip[:, :], in_=flip[:, :], compare_op=ALU.not_equal, fill=1.0, base=1 - P,
                               pattern=[[1, P]], channel_multiplier=1).then_inc(flip_ready, 1)
            with pool.Fori(0, turns // 2) as i:
                for half in range(2):
                    pool.wait_ge(flipped, 2 * i + 1)
                    pool.tensor_copy(vcol[:, half, :, :].rearrange("p c s -> p s c"),
                                     v_r[:, :, bass.ds((2 * i + half) * CH, CH)]).then_inc(vcol_ready, 1)

        @block.tensor
        def _(pe):
            def turn_over(i, half):
                pe.wait_ge(o4_ready, 2 * i + half + 2)
                for j in range(2):
                    last = pe.transpose(bT[half][:, j * P:(j + 1) * P], o4[:, half, j * P:(j + 1) * P], ident[:, :])
                last.then_inc(turn_done, 1)

            for sem in (fir_done, flipped, turn_done):
                pe.sem_inc(sem, 1)
            pe.wait_ge(flip_ready, 2)
            with pe.Fori(0, turns // 2) as i:
                for half in range(2):
                    pe.wait_ge(vcol_ready, 2 * i + half + 1)
                    pe.wait_ge(vrev_ready, 2 * i + 1)
                    pe.matmul(bV[half][:, 0:CH * NS2], flip[:, :], vcol[:, half, :, :],
                              start=True, stop=True).then_inc(flipped, 1)
                for half in range(2):
                    pe.wait_ge(tz_loaded[half], 16 * i + 16)
                    pe.wait_ge(vrev_ready, 2 * i + half + 2)
                    pe.wait_ge(o4_ready, 2 * i + 1)
                    for c4 in range(0, CH, 4):
                        for c in range(c4, c4 + 4):
                            pe.matmul(bF[half][32 * (c % 4):32 * (c % 4) + NS2, (c // 4) * P:(c // 4 + 1) * P],
                                      vrev[:, half, c, :], tz[:, half, c, 0:P], start=(c < 4), stop=False,
                                      skip_group_check=True)
                        for c in range(c4, c4 + 4):
                            last = pe.matmul(
                                bF[half][32 * (c % 4):32 * (c % 4) + nseq, (c // 4) * P:(c // 4) * P + LONG],
                                vrev[:, half, c, nseq:NS2], tz[:, half, c, P:W], start=False, stop=True,
                                skip_group_check=True)
                    last.then_inc(fir_done, 1)
                    if half == 1:
                        turn_over(i, 0)
                turn_over(i, 1)

        @block.scalar
        def _(act):
            for sem in (vrev_ready, o4_ready):
                act.sem_inc(sem, 1)
            with act.Fori(0, turns // 2) as i:
                for half in range(2):
                    act.wait_ge(flipped, 2 * i + half + 2)
                    act.wait_ge(fir_done, 2 * i + 1)
                    act.activation(vrev[:, half, :, :].rearrange("p c s -> p (c s)"), bV[half][:, 0:CH * NS2],
                                   ACT.Copy).then_inc(vrev_ready, 1)
                for half in range(2):
                    act.wait_ge(fir_done, 2 * i + half + 2)
                    act.wait_ge(turn_done, 2 * i + 1)
                    act.activation(o4[:, half, :], bF[half][:, 0:2 * P], ACT.Copy).then_inc(o4_ready, 1)
                for half in range(2):
                    act.wait_ge(turn_done, 2 * i + half + 2)
                    act.activation(long_r[:, :, bass.ds((2 * i + half) * CH, CH)],
                                   bT[half][:, 0:2 * P].rearrange("p (c s) -> p s c", c=CH)[:, 0:NS2, :],
                                   ACT.Copy).then_inc(kept, 1)


def gate_and_project(nc, a, x, ident, ngroups, v_r, short_tm, long_r, delta_tm):
    NSTR = 4
    NF, NM = 8, 13
    HT = TILES * HD
    nseq = 2 * ngroups
    with ExitStack() as ctx:
        s = Space(nc, ctx, "gate")
        w1a = s.sb("w1a", [P, P])
        w1b = s.sb("w1b", [P, HD, P])
        w2 = s.sb("w2", [P, 32])
        ow = s.sb("ow", [P, 2, D])
        col = s.sb("col", [P, 3])
        tmp = s.sb("tmp", [P, 8])
        cr = s.sb("cr", [P, 2, HD])
        mhalf = s.sb("mhalf", [P, 64])
        half = s.sb("half", [P, 64])
        xg = s.sb("xg", [P, G])
        xT = s.sb("xT", [P, G])
        S = s.sb("S", [P, 2, NSTR, TILES, D])
        cen = s.sb("cen", [P, NSTR, TILES, D])
        red = s.sb("red", [P, 6, 64])
        stz = s.sb("stz", [P, TILES, P])
        stT = s.sb("stT", [P, G])
        hg = s.sb("hg", [P, 2, G])
        lT = s.sb("lT", [P, G])
        lt = s.sb("lt", [P, HT, 4])
        pr = s.sb("pr", [P, 4, HT, 4])
        red2 = s.sb("red2", [P, 6, HT])
        mix = s.sb("mix", [P, 4, G])
        o = s.sb("o", [P, G])
        osq = s.sb("osq", [P, G])
        oT = s.sb("oT", [P, G])
        b_x, b_s, b_h0, b_h1, b_l, b_lt, b_o, b_y = (s.ps(n) for n in (
            "b_x", "b_s", "b_h0", "b_h1", "b_l", "b_lt", "b_o", "b_y"))
        b_h = (b_h0, b_h1)
        (loaded, setup_p, setup_v, setup_a, zeroed, xg_ready, s_ready, xt_done, xT_ready, chain, cen_ready, sq_ready,
         l2_in, l2_ready, st_ready, stt_done, stT_ready, h_done, hg_ready, l_done, lT_ready, lt_done, e_in, e_ready,
         prod_in, rms_in, rms_ready, o_ready, ot_done, oT_ready, y_done, x_ready, mixed, mchain,
         passes) = (
            s.sem(n) for n in (
                "loaded setup_p setup_v setup_a zeroed xg_ready s_ready xt_done xT_ready chain cen_ready sq_ready "
                "l2_in l2_ready st_ready stt_done stT_ready h_done hg_ready l_done lT_ready lt_done e_in e_ready "
                "prod_in rms_in rms_ready o_ready ot_done oT_ready y_done x_ready mixed mchain "
                "passes").split())
        block = s.block()
        NLOAD = 4 + 2 + 2 * HD + 2

        @block.sync
        def _(sp):
            sp.wait_ge(zeroed, 3)
            sp.dma_start(w1a[:, :], a["gate_w1a"]).then_inc(loaded, 16)
            sp.dma_start(w2[:, 0:4], a["gate_w2"]).then_inc(loaded, 16)
            sp.dma_start(ow[:, 0, :], a["gate_ow"]).then_inc(loaded, 16)
            sp.dma_start(col[:, 0:2], a["gate_cols"]).then_inc(loaded, 16)
            sp.dma_start(cr[:, 0, :], a["gate_res"].unsqueeze(0).to_broadcast([P, HD])).then_inc(loaded, 16)
            sp.dma_start(tmp[:, 0:1], a["gate_temp"].unsqueeze(0).to_broadcast([P, 1])).then_inc(loaded, 16)
            for h in range(HD):
                sp.dma_start(w1b[16 * h:16 * h + 16, h, :], a["gate_w1b"]).then_inc(loaded, 16)
                sp.dma_start(col[DK * h:DK * h + 4, 2:3], a["gate_b2"].rearrange("(p o) -> p o", o=1)).then_inc(loaded, 16)
            sp.wait_ge(loaded, 16 * (NLOAD - 2))

        @block.gpsimd
        def _(pool):
            pool.memset(w1b[:, :, :], 0.0).then_inc(zeroed, 1)
            pool.memset(w2[:, :], 0.0).then_inc(zeroed, 1)
            pool.memset(col[:, :], 0.0).then_inc(zeroed, 1)
            pool.memset(stz[:, :, :], 0.0).then_inc(setup_p, 1)
            pool.memset(mhalf[:, :], -0.5).then_inc(setup_p, 1)
            pool.memset(half[:, :], 0.5).then_inc(setup_p, 1)
            pool.wait_ge(setup_p, 3)
            def front(g, b, first, free=False):
                tiles = bass.ds(g * TILES, TILES)
                if not first:
                    pool.wait_ge(xt_done, g)
                    apart(pool, passes)
                pool.tensor_copy(xg[:, :].rearrange("p (t c) -> p t c", t=TILES), x[:, tiles, :]).then_inc(xg_ready, 1)
                if free:
                    pool.wait_ge(mixed, g - 1)
                    apart(pool, passes)
                pool.tensor_copy(S[:, b, 0, :, :], short_tm[:, tiles, :]).then_inc(s_ready, 1)
                pool.wait_ge(l2_in, g + 1)
                pool.tensor_tensor(red[:, 5, :], red[:, 4, :], half[:, :], ALU.pow).then_inc(l2_ready, 1)

            def step(g, b, first=False, last=False):
                if not last:
                    front(g + 1, 1 - b, False, free=not first)
                pool.wait_ge(rms_in, g + 1)
                pool.tensor_tensor(red2[:, 5, :], red2[:, 4, :], mhalf[:, 0:HT], ALU.pow).then_inc(rms_ready, 1)

            front(0, 0, True)
            step(0, 0, True)
            with pool.Fori(0, ngroups // 2 - 1) as i:
                step(2 * i + 1, 1)
                step(2 * i + 2, 0)
            step(ngroups - 1, 1, last=True)

        @block.tensor
        def _(pe):
            pe.wait_ge(loaded, 16 * (NLOAD - 2))
            pe.wait_ge(setup_v, 6)
            def front(g, b, first):
                pe.wait_ge(xg_ready, g + 1)
                for t in range(TILES):
                    last = pe.transpose(b_x[:, t * P:(t + 1) * P], xg[:, t * P:(t + 1) * P], ident[:, :])
                last.then_inc(xt_done, 1)

            def turn_statistics(g):
                pe.wait_ge(st_ready, 4 * g + 4)
                for t in range(TILES):
                    last = pe.transpose(b_s[:, t * P:(t + 1) * P], stz[:, t, :], ident[:, :])
                last.then_inc(stt_done, 1)

            def step(g, b, first=False, last=False):
                pe.wait_ge(xT_ready, g + 1)
                for h in range(HD + 1):
                    if h < HD:
                        if h >= 2:
                            pe.wait_ge(hg_ready, HD * g + h - 1)
                        pe.matmul(b_h[h % 2][:, :], w1a[:, :], xT[:, :], start=True, stop=False)
                        if h == 0:
                            pe.wait_ge(stT_ready, g + 1)
                        pe.matmul(b_h[h % 2][:, :], w1b[:, h, :], stT[:, :], start=False, stop=True).then_inc(h_done, 1)
                    if h >= 1:
                        pe.wait_ge(hg_ready, HD * g + h)
                        ins = pe.matmul(b_l[32 * (h - 1):32 * h, :], w2[:, :], hg[:, (h - 1) % 2, :],
                                         start=True, stop=True).then_inc(l_done, 1)
                pe.wait_ge(lT_ready, g + 1)
                for t in range(TILES):
                    ins = pe.transpose(b_lt[:, t * P:(t + 1) * P], lT[:, t * P:(t + 1) * P], ident[:, :])
                ins.then_inc(lt_done, 1)
                if not last:
                    front(g + 1, 1 - b, False)
                pe.wait_ge(o_ready, g + 1)
                for t in range(TILES):
                    ins = pe.transpose(b_o[:, t * P:(t + 1) * P], o[:, t * P:(t + 1) * P], ident[:, :])
                ins.then_inc(ot_done, 1)
                pe.wait_ge(oT_ready, g + 1)
                if not first:
                    pe.wait_ge(x_ready, g)
                for t in range(TILES):
                    ins = pe.matmul(b_y[:, t * D:(t + 1) * D], oT[:, t * P:(t + 1) * P], ow[:, 1, :],
                                     start=True, stop=True)
                ins.then_inc(y_done, 1)
                if not last:
                    turn_statistics(g + 1)

            front(0, 0, True)
            turn_statistics(0)
            step(0, 0, True)
            with pe.Fori(0, ngroups // 2 - 1) as i:
                step(2 * i + 1, 1)
                step(2 * i + 2, 0)
            step(ngroups - 1, 1, last=True)

        @block.scalar
        def _(act):
            act.wait_ge(loaded, 16 * (NLOAD - 2))
            act.wait_ge(setup_v, 2)
            act.activation(tmp[:, 3:4], tmp[:, 2:3], ACT.Exp, scale=-1.0).then_inc(setup_a, 1)
            act.wait_ge(setup_a, 1)
            act.activation(tmp[:, 4:5], tmp[:, 3:4], ACT.Ln, bias=1.0).then_inc(setup_a, 1)
            act.activation(cr[:, 1, :], cr[:, 0, :], ACT.Sigmoid).then_inc(setup_a, 1)
            def streams(g, b, free=False):
                tiles = bass.ds(g * TILES, TILES)
                if free:
                    act.wait_ge(mixed, g - 1)
                act.activation(S[:, b, 2, :, :], delta_tm[:, tiles, :], ACT.Copy).then_inc(s_ready, 1)
                for src, i in ((v_r, 3), (long_r, 1)):
                    for k in range(2):
                        act.activation(S[:, b, i, 1 - k::2, :], src[:, bass.ds(k * nseq + 2 * g, 2), :],
                                       ACT.Copy).then_inc(s_ready, 1)

            def statistics(g):
                act.wait_ge(xt_done, g + 1)
                act.activation(xT[:, :], b_x[:, :], ACT.Copy).then_inc(xT_ready, 1)
                act.wait_ge(cen_ready, g + 1)
                act.activation(cen[:, :, :, :], cen[:, :, :, :], ACT.Square).then_inc(sq_ready, 1)

            def turned_statistics(g):
                act.wait_ge(stt_done, g + 1)
                act.activation(stT[:, :], b_s[:, :], ACT.Copy).then_inc(stT_ready, 1)

            def front(g, b, first):
                streams(g, b)
                statistics(g)
                turned_statistics(g)

            def step(g, b, first=False, last=False):
                if not last:
                    streams(g + 1, 1 - b, free=not first)
                for h in range(HD):
                    act.wait_ge(h_done, HD * g + h + 1)
                    if h >= 2:
                        act.wait_ge(l_done, HD * g + h - 1)
                    act.activation(hg[:, h % 2, :], b_h[h % 2][:, :], ACT.Gelu_apprx_tanh,
                                   bias=col[:, 0:1]).then_inc(hg_ready, 1)
                act.wait_ge(l_done, HD * (g + 1))
                act.activation(lT[:, :], b_l[:, :], ACT.Identity, bias=col[:, 2:3]).then_inc(lT_ready, 1)
                if not last:
                    statistics(g + 1)
                tiles = bass.ds(g * TILES, TILES)
                act.wait_ge(e_in, g + 1)
                act.activation(pr[:, 1, :, :], pr[:, 0, :, :], ACT.Exp, scale=tmp[:, 6:7]).then_inc(e_ready, 1)
                act.wait_ge(ot_done, g + 1)
                act.activation(oT[:, :], b_o[:, :], ACT.Copy).then_inc(oT_ready, 1)
                act.wait_ge(y_done, g + 1)
                act.activation(x[:, tiles, :], b_y[:, :].rearrange("p (t c) -> p t c", t=TILES),
                               ACT.Copy).then_inc(x_ready, 1)
                if not last:
                    turned_statistics(g + 1)

            front(0, 0, True)
            step(0, 0, True)
            with act.Fori(0, ngroups // 2 - 1) as i:
                step(2 * i + 1, 1)
                step(2 * i + 2, 0)
            step(ngroups - 1, 1, last=True)

        @block.vector
        def _(dve):
            dve.wait_ge(loaded, 16 * (NLOAD - 2))
            dve.wait_ge(setup_p, 3)
            dve.tensor_scalar(tmp[:, 1:2], tmp[:, 0:1], -1.0, None, ALU.mult).then_inc(setup_v, 1)
            dve.wait_ge(setup_v, 1)
            dve.tensor_tensor(tmp[:, 2:3], tmp[:, 0:1], tmp[:, 1:2], ALU.max).then_inc(setup_v, 1)
            dve.wait_ge(setup_a, 3)
            dve.tensor_scalar(tmp[:, 7:8], tmp[:, 0:1], 0.0, None, ALU.max).then_inc(setup_v, 1)
            dve.wait_ge(setup_v, 3)
            dve.tensor_tensor(tmp[:, 5:6], tmp[:, 7:8], tmp[:, 4:5], ALU.add).then_inc(setup_v, 1)
            dve.wait_ge(setup_v, 4)
            dve.reciprocal(tmp[:, 6:7], tmp[:, 5:6]).then_inc(setup_v, 1)
            dve.tensor_scalar(ow[:, 1, :], ow[:, 0, :], col[:, 1:2], None, ALU.mult).then_inc(setup_v, 1)
            dve.wait_ge(setup_v, 6)
            def links(sem, n):
                def link(ins):
                    nonlocal n
                    n = n + 1
                    ins.then_inc(sem, 1)
                    dve.wait_ge(sem, n)
                return link

            stat = stz[:, :, 0:HD * 16].rearrange("p t (h s k) -> p k s t h", h=HD, s=NSTR)

            def put(k, src):
                v = src.rearrange("p (s t h) -> p s t h", s=NSTR, t=TILES)
                for i in range(NSTR):
                    last = dve.tensor_copy(stat[:, k, i, :, :], v[:, i, :, :])
                last.then_inc(st_ready, 1)

            def finish_statistics(g):
                dve.wait_ge(l2_ready, g + 1)
                put(3, red[:, 5, :])

            def front(g, b, first):
                link = links(chain, NF * g)
                rows = S[:, b, :, :, :].rearrange("p s t (h c) -> p (s t h) c", c=DK)
                crow = cen[:, :, :, :].rearrange("p s t (h c) -> p (s t h) c", c=DK)
                dve.wait_ge(s_ready, 6 * g + 6)
                if not first:
                    dve.wait_ge(stt_done, g)
                link(dve.tensor_reduce(red[:, 0, :], rows, AX.X, ALU.add))
                link(dve.tensor_scalar(red[:, 1, :], red[:, 0, :], 1.0 / DK, None, ALU.mult))
                dve.tensor_tensor(crow, rows, red[:, 1, :].unsqueeze(2).to_broadcast([P, 64, DK]),
                                  ALU.subtract).then_inc(cen_ready, 1)
                link(dve.tensor_reduce(red[:, 0, :], rows, AX.X, ALU.add, apply_absolute_value=True))
                link(dve.tensor_scalar(red[:, 0, :], red[:, 0, :], 1.0 / DK, None, ALU.mult))
                put(0, red[:, 1, :])
                put(2, red[:, 0, :])
                dve.wait_ge(sq_ready, g + 1)
                link(dve.tensor_reduce(red[:, 2, :], crow, AX.X, ALU.add))
                link(dve.tensor_scalar(red[:, 3, :], red[:, 2, :], 1.0 / DK, None, ALU.mult))
                link(dve.tensor_tensor(red[:, 4, :], red[:, 1, :], red[:, 1, :], ALU.mult))
                link(dve.tensor_tensor(red[:, 4, :], red[:, 4, :], red[:, 3, :], ALU.add))
                dve.tensor_scalar(red[:, 4, :], red[:, 4, :], float(DK), None, ALU.mult).then_inc(l2_in, 1)
                put(1, red[:, 3, :])

            def step(g, b, first=False, last=False):
                if not last:
                    front(g + 1, 1 - b, False)
                link = links(mchain, NM * g)
                dve.wait_ge(lt_done, g + 1)
                lo = b_lt[:, :].rearrange("p (a e) -> p a e", e=32)[:, :, 0:4]
                link(dve.tensor_copy(lt[:, :, :], lo))
                link(dve.tensor_reduce(red2[:, 0, :], lt[:, :, :], AX.X, ALU.max))
                dve.tensor_tensor(pr[:, 0, :, :], lt[:, :, :], red2[:, 0, :].unsqueeze(2).to_broadcast([P, HT, 4]),
                                  ALU.subtract).then_inc(e_in, 1)
                dve.wait_ge(e_ready, g + 1)
                for i in (1, 2):
                    link(dve.tensor_reduce(red2[:, i, :], pr[:, i, :, :], AX.X, ALU.add))
                    link(dve.reciprocal(red2[:, 3, :], red2[:, i, :]))
                    link(dve.tensor_tensor(pr[:, i + 1, :, :], pr[:, i, :, :],
                                           red2[:, 3, :].unsqueeze(2).to_broadcast([P, HT, 4]), ALU.mult))
                    if i == 1:
                        link(dve.tensor_scalar(pr[:, 2, :, :], pr[:, 2, :, :], 0.02, None, ALU.max))
                dve.tensor_tensor(pr[:, 3, :, 0].rearrange("p (t h) -> p t h", h=HD),
                                  pr[:, 3, :, 0].rearrange("p (t h) -> p t h", h=HD),
                                  cr[:, 1, :].unsqueeze(1).to_broadcast([P, TILES, HD]), ALU.add).then_inc(prod_in, 1)
                dve.wait_ge(prod_in, g + 1)
                for i in range(NSTR):
                    ins = dve.tensor_tensor(mix[:, i, :].rearrange("p (t c) -> p t c", c=DK),
                                            S[:, b, i, :, :].rearrange("p t (h c) -> p (t h) c", c=DK),
                                            pr[:, 3, :, i:i + 1].to_broadcast([P, HT, DK]), ALU.mult)
                ins.then_inc(mixed, 1)
                dve.wait_ge(mixed, g + 1)
                dve.tensor_tensor(mix[:, 0:2, :], mix[:, 0:2, :], mix[:, 2:4, :], ALU.add).then_inc(mchain, 1)
                n_added = NM * g + 10
                dve.wait_ge(mchain, n_added)
                link = links(mchain, n_added)
                link(dve.tensor_tensor(o[:, :], mix[:, 0, :], mix[:, 1, :], ALU.add))
                link(dve.tensor_tensor(osq[:, :], o[:, :], o[:, :], ALU.mult))
                link(dve.tensor_reduce(red2[:, 3, :], osq[:, :].rearrange("p (a c) -> p a c", c=DK), AX.X, ALU.add))
                dve.tensor_scalar(red2[:, 4, :], red2[:, 3, :], 1.0 / DK, 1e-5, ALU.mult, ALU.add).then_inc(rms_in, 1)
                dve.wait_ge(rms_ready, g + 1)
                dve.tensor_tensor(o[:, :].rearrange("p (a c) -> p a c", c=DK), o[:, :].rearrange("p (a c) -> p a c", c=DK),
                                  red2[:, 5, :].unsqueeze(2).to_broadcast([P, HT, DK]), ALU.mult).then_inc(o_ready, 1)
                if not last:
                    finish_statistics(g + 1)

            front(0, 0, True)
            finish_statistics(0)
            step(0, 0, True)
            with dve.Fori(0, ngroups // 2 - 1) as i:
                step(2 * i + 1, 1)
                step(2 * i + 2, 0)
            step(ngroups - 1, 1, last=True)


def lay_out(i):
    import numpy as np

    def A(n):
        return np.asarray(i["L0_attn_" + n])

    nl = A("Wq").shape[0]
    out = {}
    mats = [A(n).transpose(1, 0, 2) for n in ("Wq", "Wk", "Wv", "Wo", "W1")]
    mats.append(A("W2").reshape(nl, FB, P, D).transpose(2, 0, 1, 3).reshape(P, nl, FB * D))
    out["enc_mats"] = np.ascontiguousarray(np.concatenate(mats, axis=2))
    out["enc_rows"] = np.ascontiguousarray(np.concatenate(
        [A(n) for n in ("bv", "bo", "g1", "be1", "bf2", "g2", "be2")], axis=1))
    cols = [A(n).T[:, :, None] for n in ("bq", "bk", "g1", "be1")]
    cols.append(A("bf1").reshape(nl, FB, P).transpose(2, 0, 1))
    out["enc_cols"] = np.ascontiguousarray(np.concatenate(cols, axis=2))
    out["L0_attn_omega"] = A("omega")
    w1, w2, wr = (np.asarray(i["L0_ffn_" + n]) for n in ("W1", "W2", "Wr"))
    out["moe0_up"] = np.ascontiguousarray(w1.reshape(NE, 2, 2, P, D).transpose(4, 0, 1, 2, 3))
    out["moe0_down"] = np.ascontiguousarray(w2.reshape(NE, D, 2, P).transpose(3, 0, 2, 1))
    out["moe0_router"] = np.ascontiguousarray(wr.T)
    w1, w2, cf, cp, gw = (np.asarray(i["L1_ffn_" + n]) for n in ("w1", "w2", "cfc", "cproj", "gate_w"))
    out["moe1_up"] = np.ascontiguousarray(np.concatenate([w1, cf[None]]).transpose(2, 0, 1)[:, :, None, None, :])
    out["moe1_down"] = np.ascontiguousarray(np.concatenate([w2, cp[None]]).transpose(2, 0, 1)[:, :, None, :])
    out["moe1_router"] = np.ascontiguousarray(gw.T)
    w = [np.asarray(i[f"L1_attn_{n}_w"]).T[:, None, :] for n in "qkv"]
    out["dlt_wqkv"] = np.ascontiguousarray(np.concatenate(w, axis=1))
    out["dlt_bw"] = np.ascontiguousarray(np.asarray(i["L1_attn_b_w"]).T)
    out["dlt_taps"] = np.ascontiguousarray(np.stack([np.asarray(i[f"L1_attn_{n}_cw"]) for n in "qkv"], axis=1))
    out["dlt_short"] = np.asarray(i["L1_attn_fir_short_w"]).reshape(D, SHORT)
    f = np.asarray(i["L1_attn_fir_long_w"]).reshape(D, LONG)[:, ::-1]
    out["dlt_long"] = np.ascontiguousarray(np.pad(f, ((0, 0), (P, P))))
    w1 = np.asarray(i["L1_attn_mlp1_w"]).T
    out["gate_w1a"], out["gate_w1b"] = np.ascontiguousarray(w1[:D]), np.ascontiguousarray(w1[D:])
    out["gate_w2"] = np.ascontiguousarray(np.asarray(i["L1_attn_mlp2_w"]).T)
    out["gate_ow"] = np.ascontiguousarray(np.asarray(i["L1_attn_o_w"]).T)
    out["gate_cols"] = np.ascontiguousarray(np.stack(
        [np.asarray(i["L1_attn_mlp1_b"]), np.tile(np.asarray(i["L1_attn_norm_w"]), HD)], axis=1))
    out["gate_res"] = np.asarray(i["L1_attn_conv_res_logit"])
    out["gate_temp"] = np.asarray(i["L1_attn_logit_temp"])
    out["gate_b2"] = np.asarray(i["L1_attn_mlp2_b"])
    out["moe1_bias"] = np.asarray(i["L1_ffn_lb_bias"])
    return out


def store_tokens(nc, resid, update, out, ngroups):
    with ExitStack() as ctx:
        s = Space(nc, ctx, "out")
        row = s.sb("row", [P, ngroups, TILES, D])
        summed, stored = s.sem("summed"), s.sem("stored")
        block = s.block()

        @block.vector
        def _(dve):
            for g in range(ngroups):
                tiles = slice(g * TILES, (g + 1) * TILES)
                dve.tensor_tensor(row[:, g, :, :], resid[:, tiles, :], update[:, tiles, :],
                                  ALU.add).then_inc(summed, 1)

        @block.sync
        def _(sp):
            for g in range(ngroups):
                sp.wait_ge(summed, g + 1)
                sp.dma_start(out[g * G:(g + 1) * G, :].rearrange("(t p) c -> p t c", p=P),
                             row[:, g, :, :]).then_inc(stored, 16)
            sp.wait_ge(stored, 16 * ngroups)


def program(nc, a, out):
    ntok = a["x"].shape[0]
    ngroups, nseq, tiles = ntok // G, ntok // SEQ, ntok // P
    with ExitStack() as ctx:
        s = Space(nc, ctx, "top")
        resid, x = s.sb("resid", [P, tiles, D]), s.sb("x", [P, tiles, D])
        ident = s.sb("ident", [P, P])
        load_tokens(nc, a["x"], resid, ident, ngroups)
        residual_norm(nc, "n0", resid, None, x, ngroups)
        encoder(nc, a, x, ident)
        residual_norm(nc, "n1", resid, x, x, ngroups)
        mixture(nc, "moe0", x, ident, ngroups, NE, 2, a["moe0_up"], a["moe0_down"], a["moe0_router"], None)
        residual_norm(nc, "n2", resid, x, x, ngroups)
        with ExitStack() as inner:
            streams = Space(nc, inner, "str")
            v_r, short_tm, long_r, delta_tm = (streams.sb(n, [P, tiles, D]) for n in ("v", "short", "long", "delta"))
            delta_mixer(nc, a, x, ident, nseq, v_r, short_tm, delta_tm)
            long_filter(nc, a, ident, nseq, v_r, long_r)
            gate_and_project(nc, a, x, ident, ngroups, v_r, short_tm, long_r, delta_tm)
        residual_norm(nc, "n3", resid, x, x, ngroups)
        mixture(nc, "moe1", x, ident, ngroups, NE + 1, 1, a["moe1_up"], a["moe1_down"], a["moe1_router"],
                a["moe1_bias"])
        store_tokens(nc, resid, x, out, ngroups)


def kernel(**inputs):
    import numpy as np
    import concourse.bacc as bacc
    from concourse.bass_utils import run_bass_kernel_spmd

    laid = lay_out(inputs)
    x = np.asarray(inputs["L0_attn_x"])
    laid["x"] = np.ascontiguousarray(x.reshape(-1, D))
    nc = bacc.Bacc("TRN2", target_bir_lowering=False, num_devices=1)
    arrays = {f"in_{n}": v for n, v in laid.items()}
    a = {n: nc.dram_tensor(f"in_{n}", v.shape, mybir.dt.from_np(v.dtype), kind="ExternalInput").ap()
         for n, v in laid.items()}
    out = nc.dram_tensor("out_y", laid["x"].shape, F32, kind="ExternalOutput").ap()
    program(nc, a, out)
    r = run_bass_kernel_spmd(nc, [arrays], core_ids=[0])
    return r.results[0]["out_y"].reshape(x.shape)
```
